# Optimizing a Trainium2 kernel written in Bass

```python
import numpy as np
import jax
import jax.numpy as jnp

def _softmax(x, axis=-1):
    return jax.nn.softmax(x, axis=axis)

def _gelu(x):
    return jax.nn.gelu(x, approximate=True)

def _silu(x):
    return jax.nn.silu(x)

def _sigmoid(x):
    return jax.nn.sigmoid(x)

def _layernorm(x, axis=-1, eps=1e-05):
    m = jnp.mean(x, axis=axis, keepdims=True)
    v = jnp.var(x, axis=axis, keepdims=True)
    return (x - m) / jnp.sqrt(v + eps)

def _scatter_add(tgt, idx, src, axis=0):
    return tgt.at[idx].add(src)

def _segment_sum(src, seg, n):
    return jax.ops.segment_sum(src, seg, n)
kernel_name = 'mk_flamingo_gated_d1_seqx_r4_2e42fe'

def setup_inputs(seed: int=0):
    np.random.seed(seed)
    _w = jnp.asarray

    def _rec_inputs():
        import jax
        import jax.numpy as jnp
        _rk = jax.random.key(seed)
        x = 7.22e-05 + 1 * jax.random.normal(jax.random.fold_in(_rk, 1), (8, 256, 256), jnp.float32)
        _lenS = 256 - jax.random.randint(jax.random.fold_in(_rk, 7), (8,), 0, max(1, 256 // 4) + 1, jnp.int32)
        _lenS2 = 256 - jax.random.randint(jax.random.fold_in(_rk, 8), (8,), 0, max(1, 256 // 4) + 1, jnp.int32)
        _ctx_1024P = jax.random.normal(jax.random.fold_in(_rk, 11), (8, 16, 256), jnp.float32)
        _ctx_1024c = jax.random.dirichlet(jax.random.fold_in(_rk, 511), 0.3 * jnp.ones((16,), jnp.float32), (8, 256))
        _ctx_1024t = jnp.einsum('bsk,bkd->bsd', _ctx_1024c, _ctx_1024P)
        _ctx_1024t = _ctx_1024t * jax.lax.rsqrt(jnp.mean(jnp.square(_ctx_1024t)) + 1e-12) * 0.953939
        ctx_1024 = 4.13588e-05 + 0.999923 * (_ctx_1024t + 0.3 * jax.random.normal(jax.random.fold_in(_rk, 611), (8, 256, 256), jnp.float32))
        _g = jax.random.normal(jax.random.fold_in(_rk, 9001), (2, 1), jnp.float32)
        _g = jnp.sign(_g) * jnp.maximum(jnp.abs(_g), 1.0) + (_g == 0) * 1.0
        g_xattn = _g[0]
        g_ffn = _g[1]
        return (x, ctx_1024, g_xattn, g_ffn)
    x, ctx_1024, g_xattn, g_ffn = _rec_inputs()

    def _L0_xattn_setup():
        import jax, jax.numpy as jnp
        import numpy as np
        B, T, D, H = (4, 512, 256, 8)
        HD = D // H

        def _heads(t):
            b, t_, _ = t.shape
            return t.reshape(b, t_, H, HD).transpose(0, 2, 1, 3)
        key = jax.random.key(seed)
        ks = jax.random.split(key, 10)
        s = 1.0 / np.sqrt(D)
        return {'x': jax.random.normal(ks[0], (B, T, D), jnp.float32), 'y': jax.random.normal(ks[1], (B, T, D), jnp.float32), 'Wq': jax.random.normal(ks[2], (D, D), jnp.float32) * s, 'bq': jnp.zeros((D,), jnp.float32), 'Wk': jax.random.normal(ks[3], (D, D), jnp.float32) * s, 'bk': jnp.zeros((D,), jnp.float32), 'Wv': jax.random.normal(ks[4], (D, D), jnp.float32) * s, 'bv': jnp.zeros((D,), jnp.float32), 'Wo': jax.random.normal(ks[5], (D, D), jnp.float32) * s, 'bo': jnp.zeros((D,), jnp.float32)}
    _L0_xattn_all = _L0_xattn_setup()
    _L0_xattn_in = {k: v for k, v in _L0_xattn_all.items() if k in ('Wq', 'bq', 'Wk', 'bk', 'Wv', 'bv', 'Wo', 'bo')}
    del _L0_xattn_all

    def _L0_ffn_setup():
        import jax, jax.numpy as jnp
        import numpy as np
        B, S, H, DFF, E, K = (2, 512, 256, 512, 8, 2)

        def _moe(x, Wg, W1, b1, W2, b2, W3, b3):
            Bm, Sm, Hm = x.shape
            xt = x.reshape(-1, Hm)
            gout = xt @ Wg.T
            topv, topi = jax.lax.top_k(gout, K)
            w = jax.nn.softmax(topv, axis=-1)
            comb = jnp.einsum('tke,tk->te', jax.nn.one_hot(topi, E, dtype=x.dtype), w)
            g = jnp.einsum('th,efh->etf', xt, W1) + b1[:, None, :]
            v = jnp.einsum('th,efh->etf', xt, W2) + b2[:, None, :]
            h = jax.nn.silu(g) * v
            eo = jnp.einsum('etf,ehf->eth', h, W3) + b3[:, None, :]
            out = jnp.einsum('eth,te->th', eo, comb)
            return out.reshape(Bm, Sm, Hm)
        key = jax.random.key(seed)
        ks = jax.random.split(key, 8)
        sc_h = 1.0 / np.sqrt(H)
        sc_f = 1.0 / np.sqrt(DFF)
        x = jax.random.normal(ks[0], (B, S, H), dtype=jnp.float32)
        Wg = jax.random.uniform(ks[1], (E, H), jnp.float32, -sc_h, sc_h)
        W1 = jax.random.uniform(ks[2], (E, DFF, H), jnp.float32, -sc_h, sc_h)
        b1 = jax.random.uniform(ks[3], (E, DFF), jnp.float32, -sc_h, sc_h)
        W2 = jax.random.uniform(ks[4], (E, DFF, H), jnp.float32, -sc_h, sc_h)
        b2 = jax.random.uniform(ks[5], (E, DFF), jnp.float32, -sc_h, sc_h)
        W3 = jax.random.uniform(ks[6], (E, H, DFF), jnp.float32, -sc_f, sc_f)
        b3 = jax.random.uniform(ks[7], (E, H), jnp.float32, -sc_f, sc_f)
        return {'x': x, 'Wg': Wg, 'W1': W1, 'b1': b1, 'W2': W2, 'b2': b2, 'W3': W3, 'b3': b3}
    _L0_ffn_all = _L0_ffn_setup()
    _L0_ffn_in = {k: v for k, v in _L0_ffn_all.items() if k in ('Wg', 'W1', 'b1', 'W2', 'b2', 'W3', 'b3')}
    del _L0_ffn_all
    return {'x': x, 'ctx_1024': ctx_1024, 'g_xattn': g_xattn, 'g_ffn': g_ffn, 'L0_xattn_Wq': _L0_xattn_in['Wq'], 'L0_xattn_bq': _L0_xattn_in['bq'], 'L0_xattn_Wk': _L0_xattn_in['Wk'], 'L0_xattn_bk': _L0_xattn_in['bk'], 'L0_xattn_Wv': _L0_xattn_in['Wv'], 'L0_xattn_bv': _L0_xattn_in['bv'], 'L0_xattn_Wo': _L0_xattn_in['Wo'], 'L0_xattn_bo': _L0_xattn_in['bo'], 'L0_ffn_Wg': _L0_ffn_in['Wg'], 'L0_ffn_W1': _L0_ffn_in['W1'], 'L0_ffn_b1': _L0_ffn_in['b1'], 'L0_ffn_W2': _L0_ffn_in['W2'], 'L0_ffn_b2': _L0_ffn_in['b2'], 'L0_ffn_W3': _L0_ffn_in['W3'], 'L0_ffn_b3': _L0_ffn_in['b3']}

def reference(x, ctx_1024, g_xattn, g_ffn, L0_xattn_Wq, L0_xattn_bq, L0_xattn_Wk, L0_xattn_bk, L0_xattn_Wv, L0_xattn_bv, L0_xattn_Wo, L0_xattn_bo, L0_ffn_Wg, L0_ffn_W1, L0_ffn_b1, L0_ffn_W2, L0_ffn_b2, L0_ffn_W3, L0_ffn_b3):
    import jax
    import jax.numpy as jnp

    def _L0_xattn_ref(x, y, Wq, bq, Wk, bk, Wv, bv, Wo, bo):
        import jax, jax.numpy as jnp
        import numpy as np
        B, T, D, H = (4, 512, 256, 8)
        HD = D // H

        def _heads(t):
            b, t_, _ = t.shape
            return t.reshape(b, t_, H, HD).transpose(0, 2, 1, 3)
        Tq, Tk = (x.shape[1], y.shape[1])
        q = _heads(x @ Wq.T + bq)
        k = _heads(y @ Wk.T + bk)
        v = _heads(y @ Wv.T + bv)
        scale = 1.0 / np.sqrt(HD)
        logits = jnp.einsum('bhqd,bhkd->bhqk', q, k) * scale
        causal = jnp.triu(jnp.full((Tq, Tk), -jnp.inf, jnp.float32), k=1)
        logits = logits + causal
        attn = jax.nn.softmax(logits, axis=-1)
        ctx = jnp.einsum('bhqk,bhkd->bhqd', attn, v)
        ctx = ctx.transpose(0, 2, 1, 3).reshape(x.shape[0], Tq, D)
        out = ctx @ Wo.T + bo
        return out

    def _L0_ffn_ref(x, Wg, W1, b1, W2, b2, W3, b3):
        import jax, jax.numpy as jnp
        import numpy as np
        B, S, H, DFF, E, K = (2, 512, 256, 512, 8, 2)

        def _moe(x, Wg, W1, b1, W2, b2, W3, b3):
            Bm, Sm, Hm = x.shape
            xt = x.reshape(-1, Hm)
            gout = xt @ Wg.T
            topv, topi = jax.lax.top_k(gout, K)
            w = jax.nn.softmax(topv, axis=-1)
            comb = jnp.einsum('tke,tk->te', jax.nn.one_hot(topi, E, dtype=x.dtype), w)
            g = jnp.einsum('th,efh->etf', xt, W1) + b1[:, None, :]
            v = jnp.einsum('th,efh->etf', xt, W2) + b2[:, None, :]
            h = jax.nn.silu(g) * v
            eo = jnp.einsum('etf,ehf->eth', h, W3) + b3[:, None, :]
            out = jnp.einsum('eth,te->th', eo, comb)
            return out.reshape(Bm, Sm, Hm)
        return _moe(x, Wg, W1, b1, W2, b2, W3, b3)
    x = x + jnp.tanh(g_xattn[0]) * _L0_xattn_ref(_layernorm(x, axis=-1), ctx_1024, L0_xattn_Wq, L0_xattn_bq, L0_xattn_Wk, L0_xattn_bk, L0_xattn_Wv, L0_xattn_bv, L0_xattn_Wo, L0_xattn_bo)
    x = x + jnp.tanh(g_ffn[0]) * _L0_ffn_ref(_layernorm(x, axis=-1), L0_ffn_Wg, L0_ffn_W1, L0_ffn_b1, L0_ffn_W2, L0_ffn_b2, L0_ffn_W3, L0_ffn_b3)
    return x

_drawn_inputs = setup_inputs


def setup_inputs(seed=0):
    import zlib

    import numpy as np

    out = dict(_drawn_inputs(seed))
    spreads = {'L0_xattn_bq': (0.0, 0.404),
     'L0_xattn_bk': (0.0, 0.8),
     'L0_xattn_bv': (0.0, 0.1),
     'L0_xattn_bo': (0.0, 0.1)}
    factors = {'L0_ffn_b1': 8.0, 'L0_ffn_b2': 8.0, 'L0_ffn_b3': 3.616}
    for name, (base, spread) in spreads.items():
        noise = np.random.default_rng([zlib.crc32(name.encode()), seed]).standard_normal(out[name].shape)
        drawn = base * np.exp(spread * noise) if base else spread * noise
        out[name] = jnp.asarray(drawn.astype(out[name].dtype))
    for name, factor in factors.items():
        out[name] = (out[name] * factor).astype(out[name].dtype)
    return out
```

```python
from contextlib import ExitStack

import numpy as np

import concourse.bass as bass
from concourse import mybir

ALU = mybir.AluOpType
ACT = mybir.ActivationFunctionType
AX = mybir.AxisListType
F32 = mybir.dt.float32
F16 = mybir.dt.float16
BF16 = mybir.dt.bfloat16
I32 = mybir.dt.int32

P = 128
B, T, D = 8, 256, 256
H, HD = 8, 32
E, F, TOPK = 8, 512, 2
TT = T // P
NT = B * TT
N = B * T
KT = D // P
FT = F // P
HG = H // 4
EPS = 1e-5
WS = 16.0
MASKED = -1.0e30
NEVER = -3.0e38
BLOCKS = (TOPK * N + E * (P - 1)) // P
WC = 3
WE = KT * F
EW = WC * WE
EB = 2 * F + D
ROW = D + E
HI, LO = 0, 1

C_ID, C_MS, C_MT, C_TRI, C_ONE, C_IO, C_E8, C_SC, C_TOK, C_BLK = np.cumsum(
    [0, P, P, P, P, P, P, NT * E, NT * E, NT]).tolist()
C_END = C_BLK + BLOCKS + 1


def constants():
    c = np.zeros((P, C_END), np.float32)
    i = np.arange(P)
    c[:, C_ID:C_ID + P] = np.eye(P)
    c[:, C_MS:C_MS + P] = np.where(i[None, :] > i[:, None], MASKED, 0.0)
    c[:, C_MT:C_MT + P] = np.where(i[:, None] > i[None, :], MASKED, 0.0)
    c[:, C_TRI:C_TRI + P] = i[:, None] < i[None, :]
    c[:, C_ONE:C_ONE + P] = 1.0
    c[:, C_IO:C_IO + P] = i[None, :]
    c[:, C_E8:C_E8 + NT * E] = np.tile(np.arange(E) - E, NT)[None, :]
    c[:, C_SC:C_SC + NT * E] = np.tile((np.arange(NT) > 0) * 1.0, E)[None, :]
    c[:, C_TOK:C_TOK + NT] = np.arange(NT)[None, :] * P + i[:, None] - N
    c[:, C_BLK:C_BLK + BLOCKS] = np.arange(BLOCKS)[None, :]
    return c


def flamingo_kernel(nc, x, y, g, wattn, bcol, brow, wgate, wffn, bffn, consts, out):
    ctx = ExitStack()
    with ctx:
        def sb(name, shape, dt):
            return ctx.enter_context(nc.sbuf_tensor(name, shape, dt))

        def sem(name):
            return ctx.enter_context(nc.semaphore(name))

        x_rows = x.rearrange("b (t p) d -> p (b t) d", p=P)
        out_rows = out.rearrange("b (t p) d -> p (b t) d", p=P)
        out_flat = out.rearrange("b t d -> (b t) d")
        rows = nc.dram_tensor("token_rows", (N, ROW), I32, kind="Internal").ap()
        rows_v = rows.rearrange("(j p) c -> p j c", p=P)

        w_hl = [sb("ffn_w_hi", [P, E * EW], F16), sb("ffn_w_lo", [P, E * EW], F16)]
        region_a = sb("region_a", [P, E * EB], F32)
        region_x = sb("region_x", [P, NT * D], F32)
        region_w = sb("region_w", [P, WC * WE], F32)
        cst = sb("constants", [P, C_END], F32)

        at = [0]

        def carve(region, n, dt=F32):
            words = n if dt in (F32, I32) else n // 2
            view = region[:, at[0]:at[0] + words]
            at[0] += words
            assert at[0] <= region.shape[1]
            return view if dt == F32 else view.bitcast(dt)

        q_stack = [carve(region_a, H * T, F16).rearrange("p (h t) -> p h t", h=H) for _ in range(2)]
        k_stack = [carve(region_a, H * T, F16).rearrange("p (h t) -> p h t", h=H) for _ in range(2)]
        probs = [carve(region_a, 3 * 4 * P).rearrange("p (s h t) -> p s h t", s=3, h=4) for _ in range(HG)]
        y_raw = [carve(region_a, KT * T) for _ in range(2)]
        v_sb = [carve(region_a, TT * D).rearrange("p (t d) -> p t d", t=TT) for _ in range(2)]
        xh = carve(region_a, TT * 2 * D, F16).rearrange("p (t s d) -> p t s d", t=TT, s=2)
        xT = carve(region_a, 2 * KT * T, F16).rearrange("p (s k t) -> p s k t", s=2, k=KT)
        yT = sb("yT", [P, 2, KT * T], F16)
        qk_st = [[sb(f"{n}_{s}", [P, HG, T], F16) for s in ("hi", "lo")] for n in "qk"]
        xn = sb("xn", [P, TT, D], F32)
        xn2 = sb("xn2", [P, TT, D], F32)
        x2h = sb("x2h", [P, TT, 2, D], F16)
        x2T = sb("x2T", [P, 2, KT, T], F16)
        ctx32 = [sb(f"ctx32_{g}", [P, T], F32) for g in range(HG)]
        rden = sb("rden", [P, T], F32)
        ctx_hl = [sb("ctx_hi", [P, HG, T], F16), sb("ctx_lo", [P, HG, T], F16)]
        aw = [sb("attn_w_hi", [P, 4, KT, D], F16), sb("attn_w_lo", [P, 4, KT, D], F16)]
        gw_raw = sb("gate_w_raw", [P, KT * E], F32)
        gw = [sb("gate_w_hi", [P, KT, E], F16), sb("gate_w_lo", [P, KT, E], F16)]
        bc_raw = sb("bias_cols_raw", [P, 3 * KT], F32)
        bc = sb("bias_cols", [P, 3, KT], F32)
        bo = sb("bo_rows", [P, D], F32)
        g_raw = sb("g_raw", [P, 2], F32)
        tg = sb("tanh_g", [P, 2], F32)
        gsc = sb("attn_scale", [P, 1], F32)
        ident = sb("ident", [P, P], F16)
        identb = sb("identb", [P, P], BF16)
        mask_s = sb("mask_s", [P, 4, P], BF16)
        mask_t = sb("mask_t", [P, 4, P], BF16)
        onesf = sb("onesf", [P, HD], F32)
        half = sb("minus_half", [P, TT], F32)
        st1 = sb("st1", [P, TT, 6], F32)
        mv1 = sb("mv1", [P, TT, 2], F32)
        ve1 = sb("ve1", [P, TT], F32)
        rs1 = sb("rs1", [P, TT], F32)
        st2 = sb("st2", [P, TT, 6], F32)
        mv2 = sb("mv2", [P, TT, 2], F32)
        ve2 = sb("ve2", [P, TT], F32)
        rs2 = sb("rs2", [P, TT], F32)
        mx = sb("row_max", [P, H, TT], F32)
        mneg = sb("minus_max", [P, TT * H], F16)
        mrow = sb("shift_rows", [TT * H, P], F16)
        logits = sb("logits", [P, NT * E], F32)

        at[0] = 0
        hot_lo = carve(region_x, TOPK * NT * P, F16).rearrange("p (s c) -> p s c", c=P)
        hot_blk = carve(region_x, TOPK * NT * BLOCKS, F16).rearrange("p (s c) -> p s c", c=BLOCKS)
        at[0] = 0
        xg = [carve(region_x, ROW, I32) for _ in range(4)]
        xgT = [carve(region_x, 4 * P, F16) for _ in range(2)]
        at[0] = 0
        gv = carve(region_w, 2 * F)
        hh = carve(region_w, F)
        hT = [[carve(region_w, F, F16) for _ in range(2)] for _ in range(2)]
        yb = [carve(region_w, D) for _ in range(2)]
        yo = [sb(f"y_out_{i}", [P, D], F32) for i in range(2)]

        def rt(name, n=NT * E, dt=F32):
            return sb("rt_" + name, [P, n], dt)

        m1, m2, e1, e2 = (rt(n, NT) for n in ("m1", "m2", "e1", "e2"))
        at[0] = 0
        eq, oh1, oh2, lmask, base, comb, tmp, tot, scan = (carve(region_w, NT * E) for _ in range(9))
        both = rt("both", NT * E, F16)
        tri16 = sb("tri16", [P, P], F16)
        one16 = sb("one16", [P, P], F16)
        io16 = sb("io16", [P, P], F16)
        ex, den, pr1, pr2 = (rt(n, NT) for n in ("ex", "den", "pr1", "pr2"))
        nblk, nblk_f, start, start_s = rt("nblk", E, I32), rt("nblkf", E), rt("start", E), rt("starts", E)
        pos = rt("pos", TOPK * NT)
        pos_i, hi_i, lo_i = (rt(n, TOPK * NT, I32) for n in ("pos_i", "hi_i", "lo_i"))
        hi_f, lo_f = rt("hi_f", TOPK * NT), rt("lo_f", TOPK * NT)
        cmp = sb("rt_cmp", [1, (E - 1) * BLOCKS], F32)
        eidf = sb("rt_eidf", [1, BLOCKS], F32)
        eid = sb("block_expert", [1, BLOCKS], I32)
        idx_s = sb("scatter_rows", [P, BLOCKS], I32)
        idx_g = sb("gather_rows", [P, BLOCKS], I32)
        row_in = [sb(f"row_in_{i}", [P, 1], I32) for i in range(4)]
        row_out = [sb(f"row_out_{i}", [P, 1], I32) for i in range(2)]
        idx_f = rt("idx_f", BLOCKS)
        wslot = sb("slot_gate", [P, 4], F32)

        ps = ctx.enter_context(nc.psum_tensor("ps", [P, 8, 512], F32))
        turn = ps[:, 0, :]
        turn16 = turn.bitcast(F16)
        pa, pb = ps[:, 1, :], ps[:, 2, :]
        score = ps[:, 3:6, :].rearrange("p s (h t) -> p s h t", h=4)
        uden = ps[:, 6, :]
        rout = ps[:, 7, :]
        rout16 = rout.bitcast(F16)
        gvp = [ps[:, 0:2, :], ps[:, 2:4, :]]
        hTp = ps[:, 4, :]
        xTp = ps[:, 5, :].bitcast(F16)
        yp = [ps[:, 6, :], ps[:, 7, :]]

        (stood_alone, consts_in, small_in, attnw_in, x0_in, x_in, shift_in, base_stored, rows_stored,
         gates_stored, bias_in, setup_v, setup_a, setup_p, aw_hi, aw_lo, ln1_a, ln1_b, var1, rstd1,
         xn_done, xhi_done, xh_done, xT_done, ln2_a, ln2_b, var2, rstd2, xn2_done, x2hi_done, x2h_done,
         x2T_done, yhi_done, yT_done, whi_done, wlo_done, xb_done, q_mm, k_mm, v_mm, s_mm, t_mm,
         o_mm, lt_mm, mt_mm, rt_mm, r_mm, pv_mm, q_hi, q_st, k_hi, k_st, v_done, max_done, mneg_done,
         mrow_done, exp_done, rden_done, umul_done, ctxhi_done, ctx_done, x1_done, logit_done, row_in_done,
         row_out_done, route_v, route_a, route_mm, table_mm, idx_done, xgT_mm, xgT_done, gv_mm, g_done,
         v_half, gate_done, silu_done, h_done, hT_mm, hT_hi, hT_done, y_mm, y_done, yo_done, added) = (
            sem(name) for name in (
                "stood_alone consts_in small_in attnw_in x0_in x_in shift_in base_stored rows_stored "
                "gates_stored bias_in setup_v setup_a setup_p aw_hi aw_lo ln1_a ln1_b var1 rstd1 "
                "xn_done xhi_done xh_done xT_done ln2_a ln2_b var2 rstd2 xn2_done x2hi_done x2h_done "
                "x2T_done yhi_done yT_done whi_done wlo_done xb_done q_mm k_mm v_mm s_mm t_mm "
                "o_mm lt_mm mt_mm rt_mm r_mm pv_mm q_hi q_st k_hi k_st v_done max_done mneg_done "
                "mrow_done exp_done rden_done umul_done ctxhi_done ctx_done x1_done logit_done row_in_done "
                "row_out_done route_v route_a route_mm table_mm idx_done xgT_mm xgT_done gv_mm g_done "
                "v_half gate_done silu_done h_done hT_mm hT_hi hT_done y_mm y_done yo_done added "
            ).split())
        stack_in, y_in, w_in, xg_in = ([sem(f"{name}_{i}") for i in range(n)] for name, n in (
            ("stack_in", 2), ("y_in", 2), ("w_in", WC), ("xg_in", 4)))

        def begun(count):
            return not isinstance(count, int) or count > 0

        block = ctx.enter_context(nc.Block())

        def steps(eng, step):
            step(0, 0, 0, True, False)
            with eng.Fori(0, (B - 2) // 2) as i:
                step(i * 2 + 1, 1, i, False, False)
                step(i * 2 + 2, 0, i + 1, False, False)
            step(B - 1, 1, (B - 1) // 2, False, True)

        STACK = 16 * 4 * 6
        CREDIT = 2
        PAIRS = ((HI, HI), (HI, LO), (LO, HI))

        @block.sync
        def _(sp):
            sp.dma_start(cst[:, :], consts).then_inc(consts_in, 16)
            sp.dma_start(region_x[:, 0:TT * D].rearrange("p (j d) -> p j d", d=D),
                         x_rows[:, 0:TT, :]).then_inc(x0_in, 16)
            sp.dma_start(region_w[:, 0:4 * KT * D], wattn).then_inc(attnw_in, 16)
            sp.dma_start(y_raw[0], y[0]).then_inc(y_in[0], 16)
            for dst, src in ((gw_raw[:, :], wgate), (bc_raw[:, :], bcol),
                             (bo[:, :], brow.rearrange("a d -> (a d)").partition_broadcast(P)),
                             (g_raw[:, :], g.partition_broadcast(P))):
                sp.dma_start(dst, src).then_inc(small_in, 16)
            sp.dma_start(region_x[:, TT * D:].rearrange("p (j d) -> p j d", d=D),
                         x_rows[:, TT:, :]).then_inc(x_in, 16)
            sp.dma_start(y_raw[1], y[1]).then_inc(y_in[1], 16)

            def stack(which, dst, done, b, q):
                sp.wait_ge(done, b + 1)
                order = (HI, LO, HI) if which == 0 else (HI, HI, LO)
                for c, part in enumerate(order):
                    for quad in range(4):
                        sp.dma_start(
                            dst[32 * c:32 * c + 32, :, :].rearrange("p (m h) t -> p m h t", m=HG)[:, :, quad, :],
                            qk_st[which][part][32 * quad:32 * quad + 32, :, :],
                        ).then_inc(stack_in[q], 16)

            stack(0, q_stack[0], q_st, 0, 0)
            stack(1, k_stack[0], k_st, 0, 0)

            def results(b):
                sp.wait_ge(x1_done, b + 1)
                sp.dma_start(out_rows[:, bass.ds(b * TT, TT), :],
                             region_x[:, bass.ds(b * TT * D, TT * D)].rearrange("p (j d) -> p j d", d=D),
                             ).then_inc(base_stored, 16)

            def row_store(b):
                sp.wait_ge(x2h_done, b + 1)
                sp.dma_start(rows_v[:, bass.ds(b * TT, TT), 0:D],
                             x2h[:, :, :, :].rearrange("p j s d -> p j (s d)").bitcast(I32)).then_inc(rows_stored, 16)

            def step(b, q, r, first, last):
                if not first and not last:
                    if begun(b):
                        sp.wait_ge(yT_done, b)
                    sp.dma_start(y_raw[1 - q], y[bass.ds(b + 1, 1)].rearrange("a p n -> (a p) n"),
                                 ).then_inc(y_in[1 - q], 16)
                if not first:
                    results(b - 1)
                sp.wait_ge(mrow_done, b + 1)
                sp.dma_start(q_stack[q][96:97, :, :].rearrange("p h (t c) -> p (h t) c", t=TT),
                             mrow[:, :]).then_inc(shift_in, 16)
                if not last:
                    if begun(b * HG):
                        sp.wait_ge(t_mm, b * HG)
                    sp.sem_inc(stood_alone, 1)
                    stack(0, q_stack[1 - q], q_st, b + 1, 1 - q)
                if not first:
                    row_store(b - 1)
                if not last:
                    stack(1, k_stack[1 - q], k_st, b + 1, 1 - q)

            steps(sp, step)
            results(B - 1)
            row_store(B - 1)
            sp.wait_ge(pv_mm, B * HG)
            sp.wait_ge(exp_done, B * HG)
            sp.dma_start(region_a[:, :], bffn.rearrange("a d -> (a d)").partition_broadcast(P),
                         ).then_inc(bias_in, 16)
            sp.wait_ge(route_v, R_COMB)
            sp.dma_start(rows_v[:, :, D:], comb[:, :].bitcast(I32).rearrange("p (j c) -> p j c", j=NT),
                         ).then_inc(gates_stored, 16)
            sp.wait_ge(base_stored, 16 * B)
            sp.wait_ge(rows_stored, 16 * (B + 1))
            sp.wait_ge(gates_stored, 16)

        @block.scalar
        def _(act):
            act.sem_inc(rows_stored, 16)
            act.sem_inc(yo_done, CREDIT)
            act.wait_ge(attnw_in, 16)
            for c in range(4):
                act.activation(aw[HI][:, c, :, :].rearrange("p k d -> p (k d)"),
                               region_w[:, c * KT * D:(c + 1) * KT * D], ACT.Copy, scale=WS).then_inc(aw_hi, 1)
            act.wait_ge(small_in, 64)
            act.activation(gw[HI][:, :, :].rearrange("p k e -> p (k e)"), gw_raw[:, :], ACT.Copy,
                           scale=WS).then_inc(setup_a, 1)
            act.activation(tg[:, :], g_raw[:, :], ACT.Tanh).then_inc(setup_a, 1)

            def load_chunk(c, buf):
                act.dma_start(region_w[:, buf * WE:(buf + 1) * WE],
                              wffn[bass.ds(c, 1)].rearrange("a p n -> (a p) n")).then_inc(w_in[buf], 16)

            def split_chunk(b, buf):
                act.wait_ge(w_in[buf], (b + 1) * 16)
                raw = region_w[:, buf * WE:(buf + 1) * WE]
                act.activation(w_hl[HI][:, bass.ds((b * WC + buf) * WE, WE)], raw, ACT.Copy, scale=WS)
                act.activation(raw, raw, ACT.Copy, scale=WS).then_inc(whi_done, 1)

            def x_high(n):
                act.wait_ge(xn_done, n + 1)
                if begun(n):
                    act.wait_ge(lt_mm, n)
                act.activation(xh[:, :, HI, :], xn[:, :, :], ACT.Copy).then_inc(xhi_done, 1)

            def y_high(n, q, r):
                act.wait_ge(y_in[q], (r + 1) * 16)
                if begun(n):
                    act.wait_ge(v_mm, n)
                act.activation(yT[:, HI, :], y_raw[q], ACT.Copy).then_inc(yhi_done, 1)

            def qk_high(which, n):
                mm, done, src = ((q_mm, q_hi, pa), (k_mm, k_hi, pb))[which]
                act.wait_ge(mm, n + 1)
                if begun(n * HG):
                    act.wait_ge(s_mm, n * HG)
                for m in range(KT):
                    last = act.activation(qk_st[which][HI][:, m, :], src[:, m * T:(m + 1) * T], ACT.Identity,
                                          bias=bc[:, which, m:m + 1])
                last.then_inc(done, 1)

            def v_out(n, q):
                act.wait_ge(v_mm, n + 1)
                if begun((n - 1) * HG):
                    act.wait_ge(pv_mm, (n - 1) * HG)
                act.activation(v_sb[q].rearrange("p t d -> p (t d)"), pa, ACT.Copy).then_inc(v_done, 1)

            def expo(b, g):
                act.wait_ge(t_mm, b * HG + g + 1)
                if begun(b * HG - HG + g + 1):
                    act.wait_ge(pv_mm, b * HG - HG + g + 1)
                act.activation(probs[g].rearrange("p s h t -> p (s h t)"),
                               score.rearrange("p s h t -> p (s h t)"), ACT.Exp,
                               scale=float(HD) ** -0.5 / (WS * WS)).then_inc(exp_done, 1)

            def ctx_high(b, g):
                act.wait_ge(umul_done, b * HG + g + 1)
                if begun(b):
                    act.wait_ge(o_mm, b)
                act.activation(ctx_hl[HI][:, g, :], ctx32[g][:, :], ACT.Identity,
                               bias=bc[:, 2, g:g + 1]).then_inc(ctxhi_done, 1)

            def x2_high(b):
                act.wait_ge(xn2_done, b + 1)
                act.wait_ge(rows_stored, (b + 1) * 16)
                if begun(b):
                    act.wait_ge(rt_mm, b)
                act.activation(x2h[:, :, HI, :], xn2[:, :, :], ACT.Copy).then_inc(x2hi_done, 1)

            act.wait_ge(setup_v, SETUP_BIAS)
            x_high(0)
            y_high(0, 0, 0)
            qk_high(0, 0)
            qk_high(1, 0)
            v_out(0, 0)
            act.wait_ge(aw_lo, 4)
            for buf in range(WC):
                load_chunk(buf, buf)

            def step(b, q, r, first, last):
                if not last:
                    x_high(b + 1)
                    y_high(b + 1, 1 - q, r + q)
                split_chunk(b, 0)
                if not first:
                    if begun(b * WC - 1):
                        act.wait_ge(wlo_done, b * WC - 1)
                    load_chunk(b * WC + 1, 1)
                if not last:
                    qk_high(0, b + 1)
                if not first:
                    x2_high(b - 1)
                if not last:
                    qk_high(1, b + 1)
                split_chunk(b, 1)
                if not first:
                    if begun(b * WC):
                        act.wait_ge(wlo_done, b * WC)
                    load_chunk(b * WC + 2, 2)
                expo(b, 0)
                if not last:
                    v_out(b + 1, 1 - q)
                expo(b, 1)
                ctx_high(b, 0)
                split_chunk(b, 2)
                ctx_high(b, 1)
                if not last:
                    act.wait_ge(wlo_done, b * WC + 1)
                    load_chunk(b * WC + 3, 0)

            steps(act, step)
            x2_high(B - 1)
            act.wait_ge(route_v, R_DIFF)
            act.activation(ex[:, :], pr2[:, :], ACT.Exp).then_inc(route_a, 1)

            def silu(i):
                act.wait_ge(g_done, i + 1)
                act.activation(gv[:, 0:F], gv[:, 0:F], ACT.Silu).then_inc(silu_done, 1)

            def h_high(i, q):
                act.wait_ge(hT_mm, i + 1)
                if begun(i - 1):
                    act.wait_ge(y_mm, i - 1)
                act.activation(hT[q][HI], hTp, ACT.Copy).then_inc(hT_hi, 1)

            def turn_out(i, q):
                act.wait_ge(xgT_mm, i + 1)
                if begun(i - 1):
                    act.wait_ge(gv_mm, i - 1)
                act.activation(xgT[q], xTp[:, 0:4 * P], ACT.Copy).then_inc(xgT_done, 1)

            def gate(i, q, q4):
                act.wait_ge(y_done, i + 1 + CREDIT)
                if begun((i - 1) * 16):
                    act.wait_ge(added, (i - 1) * 16)
                act.activation(yo[q][:, :], yb[q], ACT.Copy, scale=wslot[:, q4:q4 + 1]).then_inc(yo_done, 1)

            turn_out(0, 0)
            silu(0)
            turn_out(1, 1)
            silu(1)
            h_high(0, 0)
            turn_out(2, 0)

            def blk(i, q4, last):
                silu(i)
                h_high(i - 1, 1 - q4 % 2)
                if not last:
                    turn_out(i + 1, 1 - q4 % 2)
                gate(i - 2, q4 % 2, (q4 + 2) % 4)

            for i in range(2, 6):
                blk(i, i % 4, False)
            with act.Fori(0, (BLOCKS - 7) // 4) as j:
                for u in range(4):
                    blk(j * 4 + (u + 6), (u + 2) % 4, False)
            blk(BLOCKS - 1, (BLOCKS - 1) % 4, True)
            h_high(BLOCKS - 1, (BLOCKS - 1) % 2)
            gate(BLOCKS - 2, (BLOCKS - 2) % 2, (BLOCKS - 2) % 4)
            gate(BLOCKS - 1, (BLOCKS - 1) % 2, (BLOCKS - 1) % 4)

        @block.gpsimd
        def _(pool):
            pool.memset(half[:, :], -0.5).then_inc(setup_p, 1)
            pool.memset(onesf[:, :], 1.0).then_inc(setup_p, 1)
            for q in range(2):
                pool.wait_ge(setup_p, 2 + q)
                pool.memset(k_stack[q][96:97, :, :], WS * WS).then_inc(setup_p, 1)

            def rstd(n, var, ve, rs, done, read):
                pool.wait_ge(var, n + 1)
                pool.tensor_tensor(rs[:, :], ve[:, :], half[:, :], ALU.pow).then_inc(done, 1)

            def y_low(n, q):
                pool.wait_ge(yhi_done, n + 1)
                pool.tensor_tensor(yT[:, LO, :], y_raw[q], yT[:, HI, :], ALU.subtract).then_inc(yT_done, 1)

            def w_low(b, buf):
                pool.wait_ge(whi_done, b * WC + buf + 1)
                c = (b * WC + buf) * WE
                pool.tensor_tensor(w_hl[LO][:, bass.ds(c, WE)], region_w[:, buf * WE:(buf + 1) * WE],
                                   w_hl[HI][:, bass.ds(c, WE)], ALU.subtract).then_inc(wlo_done, 1)

            def add_bo(b):
                pool.wait_ge(xn_done, b + 1)
                v = region_x[:, bass.ds(b * TT * D, TT * D)].rearrange("p (j d) -> p j d", d=D)
                pool.tensor_tensor(v, v, bo[:, :].unsqueeze(1).to_broadcast([P, TT, D]), ALU.add).then_inc(xb_done, 1)

            pool.wait_ge(setup_p, 4)
            rstd(0, var1, ve1, rs1, rstd1, xn_done)
            y_low(0, 0)
            pool.wait_ge(setup_v, SETUP_BO)

            def step(b, q, r, first, last):
                if not last:
                    rstd(b + 1, var1, ve1, rs1, rstd1, xn_done)
                    y_low(b + 1, 1 - q)
                w_low(b, 0)
                if not first:
                    rstd(b - 1, var2, ve2, rs2, rstd2, xn2_done)
                w_low(b, 1)
                add_bo(b)
                w_low(b, 2)

            steps(pool, step)
            rstd(B - 1, var2, ve2, rs2, rstd2, xn2_done)

            def gather(i, q):
                if begun(i - 3):
                    pool.wait_ge(v_half, i - 3)
                pool.tensor_copy(row_in[q][:, :], idx_g[:, bass.ds(i, 1)]).then_inc(row_in_done, 1)
                pool.wait_ge(row_in_done, i + 1)
                pool.sem_inc(stood_alone, 1)
                pool.indirect_dma_start(xg[q], None, rows,
                                        bass.IndirectOffsetOnAxis(ap=row_in[q][:, :], axis=0),
                                        ).then_inc(xg_in[q], 16)

            def add_rows(i, q):
                pool.tensor_copy(row_out[q][:, :], idx_s[:, bass.ds(i, 1)]).then_inc(row_out_done, 1)
                pool.wait_ge(row_out_done, i + 1)
                pool.wait_ge(yo_done, i + 1 + CREDIT)
                if not isinstance(i, int) or i > 0:
                    pool.wait_ge(added, i * 16)
                    pool.sem_inc(stood_alone, 1)
                pool.indirect_dma_start(out_flat, bass.IndirectOffsetOnAxis(ap=row_out[q][:, :], axis=0),
                                        yo[q][:, :], None, bounds_check=N - 1, oob_is_err=False,
                                        compute_op=ALU.add).then_inc(added, 16)

            pool.wait_ge(rows_stored, 16 * (B + 1))
            pool.wait_ge(gates_stored, 16)
            pool.wait_ge(base_stored, 16 * B)
            pool.wait_ge(idx_done, 3)
            for i in range(4):
                gather(i, i)

            def blk(i, q4):
                gather(i + 4, q4)
                add_rows(i, q4 % 2)

            for i in range(4):
                blk(i, i)
            with pool.Fori(0, (BLOCKS - 8) // 4) as j:
                for u in range(4):
                    blk(j * 4 + (u + 4), u)
            done = (BLOCKS - 4) // 4 * 4
            for i in range(done, BLOCKS):
                if i + 4 < BLOCKS:
                    gather(i + 4, i % 4)
                add_rows(i, i % 2)
            pool.wait_ge(added, 16 * BLOCKS)

        @block.tensor
        def _(pe):
            def split_mm(dst, left, right, kts=KT):
                n = 0
                for k in range(kts):
                    for a, c in PAIRS:
                        mm = pe.matmul(dst, left(a, k), right(c, k), start=(n == 0), stop=(n == 3 * kts - 1))
                        n += 1
                return mm

            def turns(src, dst16):
                for t in range(TT):
                    for h in (HI, LO):
                        for k in range(KT):
                            o = (h * KT + k) * T + t * P
                            mm = pe.transpose(dst16[:, o:o + P], src[:, t, h, k * P:(k + 1) * P], ident[:, :])
                return mm

            def x_turn(n):
                pe.wait_ge(xh_done, n + 1)
                if begun(n - 1):
                    pe.wait_ge(mrow_done, n - 1)
                turns(xh, turn16).then_inc(lt_mm, 1)

            def q_mul(n):
                pe.wait_ge(xT_done, n + 1)
                if begun(n):
                    pe.wait_ge(v_done, n)
                for m in range(KT):
                    mm = split_mm(pa[:, m * T:(m + 1) * T], lambda a, k: aw[a][:, 0, k, m * P:(m + 1) * P],
                                  lambda c, k: xT[:, c, k, :])
                mm.then_inc(q_mm, 1)

            def k_mul(n):
                pe.wait_ge(yT_done, n + 1)
                if begun(n - 1):
                    pe.wait_ge(x1_done, n - 1)
                if begun(n):
                    pe.wait_ge(k_st, n)
                for m in range(KT):
                    mm = split_mm(pb[:, m * T:(m + 1) * T], lambda a, k: aw[a][:, 1, k, m * P:(m + 1) * P],
                                  lambda c, k: yT[:, c, k * T:(k + 1) * T])
                mm.then_inc(k_mm, 1)

            def v_mul(n):
                pe.wait_ge(q_st, n + 1)
                for t in range(TT):
                    mm = split_mm(pa[:, t * D:(t + 1) * D],
                                  lambda a, k: yT[:, a, k * T + t * P:k * T + (t + 1) * P],
                                  lambda c, k: aw[c][:, 2, k, :])
                mm.then_inc(v_mm, 1)

            def scores(b, g, q):
                for bank, (tq, tk) in enumerate(((0, 0), (1, 0), (1, 1))):
                    if tq == tk:
                        pe.matmul(score[:, bank, :, :], identb[:, :], mask_s[:, :, :], start=True, stop=True)
                    for h in range(4):
                        mm = pe.matmul(score[:, bank, h, :], q_stack[q][0:96, 4 * g + h, tq * P:(tq + 1) * P],
                                       k_stack[q][0:96, 4 * g + h, tk * P:(tk + 1) * P],
                                       start=(tq != tk and h == 0), stop=True, skip_group_check=True)
                mm.then_inc(s_mm, 1)

            def scores_t(b, g, q):
                for bank, (tk, tq) in enumerate(((0, 0), (0, 1), (1, 1))):
                    if tq == tk:
                        pe.matmul(score[:, bank, :, :], identb[:, :], mask_t[:, :, :], start=True, stop=True)
                    for h in range(4):
                        mm = pe.matmul(score[:, bank, h, :], k_stack[q][0:97, 4 * g + h, tk * P:(tk + 1) * P],
                                       q_stack[q][0:97, 4 * g + h, tq * P:(tq + 1) * P],
                                       start=(tq != tk and h == 0), stop=True, skip_group_check=True)
                mm.then_inc(t_mm, 1)

            def mix(b, g, q):
                pe.wait_ge(exp_done, b * HG + g + 1)
                if begun(b * HG + g):
                    pe.wait_ge(umul_done, b * HG + g)
                for tk, w, col in ((0, T, 0), (1, P, P)):
                    for part in range(2):
                        for h in range(4):
                            left = onesf[:, :] if part else v_sb[q][:, tk, (4 * g + h) * HD:(4 * g + h + 1) * HD]
                            p = probs[g][:, 0:2, h, :] if tk == 0 else probs[g][:, 2:3, h, :]
                            o = uden[32 * h:32 * h + 32, part * T + col:part * T + col + w]
                            mm = pe.matmul(o.rearrange("p (s t) -> p s t", t=P), left, p,
                                           start=(tk == 0 and part == 0), stop=True,
                                           skip_group_check=True)
                mm.then_inc(pv_mm, 1)

            def o_mul(b):
                pe.wait_ge(ctx_done, (b + 1) * HG)
                pe.wait_ge(k_st, b + 2 if not isinstance(b, int) or b < B - 1 else B)
                for t in range(TT):
                    mm = split_mm(pb[:, t * D:(t + 1) * D], lambda a, k: ctx_hl[a][:, k, t * P:(t + 1) * P],
                                  lambda c, k: aw[c][:, 3, k, :])
                mm.then_inc(o_mm, 1)

            def r_turn(b):
                pe.wait_ge(x2h_done, b + 1)
                pe.wait_ge(logit_done, b + 1)
                turns(x2h, rout16).then_inc(rt_mm, 1)

            def r_mul(b):
                pe.wait_ge(x2T_done, b + 1)
                for t in range(TT):
                    mm = split_mm(rout[:, t * E:(t + 1) * E], lambda a, k: x2T[:, a, k, t * P:(t + 1) * P],
                                  lambda c, k: gw[c][:, k, :])
                mm.then_inc(r_mm, 1)

            pe.wait_ge(setup_v, SETUP_PE)
            pe.wait_ge(setup_p, 4)
            x_turn(0)
            pe.wait_ge(aw_lo, 4)
            q_mul(0)
            k_mul(0)
            v_mul(0)

            def step(b, q, r, first, last):
                pe.wait_ge(stack_in[q], (r + 1) * STACK)
                if begun(b * HG):
                    pe.wait_ge(exp_done, b * HG)
                scores(b, 0, q)
                if not first:
                    o_mul(b - 1)
                if not last:
                    x_turn(b + 1)
                pe.wait_ge(max_done, b * HG + 1)
                scores(b, 1, q)
                if not last:
                    q_mul(b + 1)
                pe.wait_ge(mneg_done, b + 1)
                if last:
                    pe.wait_ge(xT_done, B)
                pe.transpose(turn16[0:TT * H, 0:P], mneg[:, :], ident[:, :]).then_inc(mt_mm, 1)
                if not first:
                    r_turn(b - 1)
                if not last:
                    k_mul(b + 1)
                pe.wait_ge(shift_in, (b + 1) * 16)
                pe.wait_ge(max_done, b * HG + 2)
                scores_t(b, 0, q)
                if not first:
                    r_mul(b - 1)
                if not last:
                    v_mul(b + 1)
                pe.wait_ge(exp_done, b * HG + 1)
                scores_t(b, 1, q)
                mix(b, 0, q)
                mix(b, 1, q)

            steps(pe, step)
            o_mul(B - 1)
            r_turn(B - 1)
            r_mul(B - 1)

            pe.wait_ge(route_v, R_BOTH)
            both_v = both[:, :].rearrange("p (j e) -> p e j", e=E)
            pe.matmul(ps[:, 1, 0:P], tri16[:, :], both_v, start=True, stop=True)
            pe.matmul(ps[:, 2, 0:P], one16[:, :], both_v, start=True, stop=True).then_inc(route_mm, 1)
            pe.wait_ge(route_v, R_HOT)
            for c in range(TOPK * NT):
                mm = pe.matmul(ps[:, 3, 0:BLOCKS], hot_lo[:, c, :], hot_blk[:, c, :], start=(c == 0),
                               stop=(c == TOPK * NT - 1))
            mm.then_inc(table_mm, 1)

            def turn_in(i, q4, n4):
                pe.wait_ge(xg_in[q4], n4 * 16)
                if begun(i):
                    pe.wait_ge(xgT_done, i)
                for c in range(4):
                    mm = pe.transpose(xTp[:, c * P:(c + 1) * P], xg[q4].bitcast(F16)[:, c * P:(c + 1) * P], ident[:, :])
                mm.then_inc(xgT_mm, 1)

            def expert(i):
                return pe.value_load(eid[0:1, bass.ds(i, 1)], min_val=0, max_val=E - 1)

            def gv_mul(i, q):
                e = expert(i)
                pe.wait_ge(xgT_done, i + 1)
                if begun(i - 1):
                    pe.wait_ge(v_half, i - 1)
                for m in range(2):
                    mm = split_mm(gvp[q][:, m, :], lambda a, k: xgT[q][:, (a * KT + k) * P:(a * KT + k + 1) * P],
                                  lambda c, k: w_hl[c][:, bass.ds(e * EW + (m * WE + k * F), F)])
                mm.then_inc(gv_mm, 1)

            def turn_h(i):
                pe.wait_ge(h_done, i + 1)
                if begun(i):
                    pe.wait_ge(hT_done, i)
                for k in range(FT):
                    mm = pe.transpose(hTp[:, k * P:(k + 1) * P], hh[:, k * P:(k + 1) * P], cst[:, C_ID:C_ID + P])
                mm.then_inc(hT_mm, 1)

            def y_mul(i, q):
                e = expert(i)
                pe.wait_ge(hT_done, i + 1)
                pe.wait_ge(y_done, i - 1 + CREDIT)
                split_mm(yp[q][:, 0:D], lambda a, k: hT[q][a][:, k * P:(k + 1) * P],
                         lambda c, k: w_hl[c][:, bass.ds(e * EW + (2 * WE + k * D), D)],
                         FT).then_inc(y_mm, 1)

            pe.wait_ge(wlo_done, WC * B)
            pe.wait_ge(idx_done, 3)
            turn_in(0, 0, 1)
            gv_mul(0, 0)
            turn_in(1, 1, 1)
            gv_mul(1, 1)
            turn_h(0)
            turn_in(2, 2, 1)

            def blk(i, q, u4, n4, last):
                gv_mul(i, q)
                turn_h(i - 1)
                if not last:
                    turn_in(i + 1, u4, n4)
                y_mul(i - 2, q)

            with pe.Fori(0, (BLOCKS - 3) // 4) as j:
                for u in range(4):
                    blk(j * 4 + (u + 2), u % 2, (u + 3) % 4, j + (u + 3) // 4 + 1, False)
            blk(BLOCKS - 1, (BLOCKS - 1) % 2, 0, 0, True)
            turn_h(BLOCKS - 1)
            y_mul(BLOCKS - 2, (BLOCKS - 2) % 2)
            y_mul(BLOCKS - 1, (BLOCKS - 1) % 2)

        @block.vector
        def _(dve):
            def stats(n, st, mv, ve, a, b_, var):
                for t in range(TT):
                    last = dve.bn_stats(st[:, t, :], region_x[:, bass.ds((n * TT + t) * D, D)])
                last.then_inc(a, 1)
                dve.wait_ge(a, n + 1)
                dve.sem_inc(stood_alone, 1)
                for t in range(TT):
                    last = dve.bn_aggr(mv[:, t, :], st[:, t, :])
                last.then_inc(b_, 1)
                dve.wait_ge(b_, n + 1)
                dve.tensor_scalar(ve[:, :], mv[:, :, 1], EPS, None, ALU.add).then_inc(var, 1)

            def norm(n, dst, mv, rs, rstd, done):
                dve.wait_ge(rstd, n + 1)
                for t in range(TT):
                    last = dve.tensor_scalar(dst[:, t, :], region_x[:, bass.ds((n * TT + t) * D, D)],
                                             mv[:, t, 0:1], rs[:, t:t + 1], ALU.subtract, ALU.mult)
                last.then_inc(done, 1)

            def x_low(n):
                dve.wait_ge(xhi_done, n + 1)
                dve.tensor_tensor(xh[:, :, LO, :], xn[:, :, :], xh[:, :, HI, :], ALU.subtract,
                                  ).then_inc(xh_done, 1)

            def x2_low(n):
                dve.wait_ge(x2hi_done, n + 1)
                dve.tensor_tensor(x2h[:, :, LO, :], xn2[:, :, :], x2h[:, :, HI, :], ALU.subtract,
                                  ).then_inc(x2h_done, 1)

            def turn_copy(n, dst, src16, mm, done, read, count):
                dve.wait_ge(mm, n + 1)
                if begun(count):
                    dve.wait_ge(read, count)
                dve.tensor_copy(dst[:, :, :, :].rearrange("p s k t -> p (s k t)"), src16).then_inc(done, 1)

            def qk_low(which, n):
                hi_done, done, src = ((q_hi, q_st, pa), (k_hi, k_st, pb))[which]
                dve.wait_ge(hi_done, n + 1)
                for m in range(KT):
                    last = dve.scalar_tensor_tensor(
                        out=qk_st[which][LO][:, m, :], in0=src[:, m * T:(m + 1) * T], scalar=bc[:, which, m:m + 1],
                        in1=qk_st[which][HI][:, m, :], op0=ALU.add, op1=ALU.subtract)
                last.then_inc(done, 1)

            def maxima(b, g):
                dve.wait_ge(s_mm, b * HG + g + 1)
                hs = slice(4 * g, 4 * g + 4)
                dve.tensor_reduce(mx[:, hs, 0], score[:, 0, :, :], AX.X, ALU.max)
                dve.tensor_reduce(mx[:, hs, 1], score[:, 1:3, :, :].rearrange("p s h t -> p h s t"), AX.XY,
                                  ALU.max).then_inc(max_done, 1)

            def context(b, g):
                dve.wait_ge(pv_mm, b * HG + g + 1)
                dve.reciprocal(rden[:, :], uden[:, T:2 * T]).then_inc(rden_done, 1)
                dve.wait_ge(rden_done, b * HG + g + 1)
                if begun(b * HG + g - 1):
                    dve.wait_ge(ctxhi_done, b * HG + g - 1)
                dve.tensor_tensor(ctx32[g][:, :], uden[:, 0:T], rden[:, :], ALU.mult).then_inc(umul_done, 1)

            def context_low(b, g):
                dve.wait_ge(ctxhi_done, b * HG + g + 1)
                dve.wait_ge(umul_done, b * HG + g + 1)
                dve.scalar_tensor_tensor(out=ctx_hl[LO][:, g, :], in0=ctx32[g][:, :], scalar=bc[:, 2, g:g + 1],
                                         in1=ctx_hl[HI][:, g, :], op0=ALU.add,
                                         op1=ALU.subtract).then_inc(ctx_done, 1)

            def residual(b):
                dve.wait_ge(o_mm, b + 1)
                dve.wait_ge(xb_done, b + 1)
                v = region_x[:, bass.ds(b * TT * D, TT * D)]
                dve.scalar_tensor_tensor(out=v, in0=pb, scalar=gsc[:, 0:1], in1=v, op0=ALU.mult,
                                         op1=ALU.add).then_inc(x1_done, 1)

            def logit_out(b):
                dve.wait_ge(r_mm, b + 1)
                dve.tensor_scalar(logits[:, bass.ds(b * TT * E, TT * E)], rout[:, 0:TT * E], 1.0 / WS, None,
                                  ALU.mult).then_inc(logit_done, 1)

            dve.sem_inc(logit_done, 1)
            dve.sem_inc(y_done, CREDIT)
            dve.wait_ge(x0_in, 16)
            stats(0, st1, mv1, ve1, ln1_a, ln1_b, var1)
            dve.wait_ge(consts_in, 16)
            dve.tensor_copy(ident[:, :], cst[:, C_ID:C_ID + P])
            dve.tensor_copy(identb[:, :], cst[:, C_ID:C_ID + P])
            dve.tensor_copy(mask_s[:, :, :], cst[:, C_MS:C_MS + P].unsqueeze(1).to_broadcast([P, 4, P]))
            dve.tensor_copy(mask_t[:, :, :], cst[:, C_MT:C_MT + P].unsqueeze(1).to_broadcast([P, 4, P]),
                              ).then_inc(setup_v, 1)
            dve.wait_ge(setup_v, 1)
            norm(0, xn, mv1, rs1, rstd1, xn_done)
            dve.wait_ge(small_in, 64)
            dve.tensor_scalar(bc[:, :, :].rearrange("p c k -> p (c k)"), bc_raw[:, :], WS, None, ALU.mult,
                              ).then_inc(setup_v, 1)
            dve.wait_ge(setup_v, 2)
            x_low(0)
            dve.wait_ge(aw_hi, 4)
            for c in range(4):
                dve.scalar_tensor_tensor(
                    out=aw[LO][:, c, :, :].rearrange("p k d -> p (k d)"), in0=region_w[:, c * KT * D:(c + 1) * KT * D],
                    scalar=WS, in1=aw[HI][:, c, :, :].rearrange("p k d -> p (k d)"), op0=ALU.mult,
                    op1=ALU.subtract).then_inc(aw_lo, 1)
                if c == 0:
                    turn_copy(0, xT, turn16, lt_mm, xT_done, q_mm, 0)
            qk_low(0, 0)
            dve.wait_ge(setup_a, 2)
            dve.scalar_tensor_tensor(out=gw[LO][:, :, :].rearrange("p k e -> p (k e)"), in0=gw_raw[:, :],
                                     scalar=WS, in1=gw[HI][:, :, :].rearrange("p k e -> p (k e)"),
                                     op0=ALU.mult, op1=ALU.subtract)
            dve.tensor_scalar(gsc[:, :], tg[:, 0:1], 1.0 / (WS * WS), None, ALU.mult)
            dve.tensor_copy(tri16[:, :], cst[:, C_TRI:C_TRI + P])
            dve.tensor_copy(one16[:, :], cst[:, C_ONE:C_ONE + P])
            dve.tensor_copy(io16[:, :], cst[:, C_IO:C_IO + P])
            dve.tensor_scalar(bo[:, :], bo[:, :], tg[:, 0:1], None, ALU.mult).then_inc(setup_v, 1)
            dve.wait_ge(setup_v, 3)
            qk_low(1, 0)

            def step(b, q, r, first, last):
                if not last:
                    if first:
                        dve.wait_ge(x_in, 16)
                    stats(b + 1, st1, mv1, ve1, ln1_a, ln1_b, var1)
                maxima(b, 0)
                if not last:
                    norm(b + 1, xn, mv1, rs1, rstd1, xn_done)
                if not first:
                    residual(b - 1)
                    dve.wait_ge(x1_done, b)
                    dve.sem_inc(stood_alone, 1)
                    stats(b - 1, st2, mv2, ve2, ln2_a, ln2_b, var2)
                if not last:
                    x_low(b + 1)
                maxima(b, 1)
                dve.wait_ge(max_done, b * HG + 2)
                dve.tensor_scalar(mneg[:, :], mx[:, :, :].rearrange("p h t -> p (h t)"), -1.0 / (WS * WS), None,
                                  ALU.mult).then_inc(mneg_done, 1)
                if not last:
                    turn_copy(b + 1, xT, turn16, lt_mm, xT_done, q_mm, b + 1)
                if not first:
                    norm(b - 1, xn2, mv2, rs2, rstd2, xn2_done)
                dve.wait_ge(mt_mm, b + 1)
                dve.tensor_copy(mrow[:, :], turn16[0:TT * H, 0:P]).then_inc(mrow_done, 1)
                if not last:
                    qk_low(0, b + 1)
                if not first:
                    x2_low(b - 1)
                if not last:
                    qk_low(1, b + 1)
                if not first:
                    turn_copy(b - 1, x2T, rout16, rt_mm, x2T_done, r_mm, b - 1)
                context(b, 0)
                if not first:
                    logit_out(b - 1)
                context_low(b, 0)
                context(b, 1)
                context_low(b, 1)

            steps(dve, step)
            residual(B - 1)
            dve.wait_ge(x1_done, B)
            stats(B - 1, st2, mv2, ve2, ln2_a, ln2_b, var2)
            norm(B - 1, xn2, mv2, rs2, rstd2, xn2_done)
            x2_low(B - 1)
            turn_copy(B - 1, x2T, rout16, rt_mm, x2T_done, r_mm, B - 1)
            logit_out(B - 1)

            def je(t):
                return t[:, :].rearrange("p (j e) -> p j e", e=E)

            def ej(t):
                return t[:, :].rearrange("p (e j) -> p e j", e=E)

            def each(t):
                return t[:, :].unsqueeze(2).to_broadcast([P, NT, E])

            dve.wait_ge(logit_done, B + 1)
            dve.wait_ge(wlo_done, WC * B)
            e8 = cst[:, C_E8:C_E8 + NT * E].rearrange("p (j e) -> p j e", e=E)
            dve.tensor_reduce(m1[:, :], je(logits), AX.X, ALU.max).then_inc(route_v, 1)
            dve.wait_ge(route_v, 1)
            dve.tensor_tensor(je(eq), je(logits), each(m1), ALU.is_equal).then_inc(route_v, 1)
            dve.wait_ge(route_v, 2)
            dve.tensor_tensor(je(eq), je(eq), e8, ALU.mult).then_inc(route_v, 1)
            dve.wait_ge(route_v, 3)
            dve.tensor_reduce(e1[:, :], je(eq), AX.X, ALU.min).then_inc(route_v, 1)
            dve.wait_ge(route_v, 4)
            dve.tensor_tensor(je(oh1), e8, each(e1), ALU.is_equal).then_inc(route_v, 1)
            dve.wait_ge(route_v, 5)
            dve.scalar_tensor_tensor(out=lmask[:, :], in0=oh1[:, :], scalar=NEVER, in1=logits[:, :],
                                     op0=ALU.mult, op1=ALU.add).then_inc(route_v, 1)
            dve.wait_ge(route_v, 6)
            dve.tensor_reduce(m2[:, :], je(lmask), AX.X, ALU.max).then_inc(route_v, 1)
            dve.wait_ge(route_v, 7)
            dve.tensor_tensor(pr2[:, :], m2[:, :], m1[:, :], ALU.subtract).then_inc(route_v, 1)
            dve.wait_ge(route_v, 8)
            dve.tensor_tensor(je(eq), je(lmask), each(m2), ALU.is_equal).then_inc(route_v, 1)
            dve.wait_ge(route_v, 9)
            dve.tensor_tensor(je(eq), je(eq), e8, ALU.mult).then_inc(route_v, 1)
            dve.wait_ge(route_v, 10)
            dve.tensor_reduce(e2[:, :], je(eq), AX.X, ALU.min).then_inc(route_v, 1)
            dve.wait_ge(route_v, 11)
            dve.tensor_tensor(je(oh2), e8, each(e2), ALU.is_equal).then_inc(route_v, 1)
            dve.wait_ge(route_v, 12)
            dve.tensor_tensor(both[:, :], oh1[:, :], oh2[:, :], ALU.add).then_inc(route_v, 1)
            dve.wait_ge(route_v, 13)
            dve.wait_ge(route_a, 1)
            dve.tensor_scalar(den[:, :], ex[:, :], 1.0, None, ALU.add).then_inc(route_v, 1)
            dve.wait_ge(route_v, 14)
            dve.reciprocal(pr1[:, :], den[:, :]).then_inc(route_v, 1)
            dve.wait_ge(route_v, 15)
            dve.tensor_scalar(pr1[:, :], pr1[:, :], tg[:, 1:2], None, ALU.mult).then_inc(route_v, 1)
            dve.wait_ge(route_v, 16)
            dve.tensor_tensor(pr2[:, :], ex[:, :], pr1[:, :], ALU.mult).then_inc(route_v, 1)
            dve.wait_ge(route_v, 17)
            dve.tensor_tensor(je(tmp), je(oh1), each(pr1), ALU.mult).then_inc(route_v, 1)
            dve.wait_ge(route_v, 18)
            dve.tensor_tensor(je(comb), je(oh2), each(pr2), ALU.mult).then_inc(route_v, 1)
            dve.wait_ge(route_v, 19)
            dve.tensor_tensor(comb[:, :], comb[:, :], tmp[:, :], ALU.add).then_inc(route_v, 1)
            dve.wait_ge(route_v, 20)
            dve.wait_ge(route_mm, 1)
            dve.tensor_copy(tot[:, :], ps[:, 2, 0:P]).then_inc(route_v, 1)
            dve.wait_ge(route_v, 21)
            dve.tensor_tensor_scan(out=scan[:, :], data0=cst[:, C_SC:C_SC + NT * E], data1=tot[:, :], initial=0.0,
                                   op0=ALU.mult, op1=ALU.add).then_inc(route_v, 1)
            dve.wait_ge(route_v, 22)
            dve.tensor_tensor(tot[:, :], scan[:, :], tot[:, :], ALU.subtract).then_inc(route_v, 1)
            dve.wait_ge(route_v, 23)
            dve.tensor_tensor(tot[:, :], ps[:, 1, 0:P], tot[:, :], ALU.add).then_inc(route_v, 1)
            dve.wait_ge(route_v, 24)
            dve.tensor_scalar(nblk[:, :], ej(scan)[:, :, NT - 1], float(P - 1), None, ALU.add).then_inc(route_v, 1)
            dve.wait_ge(route_v, 25)
            dve.tensor_scalar(nblk[:, :], nblk[:, :], 7, None, ALU.logical_shift_right).then_inc(route_v, 1)
            dve.wait_ge(route_v, 26)
            dve.tensor_copy(nblk_f[:, :], nblk[:, :]).then_inc(route_v, 1)
            dve.wait_ge(route_v, 27)
            dve.tensor_tensor_scan(out=start[:, :], data0=cst[:, C_ONE:C_ONE + E], data1=nblk_f[:, :],
                                   initial=0.0, op0=ALU.mult, op1=ALU.add).then_inc(route_v, 1)
            dve.wait_ge(route_v, 28)
            dve.tensor_tensor(start_s[:, :], start[:, :], nblk_f[:, :], ALU.subtract).then_inc(route_v, 1)
            dve.wait_ge(route_v, 29)
            dve.tensor_scalar(start_s[:, :], start_s[:, :], float(P), None, ALU.mult).then_inc(route_v, 1)
            dve.wait_ge(route_v, 30)
            dve.tensor_tensor(ej(base), ej(tot), start_s[:, :].unsqueeze(2).to_broadcast([P, E, NT]), ALU.add,
                              ).then_inc(route_v, 1)
            dve.wait_ge(route_v, 31)
            for k, oh in enumerate((oh1, oh2)):
                dve.tensor_tensor(je(tmp), je(oh), base[:, :].rearrange("p (e j) -> p j e", e=E), ALU.mult,
                                  ).then_inc(route_v, 1)
                dve.wait_ge(route_v, 32 + 2 * k)
                dve.tensor_reduce(pos[:, k * NT:(k + 1) * NT], je(tmp), AX.X, ALU.add).then_inc(route_v, 1)
                dve.wait_ge(route_v, 33 + 2 * k)
            dve.tensor_copy(pos_i[:, :], pos[:, :]).then_inc(route_v, 1)
            dve.wait_ge(route_v, 36)
            dve.tensor_scalar(hi_i[:, :], pos_i[:, :], 7, None, ALU.logical_shift_right).then_inc(route_v, 1)
            dve.wait_ge(route_v, 37)
            dve.tensor_scalar(lo_i[:, :], pos_i[:, :], P - 1, None, ALU.bitwise_and).then_inc(route_v, 1)
            dve.wait_ge(route_v, 38)
            dve.tensor_copy(hi_f[:, :], hi_i[:, :]).then_inc(route_v, 1)
            dve.wait_ge(route_v, 39)
            dve.tensor_copy(lo_f[:, :], lo_i[:, :]).then_inc(route_v, 1)
            dve.wait_ge(route_v, 40)
            dve.wait_ge(base_stored, 16 * B)
            for c in range(TOPK * NT):
                dve.tensor_scalar(hot_lo[:, c, :], io16[:, :], lo_f[:, c:c + 1], None, ALU.is_equal)
                last = dve.tensor_scalar(hot_blk[:, c, :], cst[:, C_BLK:C_BLK + BLOCKS], hi_f[:, c:c + 1],
                                         cst[:, C_TOK + c % NT:C_TOK + c % NT + 1], ALU.is_equal, ALU.mult)
            last.then_inc(route_v, 1)
            dve.wait_ge(route_v, R_HOT)
            dve.tensor_tensor(cmp[:, :].rearrange("p (c e) -> p c e", e=E - 1),
                              cst[0:1, C_BLK:C_BLK + BLOCKS].unsqueeze(2).to_broadcast([1, BLOCKS, E - 1]),
                              start[0:1, 0:E - 1].unsqueeze(1).to_broadcast([1, BLOCKS, E - 1]), ALU.is_ge,
                              ).then_inc(route_v, 1)
            dve.wait_ge(route_v, 42)
            dve.tensor_reduce(eidf[:, :], cmp[:, :].rearrange("p (c e) -> p c e", e=E - 1), AX.X, ALU.add,
                              ).then_inc(route_v, 1)
            dve.wait_ge(route_v, 43)
            dve.tensor_copy(eid[:, :], eidf[:, :]).then_inc(idx_done, 1)
            dve.wait_ge(table_mm, 1)
            dve.tensor_scalar(idx_f[:, :], ps[:, 3, 0:BLOCKS], float(N), None, ALU.add).then_inc(route_v, 1)
            dve.wait_ge(route_v, 44)
            dve.tensor_copy(idx_s[:, :], idx_f[:, :]).then_inc(idx_done, 1)
            dve.tensor_scalar(idx_g[:, :], idx_f[:, :], float(N - 1), None, ALU.min).then_inc(idx_done, 1)
            dve.wait_ge(idx_done, 3)

            def expert(i):
                return dve.value_load(eid[0:1, bass.ds(i, 1)], min_val=0, max_val=E - 1)

            def first_out(i, q, q4):
                e = expert(i)
                dve.wait_ge(gv_mm, i + 1)
                if not isinstance(i, int) or i > 3:
                    dve.wait_ge(yo_done, i - 3 + CREDIT)
                dve.tensor_copy(wslot[:, q4:q4 + 1], xg[q4].bitcast(F32)[:, bass.ds(e + D, 1)])
                if begun(i):
                    dve.wait_ge(h_done, i)
                for m, done in enumerate((g_done, v_half)):
                    dve.scalar_tensor_tensor(out=gv[:, m * F:(m + 1) * F], in0=gvp[q][:, m, :], scalar=1.0 / WS,
                                             in1=region_a[:, bass.ds(e * EB + m * F, F)], op0=ALU.mult,
                                             op1=ALU.add).then_inc(done, 1)

            def h_out(i):
                dve.wait_ge(silu_done, i + 1)
                dve.wait_ge(v_half, i + 1)
                if begun(i):
                    dve.wait_ge(hT_mm, i)
                dve.tensor_tensor(hh, gv[:, 0:F], gv[:, F:2 * F], ALU.mult).then_inc(h_done, 1)

            def h_low(i, q):
                dve.wait_ge(hT_hi, i + 1)
                dve.tensor_tensor(hT[q][LO], hTp, hT[q][HI], ALU.subtract).then_inc(hT_done, 1)

            def y_out(i, q):
                e = expert(i)
                dve.wait_ge(y_mm, i + 1)
                dve.wait_ge(yo_done, i - 1 + CREDIT)
                dve.scalar_tensor_tensor(out=yb[q], in0=yp[q][:, 0:D], scalar=1.0 / WS,
                                         in1=region_a[:, bass.ds(e * EB + 2 * F, D)], op0=ALU.mult,
                                         op1=ALU.add).then_inc(y_done, 1)

            dve.wait_ge(bias_in, 16)
            first_out(0, 0, 0)
            h_out(0)
            first_out(1, 1, 1)
            h_low(0, 0)
            h_out(1)

            def blk(i, q4):
                first_out(i, q4 % 2, q4)
                h_low(i - 1, 1 - q4 % 2)
                h_out(i)
                y_out(i - 2, q4 % 2)

            with dve.Fori(0, (BLOCKS - 3) // 4) as j:
                for u in range(4):
                    blk(j * 4 + (u + 2), (u + 2) % 4)
            blk(BLOCKS - 1, (BLOCKS - 1) % 4)
            h_low(BLOCKS - 1, (BLOCKS - 1) % 2)
            y_out(BLOCKS - 2, (BLOCKS - 2) % 2)
            y_out(BLOCKS - 1, (BLOCKS - 1) % 2)


SETUP_PE, SETUP_BIAS, SETUP_BO = 1, 2, 3
R_DIFF, R_BOTH, R_COMB, R_HOT = 8, 13, 20, 41


def kernel(**inputs):
    import concourse.bacc as _bacc
    from concourse.bass_utils import run_bass_kernel_spmd as _run

    a = {k: np.asarray(v) for k, v in inputs.items()}

    def tiles(w):
        o, i = w.shape[-2:]
        return np.moveaxis(np.swapaxes(w, -1, -2).reshape(*w.shape[:-2], i // P, P, o), -3, -2)

    def cols(v):
        return v.reshape(KT, P).T

    x = a["x"]
    y = np.swapaxes(a["ctx_1024"], 1, 2).reshape(B, KT, P, T).transpose(0, 2, 1, 3).reshape(B, P, KT * T)
    g = np.concatenate([a["g_xattn"], a["g_ffn"]])
    wattn = np.stack([tiles(a["L0_xattn_W" + n]) for n in "qkvo"], 1).reshape(P, 4 * KT * D)
    bcol = np.stack([cols(a["L0_xattn_b" + n]) for n in "qkv"], 1).reshape(P, 3 * KT)
    brow = a["L0_xattn_bo"][None, :]
    wgate = tiles(a["L0_ffn_Wg"]).reshape(P, KT * E)
    wffn = np.stack([tiles(a["L0_ffn_W" + n]).reshape(E, P, WE) for n in "123"], 1).reshape(E * WC, P, WE)
    bffn = np.concatenate([a["L0_ffn_b1"], a["L0_ffn_b2"], a["L0_ffn_b3"]], 1).reshape(1, E * EB)
    arrays = {"in_" + k: np.ascontiguousarray(v) for k, v in dict(
        x=x, y=y, g=g, wattn=wattn, bcol=bcol, brow=brow, wgate=wgate, wffn=wffn, bffn=bffn,
        consts=constants()).items()}

    nc = _bacc.Bacc("TRN2", target_bir_lowering=False, num_devices=1)
    args = [nc.dram_tensor(k, v.shape, mybir.dt.from_np(v.dtype), kind="ExternalInput").ap()
            for k, v in arrays.items()]
    args.append(nc.dram_tensor("out", (B, T, D), F32, kind="ExternalOutput").ap())
    flamingo_kernel(nc, *args)
    r = _run(nc, [arrays], core_ids=[0])
    return r.results[0]["out"]
```

```python
from contextlib import ExitStack

import numpy as np

import concourse.bass as bass
from concourse import mybir

ALU = mybir.AluOpType
ACT = mybir.ActivationFunctionType
AX = mybir.AxisListType
F32 = mybir.dt.float32
F16 = mybir.dt.float16
BF16 = mybir.dt.bfloat16
I32 = mybir.dt.int32

P = 128
B, T, D = 8, 256, 256
H, HD = 8, 32
E, F, TOPK = 8, 512, 2
TT = T // P
NT = B * TT
N = B * T
KT = D // P
FT = F // P
HG = H // 4
EPS = 1e-5
WS = 16.0
MASKED = -1.0e30
NEVER = -3.0e38
BLOCKS = (TOPK * N + E * (P - 1)) // P
WC = 3
WE = KT * F
EW = WC * WE
EB = 2 * F + D
ROW = D + E
HI, LO = 0, 1

C_ID, C_MS, C_MT, C_TRI, C_ONE, C_IO, C_E8, C_SC, C_TOK, C_BLK = np.cumsum(
    [0, P, P, P, P, P, P, NT * E, NT * E, NT]).tolist()
C_END = C_BLK + BLOCKS + 1


def constants():
    c = np.zeros((P, C_END), np.float32)
    i = np.arange(P)
    c[:, C_ID:C_ID + P] = np.eye(P)
    c[:, C_MS:C_MS + P] = np.where(i[None, :] > i[:, None], MASKED, 0.0)
    c[:, C_MT:C_MT + P] = np.where(i[:, None] > i[None, :], MASKED, 0.0)
    c[:, C_TRI:C_TRI + P] = i[:, None] < i[None, :]
    c[:, C_ONE:C_ONE + P] = 1.0
    c[:, C_IO:C_IO + P] = i[None, :]
    c[:, C_E8:C_E8 + NT * E] = np.tile(np.arange(E) - E, NT)[None, :]
    c[:, C_SC:C_SC + NT * E] = np.tile((np.arange(NT) > 0) * 1.0, E)[None, :]
    c[:, C_TOK:C_TOK + NT] = np.arange(NT)[None, :] * P + i[:, None] - N
    c[:, C_BLK:C_BLK + BLOCKS] = np.arange(BLOCKS)[None, :]
    return c


def flamingo_kernel(nc, x, y, g, wattn, bcol, brow, wgate, wffn, bffn, consts, out):
    ctx = ExitStack()
    with ctx:
        def sb(name, shape, dt):
            return ctx.enter_context(nc.sbuf_tensor(name, shape, dt))

        def sem(name):
            return ctx.enter_context(nc.semaphore(name))

        x_rows = x.rearrange("b (t p) d -> p (b t) d", p=P)
        out_rows = out.rearrange("b (t p) d -> p (b t) d", p=P)
        out_flat = out.rearrange("b t d -> (b t) d")
        rows = nc.dram_tensor("token_rows", (N, ROW), I32, kind="Internal").ap()
        rows_v = rows.rearrange("(j p) c -> p j c", p=P)

        w_hl = [sb("ffn_w_hi", [P, E * EW], F16), sb("ffn_w_lo", [P, E * EW], F16)]
        region_a = sb("region_a", [P, E * EB], F32)
        region_x = sb("region_x", [P, NT * D], F32)
        region_w = sb("region_w", [P, WC * WE], F32)
        cst = sb("constants", [P, C_END], F32)

        at = [0]

        def carve(region, n, dt=F32):
            words = n if dt in (F32, I32) else n // 2
            view = region[:, at[0]:at[0] + words]
            at[0] += words
            assert at[0] <= region.shape[1]
            return view if dt == F32 else view.bitcast(dt)

        q_stack = [carve(region_a, H * T, F16).rearrange("p (h t) -> p h t", h=H) for _ in range(2)]
        k_stack = [carve(region_a, H * T, F16).rearrange("p (h t) -> p h t", h=H) for _ in range(2)]
        probs = [carve(region_a, 3 * 4 * P).rearrange("p (s h t) -> p s h t", s=3, h=4) for _ in range(HG)]
        y_raw = [carve(region_a, KT * T) for _ in range(2)]
        v_sb = [carve(region_a, TT * D).rearrange("p (t d) -> p t d", t=TT) for _ in range(2)]
        xh = carve(region_a, TT * 2 * D, F16).rearrange("p (t s d) -> p t s d", t=TT, s=2)
        xT = carve(region_a, 2 * KT * T, F16).rearrange("p (s k t) -> p s k t", s=2, k=KT)
        yT = sb("yT", [P, 2, KT * T], F16)
        qk_st = [[sb(f"{n}_{s}", [P, HG, T], F16) for s in ("hi", "lo")] for n in "qk"]
        xn = sb("xn", [P, TT, D], F32)
        xn2 = sb("xn2", [P, TT, D], F32)
        x2h = sb("x2h", [P, TT, 2, D], F16)
        x2T = sb("x2T", [P, 2, KT, T], F16)
        rden = sb("rden", [P, T], F32)
        ctx32 = [sb(f"ctx32_{g}", [P, T], F32) for g in range(HG)]
        ctx_hl = [sb("ctx_hi", [P, HG, T], F16), sb("ctx_lo", [P, HG, T], F16)]
        aw = [sb("attn_w_hi", [P, 4, KT, D], F16), sb("attn_w_lo", [P, 4, KT, D], F16)]
        gw_raw = sb("gate_w_raw", [P, KT * E], F32)
        gw = [sb("gate_w_hi", [P, KT, E], F16), sb("gate_w_lo", [P, KT, E], F16)]
        bc_raw = sb("bias_cols_raw", [P, 3 * KT], F32)
        bc = sb("bias_cols", [P, 3, KT], F32)
        bo = sb("bo_rows", [P, D], F32)
        g_raw = sb("g_raw", [P, 2], F32)
        tg = sb("tanh_g", [P, 2], F32)
        gsc = sb("attn_scale", [P, 1], F32)
        ident = sb("ident", [P, P], F16)
        identb = sb("identb", [P, P], BF16)
        mask_s = sb("mask_s", [P, 4, P], BF16)
        mask_t = sb("mask_t", [P, 4, P], BF16)
        onesf = sb("onesf", [P, HD], F32)
        ve1 = sb("ve1", [P, TT], F32)
        ve2 = sb("ve2", [P, TT], F32)
        half = sb("minus_half", [P, TT], F32)
        st1 = sb("st1", [P, TT, 6], F32)
        mv1 = sb("mv1", [P, TT, 2], F32)
        rs1 = sb("rs1", [P, TT], F32)
        st2 = sb("st2", [P, TT, 6], F32)
        mv2 = sb("mv2", [P, TT, 2], F32)
        rs2 = sb("rs2", [P, TT], F32)
        mx = sb("row_max", [P, H, TT], F32)
        mneg = [sb(f"minus_max_{g}", [P, 4 * TT], F16) for g in range(HG)]
        mrow = [sb(f"shift_rows_{g}", [4 * TT, P], F16) for g in range(HG)]
        logits = sb("logits", [P, NT * E], F32)

        at[0] = 0
        hot_lo = carve(region_x, TOPK * NT * P, F16).rearrange("p (s c) -> p s c", c=P)
        hot_blk = carve(region_x, TOPK * NT * BLOCKS, F16).rearrange("p (s c) -> p s c", c=BLOCKS)
        at[0] = 0
        xg = [carve(region_x, ROW, I32) for _ in range(4)]
        xgT = [carve(region_x, 4 * P, F16) for _ in range(2)]
        at[0] = 0
        gv = carve(region_w, 2 * F)
        hh = carve(region_w, F)
        hT = [[carve(region_w, F, F16) for _ in range(2)] for _ in range(2)]
        yb = [carve(region_w, D) for _ in range(2)]
        yo = [sb(f"y_out_{i}", [P, D], F32) for i in range(2)]

        def rt(name, n=NT * E, dt=F32):
            return sb("rt_" + name, [P, n], dt)

        m1, m2, e1, e2 = (rt(n, NT) for n in ("m1", "m2", "e1", "e2"))
        at[0] = 0
        eq, oh1, oh2, lmask, base, comb, tmp, tot, scan = (carve(region_w, NT * E) for _ in range(9))
        both = rt("both", NT * E, F16)
        tri16 = sb("tri16", [P, P], F16)
        one16 = sb("one16", [P, P], F16)
        io16 = sb("io16", [P, P], F16)
        ex, den, pr1, pr2 = (rt(n, NT) for n in ("ex", "den", "pr1", "pr2"))
        nblk, nblk_f, start, start_s = rt("nblk", E, I32), rt("nblkf", E), rt("start", E), rt("starts", E)
        pos = rt("pos", TOPK * NT)
        pos_i, hi_i, lo_i = (rt(n, TOPK * NT, I32) for n in ("pos_i", "hi_i", "lo_i"))
        hi_f, lo_f = rt("hi_f", TOPK * NT), rt("lo_f", TOPK * NT)
        cmp = sb("rt_cmp", [1, (E - 1) * BLOCKS], F32)
        eidf = sb("rt_eidf", [1, BLOCKS], F32)
        eid = sb("block_expert", [1, BLOCKS], I32)
        wat = sb("block_weights", [1, BLOCKS], I32)
        idx_s = sb("scatter_rows", [P, BLOCKS], I32)
        idx_g = sb("gather_rows", [P, BLOCKS], I32)
        row_in = [sb(f"row_in_{i}", [P, 1], I32) for i in range(4)]
        row_out = [sb(f"row_out_{i}", [P, 1], I32) for i in range(2)]
        idx_f = rt("idx_f", BLOCKS)
        wslot = sb("slot_gate", [P, 4], F32)

        ps = ctx.enter_context(nc.psum_tensor("ps", [P, 8, 512], F32))
        turn = ps[:, 0, :]
        turn16 = turn.bitcast(F16)
        pa, pb = ps[:, 1, :], ps[:, 2, :]
        score = ps[:, 3:6, :].rearrange("p s (h t) -> p s h t", h=4)
        shift16 = [bank.bitcast(F16)[0:4 * TT, 0:P] for bank in (pb, turn)]
        uden = ps[:, 6, :]
        rout = ps[:, 7, :]
        rout16 = rout.bitcast(F16)
        gvp = [ps[:, 0:2, :], ps[:, 2:4, :]]
        hTp = ps[:, 4, :]
        xTp = ps[:, 5, :].bitcast(F16)
        yp = [ps[:, 6, :], ps[:, 7, :]]

        (stood_alone, consts_in, small_in, x0_in, x_in, base_stored, rows_stored,
         gates_stored, bias_in, setup_v, setup_a, setup_p, aw_hi, aw_lo, ln1_a, ln1_b, var1, rstd1,
         xn_done, xhi_done, xh_done, xT_done, ln2_a, ln2_b, var2, rstd2, xn2_done, x2hi_done, x2h_done,
         x2T_done, yhi_done, yT_done, whi_done, wlo_done, xb_done, q_mm, k_mm, v_mm, s_mm, t_mm,
         o_mm, lt_mm, mt_mm, rt_mm, r_mm, pv_mm, q_hi, q_st, k_hi, k_st, v_done, max_done, mneg_done,
         mrow_done, exp_done, rden_done, umul_done, ctxhi_done, ctx_done, x1_done, logit_done, row_in_done,
         row_out_done, route_v, route_a, route_mm, table_mm, idx_done, xgT_mm, xgT_done, gv_mm, g_done,
         v_half, silu_done, h_done, hT_mm, hT_hi, hT_done, y_mm, y_done, yo_done, added) = (
            sem(name) for name in (
                "stood_alone consts_in small_in x0_in x_in base_stored rows_stored "
                "gates_stored bias_in setup_v setup_a setup_p aw_hi aw_lo ln1_a ln1_b var1 rstd1 "
                "xn_done xhi_done xh_done xT_done ln2_a ln2_b var2 rstd2 xn2_done x2hi_done x2h_done "
                "x2T_done yhi_done yT_done whi_done wlo_done xb_done q_mm k_mm v_mm s_mm t_mm "
                "o_mm lt_mm mt_mm rt_mm r_mm pv_mm q_hi q_st k_hi k_st v_done max_done mneg_done "
                "mrow_done exp_done rden_done umul_done ctxhi_done ctx_done x1_done logit_done row_in_done "
                "row_out_done route_v route_a route_mm table_mm idx_done xgT_mm xgT_done gv_mm g_done "
                "v_half silu_done h_done hT_mm hT_hi hT_done y_mm y_done yo_done added "
            ).split())
        attnw_in, stack_in, y_in, w_in, xg_in, shift_in = ([sem(f"{name}_{i}") for i in range(n)] for name, n in (
            ("attnw_in", 2), ("stack_in", 2), ("y_in", 2), ("w_in", WC), ("xg_in", 4), ("shift_in", HG)))

        def begun(count):
            return not isinstance(count, int) or count > 0

        block = ctx.enter_context(nc.Block())

        def steps(eng, step):
            step(0, 0, 0)
            step(1, 1, 0)
            with eng.Fori(0, (B - 4) // 2) as i:
                step(i * 2 + 2, 0, i + 1)
                step(i * 2 + 3, 1, i + 1)
            for b in range(B - 2, B + 2):
                step(b, b % 2, b // 2)

        def has(n):
            return not isinstance(n, int) or 0 <= n < B

        def expert_values(engine, table, first, n, step):
            return nc.values_load_multi_w_load_instructions(
                table[0:1, bass.ds(first, n)], engines=[engine], min_val=0, max_val=(E - 1) * step,
                skip_runtime_bounds_check_because="an expert is a sum of E - 1 comparisons")[1]

        STACK = 16 * 6
        CREDIT = 2
        PAIRS = ((HI, HI), (HI, LO), (LO, HI))

        @block.sync
        def _(sp):
            def load_attn_w(half):
                cols = slice(half * 2 * KT * D, (half + 1) * 2 * KT * D)
                sp.dma_start(region_w[:, cols], wattn[:, cols]).then_inc(attnw_in[half], 16)

            sp.dma_start(region_x[:, 0:TT * D].rearrange("p (j d) -> p j d", d=D),
                         x_rows[:, 0:TT, :]).then_inc(x0_in, 16)
            load_attn_w(0)
            sp.dma_start(cst[:, :], consts).then_inc(consts_in, 16)
            sp.dma_start(bc_raw[:, :], bcol).then_inc(small_in, 16)
            sp.dma_start(y_raw[0], y[0]).then_inc(y_in[0], 16)
            load_attn_w(1)
            for dst, src in ((gw_raw[:, :], wgate),
                             (bo[:, :], brow.rearrange("a d -> (a d)").partition_broadcast(P)),
                             (g_raw[:, :], g.partition_broadcast(P))):
                sp.dma_start(dst, src).then_inc(small_in, 16)
            sp.dma_start(y_raw[1], y[1]).then_inc(y_in[1], 16)
            sp.dma_start(region_x[:, TT * D:].rearrange("p (j d) -> p j d", d=D),
                         x_rows[:, TT:, :]).then_inc(x_in, 16)

            def load_chunk(c, buf):
                sp.dma_start(region_w[:, buf * WE:(buf + 1) * WE],
                             wffn[bass.ds(c, 1)].rearrange("a p n -> (a p) n")).then_inc(w_in[buf], 16)

            def stack(which, dst, done, b, q):
                sp.wait_ge(done, b + 1)
                for c, part in enumerate((HI, LO, HI) if which == 0 else (HI, HI, LO)):
                    sp.dma_start(dst[HD * c:HD * (c + 1), :, :].rearrange("p (a m) t -> p a (m t)", m=HG),
                                 qk_st[which][part][:, :, :].rearrange("p m t -> p (m t)"),
                                 ).then_inc(stack_in[q], 16)

            stack(0, q_stack[0], q_st, 0, 0)
            stack(1, k_stack[0], k_st, 0, 0)
            sp.wait_ge(aw_lo, 4)
            for buf in range(WC):
                load_chunk(buf, buf)

            def shift(b, g, q):
                sp.wait_ge(mrow_done, b * HG + g + 1)
                sp.dma_start(q_stack[q][3 * HD:3 * HD + 1, 4 * g:4 * g + 4, :].rearrange("p h (t c) -> p (h t) c", t=TT),
                             mrow[g][:, :]).then_inc(shift_in[g], 16)

            def results(b):
                sp.wait_ge(x1_done, b + 1)
                sp.dma_start(out_rows[:, bass.ds(b * TT, TT), :],
                             region_x[:, bass.ds(b * TT * D, TT * D)].rearrange("p (j d) -> p j d", d=D),
                             ).then_inc(base_stored, 16)

            def row_store(b):
                sp.wait_ge(x2h_done, b + 1)
                sp.dma_start(rows_v[:, bass.ds(b * TT, TT), 0:D],
                             x2h[:, :, :, :].rearrange("p j s d -> p j (s d)").bitcast(I32)).then_inc(rows_stored, 16)

            def step(b, q, r):
                if has(b - 1) and has(b):
                    sp.wait_ge(wlo_done, b * WC)
                    load_chunk(b * WC + 2, 2)
                if has(b + 2):
                    sp.wait_ge(yT_done, b + 1)
                    sp.dma_start(y_raw[q], y[bass.ds(b + 2, 1)].rearrange("a p n -> (a p) n"),
                                 ).then_inc(y_in[q], 16)
                if has(b):
                    shift(b, 0, q)
                if has(b + 1):
                    sp.wait_ge(wlo_done, b * WC + 1)
                    load_chunk(b * WC + 3, 0)
                if has(b):
                    shift(b, 1, q)
                if has(b + 1):
                    if begun(b * HG):
                        sp.wait_ge(t_mm, b * HG)
                    sp.sem_inc(stood_alone, 1)
                    stack(0, q_stack[1 - q], q_st, b + 1, 1 - q)
                    stack(1, k_stack[1 - q], k_st, b + 1, 1 - q)
                if has(b - 1):
                    results(b - 1)
                if has(b + 1):
                    sp.wait_ge(wlo_done, b * WC + 2)
                    load_chunk(b * WC + 4, 1)
                if has(b - 1):
                    row_store(b - 1)

            steps(sp, step)
            sp.wait_ge(pv_mm, B * HG)
            sp.wait_ge(exp_done, B * HG)
            sp.dma_start(region_a[:, :], bffn.rearrange("a d -> (a d)").partition_broadcast(P),
                         ).then_inc(bias_in, 16)
            sp.wait_ge(route_v, R_COMB)
            sp.dma_start(rows_v[:, :, D:], comb[:, :].bitcast(I32).rearrange("p (j c) -> p j c", j=NT),
                         ).then_inc(gates_stored, 16)
            sp.wait_ge(base_stored, 16 * B)
            sp.wait_ge(rows_stored, 16 * B)
            sp.wait_ge(gates_stored, 16)

        @block.scalar
        def _(act):
            act.sem_inc(yo_done, CREDIT)
            def attn_w_high(c):
                act.wait_ge(attnw_in[c // 2], 16)
                act.activation(aw[HI][:, c, :, :].rearrange("p k d -> p (k d)"),
                               region_w[:, c * KT * D:(c + 1) * KT * D], ACT.Copy, scale=WS).then_inc(aw_hi, 1)

            def split_chunk(b, buf):
                act.wait_ge(w_in[buf], (b + 1) * 16)
                raw = region_w[:, buf * WE:(buf + 1) * WE]
                act.activation(w_hl[HI][:, bass.ds((b * WC + buf) * WE, WE)], raw, ACT.Copy, scale=WS)
                act.activation(raw, raw, ACT.Copy, scale=WS).then_inc(whi_done, 1)

            def x_high(n):
                act.wait_ge(xn_done, n + 1)
                if begun(n):
                    act.wait_ge(lt_mm, n)
                act.activation(xh[:, :, HI, :], xn[:, :, :], ACT.Copy).then_inc(xhi_done, 1)

            def y_high(n, q, r):
                act.wait_ge(y_in[q], (r + 1) * 16)
                if begun(n):
                    act.wait_ge(v_mm, n)
                act.activation(yT[:, HI, :], y_raw[q], ACT.Copy).then_inc(yhi_done, 1)

            def qk_high(which, n):
                mm, done, src = ((q_mm, q_hi, pa), (k_mm, k_hi, pb))[which]
                act.wait_ge(mm, n + 1)
                if begun((n - 1) * HG + 1):
                    act.wait_ge(s_mm, (n - 1) * HG + 1)
                for m in range(KT):
                    last = act.activation(qk_st[which][HI][:, m, :], src[:, m * T:(m + 1) * T], ACT.Identity,
                                          bias=bc[:, which, m:m + 1])
                last.then_inc(done, 1)

            def v_out(n, q):
                act.wait_ge(v_mm, n + 1)
                if begun((n - 1) * HG):
                    act.wait_ge(pv_mm, (n - 1) * HG)
                act.activation(v_sb[q].rearrange("p t d -> p (t d)"), pa, ACT.Copy).then_inc(v_done, 1)

            def expo(b, g):
                act.wait_ge(t_mm, b * HG + g + 1)
                if begun(b * HG - HG + g + 1):
                    act.wait_ge(pv_mm, b * HG - HG + g + 1)
                act.activation(probs[g].rearrange("p s h t -> p (s h t)"),
                               score.rearrange("p s h t -> p (s h t)"), ACT.Exp,
                               scale=float(HD) ** -0.5 / (WS * WS)).then_inc(exp_done, 1)

            def ctx_high(b, g):
                act.wait_ge(umul_done, b * HG + g + 1)
                if begun(b):
                    act.wait_ge(o_mm, b)
                act.activation(ctx_hl[HI][:, g, :], ctx32[g][:, :], ACT.Identity,
                               bias=bc[:, 2, g:g + 1]).then_inc(ctxhi_done, 1)

            def x2_high(b):
                act.wait_ge(xn2_done, b + 1)
                if begun(b * 16):
                    act.wait_ge(rows_stored, b * 16)
                if begun(b):
                    act.wait_ge(rt_mm, b)
                act.activation(x2h[:, :, HI, :], xn2[:, :, :], ACT.Copy).then_inc(x2hi_done, 1)

            def x2_turn_out(b):
                act.wait_ge(rt_mm, b + 1)
                if begun(b):
                    act.wait_ge(r_mm, b)
                act.activation(x2T[:, :, :, :].rearrange("p s k t -> p (s k t)"), rout16,
                               ACT.Copy).then_inc(x2T_done, 1)

            def shift_out(b, g):
                act.wait_ge(mt_mm, b * HG + g + 1)
                if begun(b):
                    act.wait_ge(shift_in[g], b * 16)
                act.activation(mrow[g][:, :], shift16[g], ACT.Copy).then_inc(mrow_done, 1)

            attn_w_high(0)
            x_high(0)
            attn_w_high(1)
            y_high(0, 0, 0)
            attn_w_high(2)
            attn_w_high(3)
            act.wait_ge(small_in, 64)
            act.activation(gw[HI][:, :, :].rearrange("p k e -> p (k e)"), gw_raw[:, :], ACT.Copy,
                           scale=WS).then_inc(setup_a, 1)
            act.activation(tg[:, :], g_raw[:, :], ACT.Tanh).then_inc(setup_a, 1)
            act.wait_ge(setup_v, SETUP_BIAS)
            qk_high(0, 0)
            qk_high(1, 0)
            x_high(1)

            def step(b, q, r):
                if has(b):
                    v_out(b, q)
                if has(b + 1):
                    y_high(b + 1, 1 - q, r + q)
                if has(b):
                    split_chunk(b, 0)
                if has(b - 2):
                    x2_turn_out(b - 2)
                if has(b):
                    shift_out(b, 0)
                if has(b - 1):
                    ctx_high(b - 1, 1)
                if has(b + 1):
                    qk_high(0, b + 1)
                    qk_high(1, b + 1)
                if has(b):
                    shift_out(b, 1)
                    expo(b, 0)
                    split_chunk(b, 1)
                    expo(b, 1)
                if has(b + 2):
                    x_high(b + 2)
                if has(b - 1):
                    x2_high(b - 1)
                if has(b):
                    split_chunk(b, 2)
                    ctx_high(b, 0)

            steps(act, step)
            act.wait_ge(route_v, R_DIFF)
            act.activation(ex[:, :], pr2[:, :], ACT.Exp).then_inc(route_a, 1)

            def silu(i):
                act.wait_ge(g_done, i + 1)
                act.activation(gv[:, 0:F], gv[:, 0:F], ACT.Silu).then_inc(silu_done, 1)

            def h_high(i, q):
                act.wait_ge(hT_mm, i + 1)
                if begun(i - 1):
                    act.wait_ge(y_mm, i - 1)
                act.activation(hT[q][HI], hTp, ACT.Copy).then_inc(hT_hi, 1)

            def turn_out(i, q):
                act.wait_ge(xgT_mm, i + 1)
                if begun(i - 1):
                    act.wait_ge(gv_mm, i - 1)
                act.activation(xgT[q], xTp[:, 0:4 * P], ACT.Copy).then_inc(xgT_done, 1)

            def gate(i, q, q4):
                act.wait_ge(y_done, i + 1 + CREDIT)
                if begun((i - 1) * 16):
                    act.wait_ge(added, (i - 1) * 16)
                act.activation(yo[q][:, :], yb[q], ACT.Copy, scale=wslot[:, q4:q4 + 1]).then_inc(yo_done, 1)

            turn_out(0, 0)
            turn_out(1, 1)
            silu(0)
            h_high(0, 0)
            turn_out(2, 0)
            silu(1)

            def blk(i, q4, last):
                h_high(i - 1, 1 - q4 % 2)
                if not last:
                    turn_out(i + 1, 1 - q4 % 2)
                silu(i)
                gate(i - 2, q4 % 2, (q4 + 2) % 4)

            for i in range(2, 6):
                blk(i, i % 4, False)
            with act.Fori(0, (BLOCKS - 7) // 4) as j:
                for u in range(4):
                    blk(j * 4 + (u + 6), (u + 2) % 4, False)
            blk(BLOCKS - 1, (BLOCKS - 1) % 4, True)
            h_high(BLOCKS - 1, (BLOCKS - 1) % 2)
            gate(BLOCKS - 2, (BLOCKS - 2) % 2, (BLOCKS - 2) % 4)
            gate(BLOCKS - 1, (BLOCKS - 1) % 2, (BLOCKS - 1) % 4)

        @block.gpsimd
        def _(pool):
            pool.memset(half[:, :], -0.5).then_inc(setup_p, 1)
            pool.memset(onesf[:, :], 1.0).then_inc(setup_p, 1)
            for q in range(2):
                pool.wait_ge(setup_p, 2 + q)
                pool.memset(k_stack[q][96:97, :, :], WS * WS).then_inc(setup_p, 1)

            def rstd(n, var, ve, rs, done):
                pool.wait_ge(var, n + 1)
                pool.tensor_tensor(rs[:, :], ve[:, :], half[:, :], ALU.pow).then_inc(done, 1)

            def y_low(n, q):
                pool.wait_ge(yhi_done, n + 1)
                pool.tensor_tensor(yT[:, LO, :], y_raw[q], yT[:, HI, :], ALU.subtract).then_inc(yT_done, 1)

            def w_low(b, buf):
                pool.wait_ge(whi_done, b * WC + buf + 1)
                c = (b * WC + buf) * WE
                pool.tensor_tensor(w_hl[LO][:, bass.ds(c, WE)], region_w[:, buf * WE:(buf + 1) * WE],
                                   w_hl[HI][:, bass.ds(c, WE)], ALU.subtract).then_inc(wlo_done, 1)

            def add_bo(b):
                pool.wait_ge(xn_done, b + 1)
                v = region_x[:, bass.ds(b * TT * D, TT * D)].rearrange("p (j d) -> p j d", d=D)
                pool.tensor_tensor(v, v, bo[:, :].unsqueeze(1).to_broadcast([P, TT, D]), ALU.add).then_inc(xb_done, 1)

            def x_low(n):
                pool.wait_ge(xhi_done, n + 1)
                pool.tensor_tensor(xh[:, :, LO, :], xn[:, :, :], xh[:, :, HI, :], ALU.subtract,
                                   ).then_inc(xh_done, 1)

            def x2_low(n):
                pool.wait_ge(x2hi_done, n + 1)
                pool.tensor_tensor(x2h[:, :, LO, :], xn2[:, :, :], x2h[:, :, HI, :], ALU.subtract,
                                   ).then_inc(x2h_done, 1)

            pool.wait_ge(setup_p, 4)
            rstd(0, var1, ve1, rs1, rstd1)
            x_low(0)
            y_low(0, 0)
            rstd(1, var1, ve1, rs1, rstd1)
            x_low(1)
            pool.wait_ge(setup_v, SETUP_BO)

            def step(b, q, r):
                if has(b + 1):
                    y_low(b + 1, 1 - q)
                if has(b):
                    w_low(b, 0)
                    add_bo(b)
                if has(b + 2):
                    rstd(b + 2, var1, ve1, rs1, rstd1)
                if has(b - 1):
                    rstd(b - 1, var2, ve2, rs2, rstd2)
                if has(b):
                    w_low(b, 1)
                if has(b + 2):
                    x_low(b + 2)
                if has(b - 1):
                    x2_low(b - 1)
                if has(b):
                    w_low(b, 2)

            steps(pool, step)

            def gather(i, q):
                if begun(i - 3):
                    pool.wait_ge(v_half, i - 3)
                pool.tensor_copy(row_in[q][:, :], idx_g[:, bass.ds(i, 1)]).then_inc(row_in_done, 1)
                pool.wait_ge(row_in_done, i + 1)
                pool.sem_inc(stood_alone, 1)
                pool.indirect_dma_start(xg[q], None, rows,
                                        bass.IndirectOffsetOnAxis(ap=row_in[q][:, :], axis=0),
                                        ).then_inc(xg_in[q], 16)

            def add_rows(i, q):
                pool.tensor_copy(row_out[q][:, :], idx_s[:, bass.ds(i, 1)]).then_inc(row_out_done, 1)
                pool.wait_ge(row_out_done, i + 1)
                pool.wait_ge(yo_done, i + 1 + CREDIT)
                if not isinstance(i, int) or i > 0:
                    pool.wait_ge(added, i * 16)
                    pool.sem_inc(stood_alone, 1)
                pool.indirect_dma_start(out_flat, bass.IndirectOffsetOnAxis(ap=row_out[q][:, :], axis=0),
                                        yo[q][:, :], None, bounds_check=N - 1, oob_is_err=False,
                                        compute_op=ALU.add).then_inc(added, 16)

            pool.wait_ge(rows_stored, 16 * B)
            pool.wait_ge(gates_stored, 16)
            pool.wait_ge(base_stored, 16 * B)
            pool.wait_ge(idx_done, 4)
            for i in range(4):
                gather(i, i)

            def blk(i, q4):
                gather(i + 4, q4)
                add_rows(i, q4 % 2)

            for i in range(4):
                blk(i, i)
            with pool.Fori(0, (BLOCKS - 8) // 4) as j:
                for u in range(4):
                    blk(j * 4 + (u + 4), u)
            done = (BLOCKS - 4) // 4 * 4
            for i in range(done, BLOCKS):
                if i + 4 < BLOCKS:
                    gather(i + 4, i % 4)
                add_rows(i, i % 2)
            pool.wait_ge(added, 16 * BLOCKS)

        @block.tensor
        def _(pe):
            def split_mm(dst, left, right, kts=KT):
                n = 0
                for k in range(kts):
                    for a, c in PAIRS:
                        mm = pe.matmul(dst, left(a, k), right(c, k), start=(n == 0), stop=(n == 3 * kts - 1))
                        n += 1
                return mm

            def turns(src, dst16):
                for t in range(TT):
                    for h in (HI, LO):
                        for k in range(KT):
                            o = (h * KT + k) * T + t * P
                            mm = pe.transpose(dst16[:, o:o + P], src[:, t, h, k * P:(k + 1) * P], ident[:, :])
                return mm

            def x_turn(n):
                pe.wait_ge(xh_done, n + 1)
                if begun((n - 1) * HG):
                    pe.wait_ge(mrow_done, (n - 1) * HG)
                turns(xh, turn16).then_inc(lt_mm, 1)

            def q_mul(n):
                pe.wait_ge(xT_done, n + 1)
                if begun(n):
                    pe.wait_ge(v_done, n)
                for m in range(KT):
                    mm = split_mm(pa[:, m * T:(m + 1) * T], lambda a, k: aw[a][:, 0, k, m * P:(m + 1) * P],
                                  lambda c, k: xT[:, c, k, :])
                mm.then_inc(q_mm, 1)

            def k_mul(n):
                pe.wait_ge(yT_done, n + 1)
                if begun((n - 1) * HG + 1):
                    pe.wait_ge(mrow_done, (n - 1) * HG + 1)
                for m in range(KT):
                    mm = split_mm(pb[:, m * T:(m + 1) * T], lambda a, k: aw[a][:, 1, k, m * P:(m + 1) * P],
                                  lambda c, k: yT[:, c, k * T:(k + 1) * T])
                mm.then_inc(k_mm, 1)

            def v_mul(n):
                pe.wait_ge(q_st, n + 1)
                for t in range(TT):
                    mm = split_mm(pa[:, t * D:(t + 1) * D],
                                  lambda a, k: yT[:, a, k * T + t * P:k * T + (t + 1) * P],
                                  lambda c, k: aw[c][:, 2, k, :])
                mm.then_inc(v_mm, 1)

            def scores(b, g, q):
                for bank, (tq, tk) in enumerate(((0, 0), (1, 0), (1, 1))):
                    if tq == tk:
                        pe.matmul(score[:, bank, :, :], identb[:, :], mask_s[:, :, :], start=True, stop=True)
                    for h in range(4):
                        mm = pe.matmul(score[:, bank, h, :], q_stack[q][0:96, 4 * g + h, tq * P:(tq + 1) * P],
                                       k_stack[q][0:96, 4 * g + h, tk * P:(tk + 1) * P],
                                       start=(tq != tk and h == 0), stop=True, skip_group_check=True)
                mm.then_inc(s_mm, 1)

            def scores_t(b, g, q):
                for bank, (tk, tq) in enumerate(((0, 0), (0, 1), (1, 1))):
                    if tq == tk:
                        pe.matmul(score[:, bank, :, :], identb[:, :], mask_t[:, :, :], start=True, stop=True)
                    for h in range(4):
                        mm = pe.matmul(score[:, bank, h, :], k_stack[q][0:97, 4 * g + h, tk * P:(tk + 1) * P],
                                       q_stack[q][0:97, 4 * g + h, tq * P:(tq + 1) * P],
                                       start=(tq != tk and h == 0), stop=True, skip_group_check=True)
                mm.then_inc(t_mm, 1)

            def mix(b, g, q):
                pe.wait_ge(exp_done, b * HG + g + 1)
                if begun(b * HG + g):
                    pe.wait_ge(umul_done, b * HG + g)
                for tk, w, col in ((0, T, 0), (1, P, P)):
                    for part in range(2):
                        for h in range(4):
                            left = onesf[:, :] if part else v_sb[q][:, tk, (4 * g + h) * HD:(4 * g + h + 1) * HD]
                            p = probs[g][:, 0:2, h, :] if tk == 0 else probs[g][:, 2:3, h, :]
                            o = uden[32 * h:32 * h + 32, part * T + col:part * T + col + w]
                            mm = pe.matmul(o.rearrange("p (s t) -> p s t", t=P), left, p,
                                           start=(tk == 0 and part == 0), stop=True,
                                           skip_group_check=True)
                mm.then_inc(pv_mm, 1)

            def o_mul(b):
                pe.wait_ge(ctx_done, (b + 1) * HG)
                if begun(b):
                    pe.wait_ge(logit_done, b)
                for t in range(TT):
                    mm = split_mm(rout[:, t * D:(t + 1) * D], lambda a, k: ctx_hl[a][:, k, t * P:(t + 1) * P],
                                  lambda c, k: aw[c][:, 3, k, :])
                mm.then_inc(o_mm, 1)

            def r_turn(b):
                pe.wait_ge(x2h_done, b + 1)
                turns(x2h, rout16).then_inc(rt_mm, 1)

            def r_mul(b):
                pe.wait_ge(x2T_done, b + 1)
                for t in range(TT):
                    mm = split_mm(rout[:, t * E:(t + 1) * E], lambda a, k: x2T[:, a, k, t * P:(t + 1) * P],
                                  lambda c, k: gw[c][:, k, :])
                mm.then_inc(r_mm, 1)

            pe.wait_ge(setup_v, SETUP_PE)
            pe.wait_ge(setup_p, 4)
            x_turn(0)
            pe.wait_ge(aw_lo, 1)
            q_mul(0)
            pe.wait_ge(aw_lo, 2)
            k_mul(0)
            pe.wait_ge(aw_lo, 3)
            v_mul(0)
            pe.wait_ge(aw_lo, 4)

            def shift_turn(b, g):
                pe.wait_ge(mneg_done, b * HG + g + 1)
                if g == 0:
                    pe.wait_ge(k_st, b + 1)
                elif has(b + 1):
                    pe.wait_ge(xT_done, b + 2)
                else:
                    pe.wait_ge(xT_done, B)
                pe.transpose(shift16[g], mneg[g][:, :], ident[:, :]).then_inc(mt_mm, 1)

            pe.wait_ge(setup_v, SETUP_MASKS)

            def step(b, q, r):
                if has(b):
                    pe.wait_ge(stack_in[q], (r + 1) * STACK)
                    if begun(b * HG):
                        pe.wait_ge(exp_done, b * HG)
                    scores(b, 0, q)
                if has(b - 1):
                    mix(b - 1, 1, 1 - q)
                if has(b - 2):
                    r_turn(b - 2)
                if has(b + 1):
                    x_turn(b + 1)
                if has(b):
                    shift_turn(b, 0)
                    pe.wait_ge(max_done, b * HG + 1)
                    scores(b, 1, q)
                if has(b + 1):
                    q_mul(b + 1)
                if has(b - 2):
                    r_mul(b - 2)
                if has(b + 1):
                    k_mul(b + 1)
                if has(b):
                    shift_turn(b, 1)
                    pe.wait_ge(max_done, b * HG + 2)
                    pe.wait_ge(shift_in[0], (b + 1) * 16)
                    scores_t(b, 0, q)
                if has(b - 1):
                    o_mul(b - 1)
                if has(b):
                    pe.wait_ge(shift_in[1], (b + 1) * 16)
                    pe.wait_ge(exp_done, b * HG + 1)
                    scores_t(b, 1, q)
                if has(b + 1):
                    v_mul(b + 1)
                if has(b):
                    mix(b, 0, q)

            steps(pe, step)

            pe.wait_ge(route_v, R_BOTH)
            both_v = both[:, :].rearrange("p (j e) -> p e j", e=E)
            pe.matmul(ps[:, 1, 0:P], tri16[:, :], both_v, start=True, stop=True)
            pe.matmul(ps[:, 2, 0:P], one16[:, :], both_v, start=True, stop=True).then_inc(route_mm, 1)
            pe.wait_ge(route_v, R_HOT)
            for c in range(TOPK * NT):
                mm = pe.matmul(ps[:, 3, 0:BLOCKS], hot_lo[:, c, :], hot_blk[:, c, :], start=(c == 0),
                               stop=(c == TOPK * NT - 1))
            mm.then_inc(table_mm, 1)

            def turn_in(i, q4, n4):
                pe.wait_ge(xg_in[q4], n4 * 16)
                if begun(i):
                    pe.wait_ge(xgT_done, i)
                for c in range(4):
                    mm = pe.transpose(xTp[:, c * P:(c + 1) * P], xg[q4].bitcast(F16)[:, c * P:(c + 1) * P], ident[:, :])
                mm.then_inc(xgT_mm, 1)

            def gv_mul(i, q, at):
                pe.wait_ge(xgT_done, i + 1)
                if begun(i - 1):
                    pe.wait_ge(v_half, i - 1)
                for m in range(2):
                    mm = split_mm(gvp[q][:, m, :], lambda a, k: xgT[q][:, (a * KT + k) * P:(a * KT + k + 1) * P],
                                  lambda c, k: w_hl[c][:, bass.ds(at + (m * WE + k * F), F)])
                mm.then_inc(gv_mm, 1)

            def turn_h(i):
                pe.wait_ge(h_done, i + 1)
                if begun(i):
                    pe.wait_ge(hT_done, i)
                for k in range(FT):
                    mm = pe.transpose(hTp[:, k * P:(k + 1) * P], hh[:, k * P:(k + 1) * P], cst[:, C_ID:C_ID + P])
                mm.then_inc(hT_mm, 1)

            def y_mul(i, q, at):
                pe.wait_ge(hT_done, i + 1)
                pe.wait_ge(y_done, i - 1 + CREDIT)
                split_mm(yp[q][:, 0:D], lambda a, k: hT[q][a][:, k * P:(k + 1) * P],
                         lambda c, k: w_hl[c][:, bass.ds(at + (2 * WE + k * D), D)],
                         FT).then_inc(y_mm, 1)

            pe.wait_ge(wlo_done, WC * B)
            pe.wait_ge(idx_done, 4)
            at = expert_values(mybir.EngineType.PE, wat, 0, 2, EW)
            turn_in(0, 0, 1)
            turn_in(1, 1, 1)
            gv_mul(0, 0, at[0])
            gv_mul(1, 1, at[1])
            turn_h(0)
            turn_in(2, 2, 1)

            def blk(i, q, u4, n4, last, here, before):
                gv_mul(i, q, here)
                turn_h(i - 1)
                if not last:
                    turn_in(i + 1, u4, n4)
                y_mul(i - 2, q, before)

            with pe.Fori(0, (BLOCKS - 3) // 4) as j:
                at = expert_values(mybir.EngineType.PE, wat, j * 4, 6, EW)
                for u in range(4):
                    blk(j * 4 + (u + 2), u % 2, (u + 3) % 4, j + (u + 3) // 4 + 1, False, at[u + 2], at[u])
            at = expert_values(mybir.EngineType.PE, wat, BLOCKS - 3, 3, EW)
            blk(BLOCKS - 1, (BLOCKS - 1) % 2, 0, 0, True, at[2], at[0])
            turn_h(BLOCKS - 1)
            y_mul(BLOCKS - 2, (BLOCKS - 2) % 2, at[1])
            y_mul(BLOCKS - 1, (BLOCKS - 1) % 2, at[2])

        @block.vector
        def _(dve):
            def stats(n, st, mv, ve, a, b_, var):
                for t in range(TT):
                    last = dve.bn_stats(st[:, t, :], region_x[:, bass.ds((n * TT + t) * D, D)])
                last.then_inc(a, 1)
                dve.wait_ge(a, n + 1)
                dve.sem_inc(stood_alone, 1)
                for t in range(TT):
                    last = dve.bn_aggr(mv[:, t, :], st[:, t, :])
                last.then_inc(b_, 1)
                dve.wait_ge(b_, n + 1)
                dve.tensor_scalar(ve[:, :], mv[:, :, 1], EPS, None, ALU.add).then_inc(var, 1)

            def norm(n, dst, mv, rs, rstd, done, low_done):
                dve.wait_ge(rstd, n + 1)
                if begun(n):
                    dve.wait_ge(low_done, n)
                for t in range(TT):
                    last = dve.tensor_scalar(dst[:, t, :], region_x[:, bass.ds((n * TT + t) * D, D)],
                                             mv[:, t, 0:1], rs[:, t:t + 1], ALU.subtract, ALU.mult)
                last.then_inc(done, 1)

            def x_turn_out(n):
                dve.wait_ge(lt_mm, n + 1)
                if begun(n):
                    dve.wait_ge(q_mm, n)
                dve.tensor_copy(xT[:, :, :, :].rearrange("p s k t -> p (s k t)"), turn16).then_inc(xT_done, 1)

            def qk_low(which, n):
                hi_done, done, src = ((q_hi, q_st, pa), (k_hi, k_st, pb))[which]
                dve.wait_ge(hi_done, n + 1)
                for m in range(KT):
                    last = dve.scalar_tensor_tensor(
                        out=qk_st[which][LO][:, m, :], in0=src[:, m * T:(m + 1) * T], scalar=bc[:, which, m:m + 1],
                        in1=qk_st[which][HI][:, m, :], op0=ALU.add, op1=ALU.subtract)
                last.then_inc(done, 1)

            def maxima(b, g):
                dve.wait_ge(s_mm, b * HG + g + 1)
                hs = slice(4 * g, 4 * g + 4)
                dve.tensor_reduce(mx[:, hs, 0], score[:, 0, :, :], AX.X, ALU.max)
                dve.tensor_reduce(mx[:, hs, 1], score[:, 1:3, :, :].rearrange("p s h t -> p h s t"), AX.XY,
                                  ALU.max).then_inc(max_done, 1)
                dve.wait_ge(max_done, b * HG + g + 1)
                dve.tensor_scalar(mneg[g][:, :], mx[:, hs, :].rearrange("p h t -> p (h t)"), -1.0 / (WS * WS), None,
                                  ALU.mult).then_inc(mneg_done, 1)

            def context(b, g):
                dve.wait_ge(pv_mm, b * HG + g + 1)
                dve.reciprocal(rden[:, :], uden[:, T:2 * T]).then_inc(rden_done, 1)
                dve.wait_ge(rden_done, b * HG + g + 1)
                if begun(b * HG + g - 1):
                    dve.wait_ge(ctxhi_done, b * HG + g - 1)
                dve.tensor_tensor(ctx32[g][:, :], uden[:, 0:T], rden[:, :], ALU.mult).then_inc(umul_done, 1)

            def context_low(b, g):
                dve.wait_ge(ctxhi_done, b * HG + g + 1)
                dve.wait_ge(umul_done, b * HG + g + 1)
                dve.scalar_tensor_tensor(out=ctx_hl[LO][:, g, :], in0=ctx32[g][:, :], scalar=bc[:, 2, g:g + 1],
                                         in1=ctx_hl[HI][:, g, :], op0=ALU.add,
                                         op1=ALU.subtract).then_inc(ctx_done, 1)

            def residual(b):
                dve.wait_ge(o_mm, b + 1)
                dve.wait_ge(xb_done, b + 1)
                v = region_x[:, bass.ds(b * TT * D, TT * D)]
                dve.scalar_tensor_tensor(out=v, in0=rout, scalar=gsc[:, 0:1], in1=v, op0=ALU.mult,
                                         op1=ALU.add).then_inc(x1_done, 1)

            def logit_out(b):
                dve.wait_ge(r_mm, b + 1)
                dve.tensor_scalar(logits[:, bass.ds(b * TT * E, TT * E)], rout[:, 0:TT * E], 1.0 / WS, None,
                                  ALU.mult).then_inc(logit_done, 1)

            dve.sem_inc(y_done, CREDIT)
            dve.wait_ge(x0_in, 16)
            stats(0, st1, mv1, ve1, ln1_a, ln1_b, var1)
            norm(0, xn, mv1, rs1, rstd1, xn_done, xh_done)
            dve.wait_ge(consts_in, 16)
            dve.tensor_copy(ident[:, :], cst[:, C_ID:C_ID + P]).then_inc(setup_v, 1)
            dve.wait_ge(setup_v, 1)

            def attn_w_low(c):
                dve.wait_ge(aw_hi, c + 1)
                dve.scalar_tensor_tensor(
                    out=aw[LO][:, c, :, :].rearrange("p k d -> p (k d)"), in0=region_w[:, c * KT * D:(c + 1) * KT * D],
                    scalar=WS, in1=aw[HI][:, c, :, :].rearrange("p k d -> p (k d)"), op0=ALU.mult,
                    op1=ALU.subtract).then_inc(aw_lo, 1)

            attn_w_low(0)
            x_turn_out(0)
            attn_w_low(1)
            dve.wait_ge(small_in, 64)
            dve.tensor_scalar(bc[:, :, :].rearrange("p c k -> p (c k)"), bc_raw[:, :], WS, None, ALU.mult,
                              ).then_inc(setup_v, 1)
            dve.wait_ge(setup_v, 2)
            attn_w_low(2)
            qk_low(0, 0)
            qk_low(1, 0)
            attn_w_low(3)
            dve.tensor_copy(identb[:, :], cst[:, C_ID:C_ID + P])
            dve.tensor_copy(mask_s[:, :, :], cst[:, C_MS:C_MS + P].unsqueeze(1).to_broadcast([P, 4, P]))
            dve.tensor_copy(mask_t[:, :, :], cst[:, C_MT:C_MT + P].unsqueeze(1).to_broadcast([P, 4, P]),
                            ).then_inc(setup_v, 1)
            dve.wait_ge(setup_a, 2)
            dve.scalar_tensor_tensor(out=gw[LO][:, :, :].rearrange("p k e -> p (k e)"), in0=gw_raw[:, :],
                                     scalar=WS, in1=gw[HI][:, :, :].rearrange("p k e -> p (k e)"),
                                     op0=ALU.mult, op1=ALU.subtract)
            dve.tensor_scalar(gsc[:, :], tg[:, 0:1], 1.0 / (WS * WS), None, ALU.mult)
            dve.tensor_copy(tri16[:, :], cst[:, C_TRI:C_TRI + P])
            dve.tensor_copy(one16[:, :], cst[:, C_ONE:C_ONE + P])
            dve.tensor_copy(io16[:, :], cst[:, C_IO:C_IO + P])
            dve.tensor_scalar(bo[:, :], bo[:, :], tg[:, 0:1], None, ALU.mult).then_inc(setup_v, 1)
            dve.wait_ge(setup_v, 4)

            dve.wait_ge(x_in, 16)
            stats(1, st1, mv1, ve1, ln1_a, ln1_b, var1)
            norm(1, xn, mv1, rs1, rstd1, xn_done, xh_done)

            def step(b, q, r):
                if has(b):
                    maxima(b, 0)
                if has(b + 1):
                    x_turn_out(b + 1)
                if has(b - 1):
                    context(b - 1, 1)
                if has(b):
                    maxima(b, 1)
                if has(b - 1):
                    context_low(b - 1, 1)
                if has(b - 2):
                    logit_out(b - 2)
                if has(b + 1):
                    qk_low(0, b + 1)
                    qk_low(1, b + 1)
                if has(b + 2):
                    stats(b + 2, st1, mv1, ve1, ln1_a, ln1_b, var1)
                if has(b - 1):
                    residual(b - 1)
                    dve.wait_ge(x1_done, b)
                    dve.sem_inc(stood_alone, 1)
                    stats(b - 1, st2, mv2, ve2, ln2_a, ln2_b, var2)
                if has(b + 2):
                    norm(b + 2, xn, mv1, rs1, rstd1, xn_done, xh_done)
                if has(b - 1):
                    norm(b - 1, xn2, mv2, rs2, rstd2, xn2_done, x2h_done)
                if has(b):
                    context(b, 0)
                    context_low(b, 0)

            steps(dve, step)

            def je(t):
                return t[:, :].rearrange("p (j e) -> p j e", e=E)

            def ej(t):
                return t[:, :].rearrange("p (e j) -> p e j", e=E)

            def each(t):
                return t[:, :].unsqueeze(2).to_broadcast([P, NT, E])

            dve.wait_ge(logit_done, B)
            dve.wait_ge(wlo_done, WC * B)
            e8 = cst[:, C_E8:C_E8 + NT * E].rearrange("p (j e) -> p j e", e=E)
            dve.tensor_reduce(m1[:, :], je(logits), AX.X, ALU.max).then_inc(route_v, 1)
            dve.wait_ge(route_v, 1)
            dve.tensor_tensor(je(eq), je(logits), each(m1), ALU.is_equal).then_inc(route_v, 1)
            dve.wait_ge(route_v, 2)
            dve.tensor_tensor(je(eq), je(eq), e8, ALU.mult).then_inc(route_v, 1)
            dve.wait_ge(route_v, 3)
            dve.tensor_reduce(e1[:, :], je(eq), AX.X, ALU.min).then_inc(route_v, 1)
            dve.wait_ge(route_v, 4)
            dve.tensor_tensor(je(oh1), e8, each(e1), ALU.is_equal).then_inc(route_v, 1)
            dve.wait_ge(route_v, 5)
            dve.scalar_tensor_tensor(out=lmask[:, :], in0=oh1[:, :], scalar=NEVER, in1=logits[:, :],
                                     op0=ALU.mult, op1=ALU.add).then_inc(route_v, 1)
            dve.wait_ge(route_v, 6)
            dve.tensor_reduce(m2[:, :], je(lmask), AX.X, ALU.max).then_inc(route_v, 1)
            dve.wait_ge(route_v, 7)
            dve.tensor_tensor(pr2[:, :], m2[:, :], m1[:, :], ALU.subtract).then_inc(route_v, 1)
            dve.wait_ge(route_v, 8)
            dve.tensor_tensor(je(eq), je(lmask), each(m2), ALU.is_equal).then_inc(route_v, 1)
            dve.wait_ge(route_v, 9)
            dve.tensor_tensor(je(eq), je(eq), e8, ALU.mult).then_inc(route_v, 1)
            dve.wait_ge(route_v, 10)
            dve.tensor_reduce(e2[:, :], je(eq), AX.X, ALU.min).then_inc(route_v, 1)
            dve.wait_ge(route_v, 11)
            dve.tensor_tensor(je(oh2), e8, each(e2), ALU.is_equal).then_inc(route_v, 1)
            dve.wait_ge(route_v, 12)
            dve.tensor_tensor(both[:, :], oh1[:, :], oh2[:, :], ALU.add).then_inc(route_v, 1)
            dve.wait_ge(route_v, 13)
            dve.wait_ge(route_a, 1)
            dve.tensor_scalar(den[:, :], ex[:, :], 1.0, None, ALU.add).then_inc(route_v, 1)
            dve.wait_ge(route_v, 14)
            dve.reciprocal(pr1[:, :], den[:, :]).then_inc(route_v, 1)
            dve.wait_ge(route_v, 15)
            dve.tensor_scalar(pr1[:, :], pr1[:, :], tg[:, 1:2], None, ALU.mult).then_inc(route_v, 1)
            dve.wait_ge(route_v, 16)
            dve.tensor_tensor(pr2[:, :], ex[:, :], pr1[:, :], ALU.mult).then_inc(route_v, 1)
            dve.wait_ge(route_v, 17)
            dve.tensor_tensor(je(tmp), je(oh1), each(pr1), ALU.mult).then_inc(route_v, 1)
            dve.wait_ge(route_v, 18)
            dve.tensor_tensor(je(comb), je(oh2), each(pr2), ALU.mult).then_inc(route_v, 1)
            dve.wait_ge(route_v, 19)
            dve.tensor_tensor(comb[:, :], comb[:, :], tmp[:, :], ALU.add).then_inc(route_v, 1)
            dve.wait_ge(route_v, 20)
            dve.wait_ge(route_mm, 1)
            dve.tensor_copy(tot[:, :], ps[:, 2, 0:P]).then_inc(route_v, 1)
            dve.wait_ge(route_v, 21)
            dve.tensor_tensor_scan(out=scan[:, :], data0=cst[:, C_SC:C_SC + NT * E], data1=tot[:, :], initial=0.0,
                                   op0=ALU.mult, op1=ALU.add).then_inc(route_v, 1)
            dve.wait_ge(route_v, 22)
            dve.tensor_tensor(tot[:, :], scan[:, :], tot[:, :], ALU.subtract).then_inc(route_v, 1)
            dve.wait_ge(route_v, 23)
            dve.tensor_tensor(tot[:, :], ps[:, 1, 0:P], tot[:, :], ALU.add).then_inc(route_v, 1)
            dve.wait_ge(route_v, 24)
            dve.tensor_scalar(nblk[:, :], ej(scan)[:, :, NT - 1], float(P - 1), None, ALU.add).then_inc(route_v, 1)
            dve.wait_ge(route_v, 25)
            dve.tensor_scalar(nblk[:, :], nblk[:, :], 7, None, ALU.logical_shift_right).then_inc(route_v, 1)
            dve.wait_ge(route_v, 26)
            dve.tensor_copy(nblk_f[:, :], nblk[:, :]).then_inc(route_v, 1)
            dve.wait_ge(route_v, 27)
            dve.tensor_tensor_scan(out=start[:, :], data0=cst[:, C_ONE:C_ONE + E], data1=nblk_f[:, :],
                                   initial=0.0, op0=ALU.mult, op1=ALU.add).then_inc(route_v, 1)
            dve.wait_ge(route_v, 28)
            dve.tensor_tensor(start_s[:, :], start[:, :], nblk_f[:, :], ALU.subtract).then_inc(route_v, 1)
            dve.wait_ge(route_v, 29)
            dve.tensor_scalar(start_s[:, :], start_s[:, :], float(P), None, ALU.mult).then_inc(route_v, 1)
            dve.wait_ge(route_v, 30)
            dve.tensor_tensor(ej(base), ej(tot), start_s[:, :].unsqueeze(2).to_broadcast([P, E, NT]), ALU.add,
                              ).then_inc(route_v, 1)
            dve.wait_ge(route_v, 31)
            for k, oh in enumerate((oh1, oh2)):
                dve.tensor_tensor(je(tmp), je(oh), base[:, :].rearrange("p (e j) -> p j e", e=E), ALU.mult,
                                  ).then_inc(route_v, 1)
                dve.wait_ge(route_v, 32 + 2 * k)
                dve.tensor_reduce(pos[:, k * NT:(k + 1) * NT], je(tmp), AX.X, ALU.add).then_inc(route_v, 1)
                dve.wait_ge(route_v, 33 + 2 * k)
            dve.tensor_copy(pos_i[:, :], pos[:, :]).then_inc(route_v, 1)
            dve.wait_ge(route_v, 36)
            dve.tensor_scalar(hi_i[:, :], pos_i[:, :], 7, None, ALU.logical_shift_right).then_inc(route_v, 1)
            dve.wait_ge(route_v, 37)
            dve.tensor_scalar(lo_i[:, :], pos_i[:, :], P - 1, None, ALU.bitwise_and).then_inc(route_v, 1)
            dve.wait_ge(route_v, 38)
            dve.tensor_copy(hi_f[:, :], hi_i[:, :]).then_inc(route_v, 1)
            dve.wait_ge(route_v, 39)
            dve.tensor_copy(lo_f[:, :], lo_i[:, :]).then_inc(route_v, 1)
            dve.wait_ge(route_v, 40)
            dve.wait_ge(base_stored, 16 * B)
            dve.tensor_tensor(hot_lo, io16[:, :].unsqueeze(1).to_broadcast([P, TOPK * NT, P]),
                              lo_f[:, :].unsqueeze(2).to_broadcast([P, TOPK * NT, P]), ALU.is_equal)
            dve.tensor_tensor(hot_blk, cst[:, C_BLK:C_BLK + BLOCKS].unsqueeze(1).to_broadcast([P, TOPK * NT, BLOCKS]),
                              hi_f[:, :].unsqueeze(2).to_broadcast([P, TOPK * NT, BLOCKS]), ALU.is_equal,
                              ).then_inc(route_v, 1)
            dve.wait_ge(route_v, 41)
            for k in range(TOPK):
                last = dve.tensor_tensor(hot_blk[:, k * NT:(k + 1) * NT, :], hot_blk[:, k * NT:(k + 1) * NT, :],
                                         cst[:, C_TOK:C_TOK + NT].unsqueeze(2).to_broadcast([P, NT, BLOCKS]), ALU.mult)
            last.then_inc(route_v, 1)
            dve.tensor_tensor(cmp[:, :].rearrange("p (c e) -> p c e", e=E - 1),
                              cst[0:1, C_BLK:C_BLK + BLOCKS].unsqueeze(2).to_broadcast([1, BLOCKS, E - 1]),
                              start[0:1, 0:E - 1].unsqueeze(1).to_broadcast([1, BLOCKS, E - 1]), ALU.is_ge,
                              ).then_inc(route_v, 1)
            dve.wait_ge(route_v, 43)
            dve.tensor_reduce(eidf[:, :], cmp[:, :].rearrange("p (c e) -> p c e", e=E - 1), AX.X, ALU.add,
                              ).then_inc(route_v, 1)
            dve.wait_ge(route_v, 44)
            dve.tensor_copy(eid[:, :], eidf[:, :]).then_inc(idx_done, 1)
            dve.tensor_scalar(wat[:, :], eidf[:, :], float(EW), None, ALU.mult).then_inc(idx_done, 1)
            dve.wait_ge(table_mm, 1)
            dve.tensor_scalar(idx_f[:, :], ps[:, 3, 0:BLOCKS], float(N), None, ALU.add).then_inc(route_v, 1)
            dve.wait_ge(route_v, 45)
            dve.tensor_copy(idx_s[:, :], idx_f[:, :]).then_inc(idx_done, 1)
            dve.tensor_scalar(idx_g[:, :], idx_f[:, :], float(N - 1), None, ALU.min).then_inc(idx_done, 1)
            dve.wait_ge(idx_done, 4)

            def first_out(i, q, q4, e):
                dve.wait_ge(gv_mm, i + 1)
                if not isinstance(i, int) or i > 3:
                    dve.wait_ge(yo_done, i - 3 + CREDIT)
                dve.tensor_copy(wslot[:, q4:q4 + 1], xg[q4].bitcast(F32)[:, bass.ds(e + D, 1)])
                if begun(i):
                    dve.wait_ge(h_done, i)
                for m, done in enumerate((g_done, v_half)):
                    dve.scalar_tensor_tensor(out=gv[:, m * F:(m + 1) * F], in0=gvp[q][:, m, :], scalar=1.0 / WS,
                                             in1=region_a[:, bass.ds(e * EB + m * F, F)], op0=ALU.mult,
                                             op1=ALU.add).then_inc(done, 1)

            def h_out(i):
                dve.wait_ge(silu_done, i + 1)
                dve.wait_ge(v_half, i + 1)
                if begun(i):
                    dve.wait_ge(hT_mm, i)
                dve.tensor_tensor(hh, gv[:, 0:F], gv[:, F:2 * F], ALU.mult).then_inc(h_done, 1)

            def h_low(i, q):
                dve.wait_ge(hT_hi, i + 1)
                dve.tensor_tensor(hT[q][LO], hTp, hT[q][HI], ALU.subtract).then_inc(hT_done, 1)

            def y_out(i, q, e):
                dve.wait_ge(y_mm, i + 1)
                dve.wait_ge(yo_done, i - 1 + CREDIT)
                dve.scalar_tensor_tensor(out=yb[q], in0=yp[q][:, 0:D], scalar=1.0 / WS,
                                         in1=region_a[:, bass.ds(e * EB + 2 * F, D)], op0=ALU.mult,
                                         op1=ALU.add).then_inc(y_done, 1)

            dve.wait_ge(bias_in, 16)
            e = expert_values(mybir.EngineType.DVE, eid, 0, 2, 1)
            first_out(0, 0, 0, e[0])
            h_out(0)
            first_out(1, 1, 1, e[1])
            h_low(0, 0)
            h_out(1)

            def blk(i, q4, here, before):
                first_out(i, q4 % 2, q4, here)
                h_low(i - 1, 1 - q4 % 2)
                h_out(i)
                y_out(i - 2, q4 % 2, before)

            with dve.Fori(0, (BLOCKS - 3) // 4) as j:
                e = expert_values(mybir.EngineType.DVE, eid, j * 4, 6, 1)
                for u in range(4):
                    blk(j * 4 + (u + 2), (u + 2) % 4, e[u + 2], e[u])
            e = expert_values(mybir.EngineType.DVE, eid, BLOCKS - 3, 3, 1)
            blk(BLOCKS - 1, (BLOCKS - 1) % 4, e[2], e[0])
            h_low(BLOCKS - 1, (BLOCKS - 1) % 2)
            y_out(BLOCKS - 2, (BLOCKS - 2) % 2, e[1])
            y_out(BLOCKS - 1, (BLOCKS - 1) % 2, e[2])


SETUP_PE, SETUP_BIAS, SETUP_MASKS, SETUP_BO = 1, 2, 3, 4
R_DIFF, R_BOTH, R_COMB, R_HOT = 8, 13, 20, 42


def kernel(**inputs):
    import concourse.bacc as _bacc
    from concourse.bass_utils import run_bass_kernel_spmd as _run

    a = {k: np.asarray(v) for k, v in inputs.items()}

    def tiles(w):
        o, i = w.shape[-2:]
        return np.moveaxis(np.swapaxes(w, -1, -2).reshape(*w.shape[:-2], i // P, P, o), -3, -2)

    def cols(v):
        return v.reshape(KT, P).T

    order = np.arange(D).reshape(H // HG, HG, HD).transpose(1, 2, 0).reshape(-1)

    x = a["x"]
    y = np.swapaxes(a["ctx_1024"], 1, 2).reshape(B, KT, P, T).transpose(0, 2, 1, 3).reshape(B, P, KT * T)
    g = np.concatenate([a["g_xattn"], a["g_ffn"]])
    wattn = np.stack([tiles(a["L0_xattn_W" + n][order] if n in "qk" else a["L0_xattn_W" + n]) for n in "qkvo"], 1).reshape(P, 4 * KT * D)
    bcol = np.stack([cols(a["L0_xattn_b" + n][order] if n in "qk" else a["L0_xattn_b" + n]) for n in "qkv"], 1).reshape(P, 3 * KT)
    brow = a["L0_xattn_bo"][None, :]
    wgate = tiles(a["L0_ffn_Wg"]).reshape(P, KT * E)
    wffn = np.stack([tiles(a["L0_ffn_W" + n]).reshape(E, P, WE) for n in "123"], 1).reshape(E * WC, P, WE)
    bffn = np.concatenate([a["L0_ffn_b1"], a["L0_ffn_b2"], a["L0_ffn_b3"]], 1).reshape(1, E * EB)
    arrays = {"in_" + k: np.ascontiguousarray(v) for k, v in dict(
        x=x, y=y, g=g, wattn=wattn, bcol=bcol, brow=brow, wgate=wgate, wffn=wffn, bffn=bffn,
        consts=constants()).items()}

    nc = _bacc.Bacc("TRN2", target_bir_lowering=False, num_devices=1)
    args = [nc.dram_tensor(k, v.shape, mybir.dt.from_np(v.dtype), kind="ExternalInput").ap()
            for k, v in arrays.items()]
    args.append(nc.dram_tensor("out", (B, T, D), F32, kind="ExternalOutput").ap())
    flamingo_kernel(nc, *args)
    r = _run(nc, [arrays], core_ids=[0])
    return r.results[0]["out"]
```

```python
from contextlib import ExitStack

import numpy as np

import concourse.bass as bass
from concourse import mybir

ALU = mybir.AluOpType
ACT = mybir.ActivationFunctionType
AX = mybir.AxisListType
F32 = mybir.dt.float32
F16 = mybir.dt.float16
BF16 = mybir.dt.bfloat16
I32 = mybir.dt.int32

P = 128
B, T, D = 8, 256, 256
H, HD = 8, 32
E, F, TOPK = 8, 512, 2
TT = T // P
NT = B * TT
N = B * T
KT = D // P
FT = F // P
HG = H // 4
EPS = 1e-5
WS = 16.0
MASKED = -1.0e30
NEVER = -3.0e38
BLOCKS = (TOPK * N + E * (P - 1)) // P
WC = 3
WE = KT * F
EW = WC * WE
EB = 2 * F + D
ROW = D + E
HI, LO = 0, 1

C_ID, C_MS, C_MT, C_TRI, C_ONE, C_IO, C_E8, C_SC, C_TOK, C_BLK = np.cumsum(
    [0, P, P, P, P, P, P, NT * E, NT * E, NT]).tolist()
C_END = C_BLK + BLOCKS + 1


def constants():
    c = np.zeros((P, C_END), np.float32)
    i = np.arange(P)
    c[:, C_ID:C_ID + P] = np.eye(P)
    c[:, C_MS:C_MS + P] = np.where(i[None, :] > i[:, None], MASKED, 0.0)
    c[:, C_MT:C_MT + P] = np.where(i[:, None] > i[None, :], MASKED, 0.0)
    c[:, C_TRI:C_TRI + P] = i[:, None] < i[None, :]
    c[:, C_ONE:C_ONE + P] = 1.0
    c[:, C_IO:C_IO + P] = i[None, :]
    c[:, C_E8:C_E8 + NT * E] = np.tile(np.arange(E) - E, NT)[None, :]
    c[:, C_SC:C_SC + NT * E] = np.tile((np.arange(NT) > 0) * 1.0, E)[None, :]
    c[:, C_TOK:C_TOK + NT] = np.arange(NT)[None, :] * P + i[:, None] - N
    c[:, C_BLK:C_BLK + BLOCKS] = np.arange(BLOCKS)[None, :]
    return c


def flamingo_kernel(nc, x, y, g, wattn, bcol, brow, wgate, wffn, bffn, consts, out):
    ctx = ExitStack()
    with ctx:
        def sb(name, shape, dt):
            return ctx.enter_context(nc.sbuf_tensor(name, shape, dt))

        def sem(name):
            return ctx.enter_context(nc.semaphore(name))

        x_rows = x.rearrange("b (t p) d -> p (b t) d", p=P)
        out_rows = out.rearrange("b (t p) d -> p (b t) d", p=P)
        out_flat = out.rearrange("b t d -> (b t) d")
        rows = nc.dram_tensor("token_rows", (N, ROW), I32, kind="Internal").ap()
        rows_v = rows.rearrange("(j p) c -> p j c", p=P)

        w_hl = [sb("ffn_w_hi", [P, E * EW], F16), sb("ffn_w_lo", [P, E * EW], F16)]
        region_a = sb("region_a", [P, E * EB], F32)
        region_x = sb("region_x", [P, NT * D], F32)
        region_w = sb("region_w", [P, WC * WE], F32)
        cst = sb("constants", [P, C_END], F32)

        at = [0]

        def carve(region, n, dt=F32):
            words = n if dt in (F32, I32) else n // 2
            view = region[:, at[0]:at[0] + words]
            at[0] += words
            assert at[0] <= region.shape[1]
            return view if dt == F32 else view.bitcast(dt)

        q_stack = [carve(region_a, H * T, F16).rearrange("p (h t) -> p h t", h=H) for _ in range(2)]
        k_stack = [carve(region_a, H * T, F16).rearrange("p (h t) -> p h t", h=H) for _ in range(2)]
        probs = [carve(region_a, 3 * 4 * P).rearrange("p (s h t) -> p s h t", s=3, h=4) for _ in range(HG)]
        y_raw = [carve(region_a, KT * T) for _ in range(2)]
        v_sb = [carve(region_a, TT * D).rearrange("p (t d) -> p t d", t=TT) for _ in range(2)]
        xh = carve(region_a, TT * 2 * D, F16).rearrange("p (t s d) -> p t s d", t=TT, s=2)
        xT = carve(region_a, 2 * KT * T, F16).rearrange("p (s k t) -> p s k t", s=2, k=KT)
        yT = sb("yT", [P, 2, KT * T], F16)
        qk_st = [[sb(f"{n}_{s}", [P, HG, T], F16) for s in ("hi", "lo")] for n in "qk"]
        xn = sb("xn", [P, TT, D], F32)
        xn2 = sb("xn2", [P, TT, D], F32)
        x2h = sb("x2h", [P, TT, 2, D], F16)
        x2T = sb("x2T", [P, 2, KT, T], F16)
        rden = sb("rden", [P, T], F32)
        ctx32 = [sb(f"ctx32_{g}", [P, T], F32) for g in range(HG)]
        ctx_hl = [sb("ctx_hi", [P, HG, T], F16), sb("ctx_lo", [P, HG, T], F16)]
        aw = [sb("attn_w_hi", [P, 4, KT, D], F16), sb("attn_w_lo", [P, 4, KT, D], F16)]
        gw_raw = sb("gate_w_raw", [P, KT * E], F32)
        gw = [sb("gate_w_hi", [P, KT, E], F16), sb("gate_w_lo", [P, KT, E], F16)]
        bc_raw = sb("bias_cols_raw", [P, 3 * KT], F32)
        bc = sb("bias_cols", [P, 3, KT], F32)
        bo = sb("bo_rows", [P, D], F32)
        g_raw = sb("g_raw", [P, 2], F32)
        tg = sb("tanh_g", [P, 2], F32)
        gsc = sb("attn_scale", [P, 1], F32)
        ident = sb("ident", [P, P], F16)
        identb = sb("identb", [P, P], BF16)
        mask_s = sb("mask_s", [P, 4, P], BF16)
        mask_t = sb("mask_t", [P, 4, P], BF16)
        onesf = sb("onesf", [P, HD], F32)
        ve1 = sb("ve1", [P, TT], F32)
        ve2 = sb("ve2", [P, TT], F32)
        half = sb("minus_half", [P, TT], F32)
        st1 = sb("st1", [P, TT, 6], F32)
        mv1 = sb("mv1", [P, TT, 2], F32)
        rs1 = sb("rs1", [P, TT], F32)
        st2 = sb("st2", [P, TT, 6], F32)
        mv2 = sb("mv2", [P, TT, 2], F32)
        rs2 = sb("rs2", [P, TT], F32)
        mx = sb("row_max", [P, H, TT], F32)
        mneg = [sb(f"minus_max_{g}", [P, 4 * TT], F16) for g in range(HG)]
        mrow = [sb(f"shift_rows_{g}", [4 * TT, P], F16) for g in range(HG)]
        logits = sb("logits", [P, NT * E], F32)

        at[0] = 0
        hot_lo = carve(region_x, TOPK * NT * P, F16).rearrange("p (s c) -> p s c", c=P)
        hot_blk = carve(region_x, TOPK * NT * BLOCKS, F16).rearrange("p (s c) -> p s c", c=BLOCKS)
        at[0] = 0
        xg = [carve(region_x, ROW, I32) for _ in range(4)]
        xgT = [carve(region_x, 4 * P, F16) for _ in range(2)]
        at[0] = 0
        gv = carve(region_w, 2 * F)
        hh = carve(region_w, F)
        hT = [[carve(region_w, F, F16) for _ in range(2)] for _ in range(2)]
        yb = [carve(region_w, D) for _ in range(2)]
        yo = [sb(f"y_out_{i}", [P, D], F32) for i in range(2)]

        def rt(name, n=NT * E, dt=F32):
            return sb("rt_" + name, [P, n], dt)

        m1, m2, e1, e2 = (rt(n, NT) for n in ("m1", "m2", "e1", "e2"))
        at[0] = 0
        eq, oh1, oh2, lmask, base, comb, tmp, tot, scan = (carve(region_w, NT * E) for _ in range(9))
        both = rt("both", NT * E, F16)
        tri16 = sb("tri16", [P, P], F16)
        one16 = sb("one16", [P, P], F16)
        io16 = sb("io16", [P, P], F16)
        ex, den, diff, pr1, pr2 = (rt(n, NT) for n in ("ex", "den", "diff", "pr1", "pr2"))
        nblk, nblk_f, start, start_s = rt("nblk", E, I32), rt("nblkf", E), rt("start", E), rt("starts", E)
        pos = rt("pos", TOPK * NT)
        pos_i, hi_i, lo_i = (rt(n, TOPK * NT, I32) for n in ("pos_i", "hi_i", "lo_i"))
        hi_f, lo_f = rt("hi_f", TOPK * NT), rt("lo_f", TOPK * NT)
        cmp = sb("rt_cmp", [1, (E - 1) * BLOCKS], F32)
        eidf = sb("rt_eidf", [1, BLOCKS], F32)
        eid = sb("block_expert", [1, BLOCKS], I32)
        wat = sb("block_weights", [1, BLOCKS], I32)
        idx_s = sb("scatter_rows", [P, BLOCKS], I32)
        idx_g = sb("gather_rows", [P, BLOCKS], I32)
        row_in = [sb(f"row_in_{i}", [P, 1], I32) for i in range(4)]
        row_out = [sb(f"row_out_{i}", [P, 1], I32) for i in range(2)]
        idx_f = rt("idx_f", BLOCKS)
        wslot = sb("slot_gate", [P, 4], F32)

        ps = ctx.enter_context(nc.psum_tensor("ps", [P, 8, 512], F32))
        turn = ps[:, 0, :]
        turn16 = turn.bitcast(F16)
        pa, pb = ps[:, 1, :], ps[:, 2, :]
        score = ps[:, 3:6, :].rearrange("p s (h t) -> p s h t", h=4)
        shift16 = [bank.bitcast(F16)[0:4 * TT, 0:P] for bank in (pb, turn)]
        uden_bank = ps[:, 6, :]
        rout = ps[:, 7, :]
        rout16 = rout.bitcast(F16)
        gvp = [ps[:, 0:2, :], ps[:, 2:4, :]]
        hTp = ps[:, 4, :]
        xTp = ps[:, 5, :].bitcast(F16)
        yp = [ps[:, 6, :], ps[:, 7, :]]

        (stood_alone, consts_in, small_in, x0_in, x_in, base_stored, rows_stored,
         gates_stored, bias_in, setup_v, setup_a, setup_p, aw_hi, aw_lo, ln1_a, ln1_b, var1, rstd1,
         xn_done, xhi_done, xh_done, xT_done, ln2_a, ln2_b, var2, rstd2, xn2_done, x2hi_done, x2h_done,
         x2T_done, yhi_done, yT_done, whi_done, wlo_done, xb_done, q_mm, k_mm, v_mm, s_mm, t_mm,
         o_mm, lt_mm, mt_mm, rt_mm, r_mm, pv_mm, q_hi, q_st, k_hi, k_st, v_done, max_done, mneg_done,
         mrow_done, exp_done, rden_done, umul_done, ctxhi_done, ctx_done, x1_done, logit_done, row_in_done,
         row_out_done, route_v, route_a, route_mm, table_mm, idx_done, comb_done, hot_done, xgT_mm, xgT_done, gv_mm, g_done,
         v_half, silu_done, h_done, hT_mm, hT_hi, hT_done, y_mm, y_done, yo_done, added) = (
            sem(name) for name in (
                "stood_alone consts_in small_in x0_in x_in base_stored rows_stored "
                "gates_stored bias_in setup_v setup_a setup_p aw_hi aw_lo ln1_a ln1_b var1 rstd1 "
                "xn_done xhi_done xh_done xT_done ln2_a ln2_b var2 rstd2 xn2_done x2hi_done x2h_done "
                "x2T_done yhi_done yT_done whi_done wlo_done xb_done q_mm k_mm v_mm s_mm t_mm "
                "o_mm lt_mm mt_mm rt_mm r_mm pv_mm q_hi q_st k_hi k_st v_done max_done mneg_done "
                "mrow_done exp_done rden_done umul_done ctxhi_done ctx_done x1_done logit_done row_in_done "
                "row_out_done route_v route_a route_mm table_mm idx_done comb_done hot_done xgT_mm xgT_done gv_mm g_done "
                "v_half silu_done h_done hT_mm hT_hi hT_done y_mm y_done yo_done added "
            ).split())
        attnw_in, stack_in, y_in, w_in, xg_in, shift_in = ([sem(f"{name}_{i}") for i in range(n)] for name, n in (
            ("attnw_in", 2), ("stack_in", 2), ("y_in", 2), ("w_in", WC), ("xg_in", 4), ("shift_in", HG)))

        def begun(count):
            return not isinstance(count, int) or count > 0

        block = ctx.enter_context(nc.Block())

        def steps(eng, step):
            step(0, 0, 0)
            step(1, 1, 0)
            with eng.Fori(0, (B - 4) // 2) as i:
                step(i * 2 + 2, 0, i + 1)
                step(i * 2 + 3, 1, i + 1)
            for b in range(B - 2, B + 2):
                step(b, b % 2, b // 2)

        def final(b):
            return isinstance(b, int) and b == B - 1

        def uden(b, g):
            return pa if final(b) and g == 1 else uden_bank

        def attn_out(b):
            return pb if final(b) else rout

        def has(n):
            return not isinstance(n, int) or 0 <= n < B

        def expert_values(engine, table, first, n, step):
            return nc.values_load_multi_w_load_instructions(
                table[0:1, bass.ds(first, n)], engines=[engine], min_val=0, max_val=(E - 1) * step,
                skip_runtime_bounds_check_because="an expert is a sum of E - 1 comparisons")[1]

        STACK = 16 * 6
        CREDIT = 2
        PAIRS = ((HI, HI), (HI, LO), (LO, HI))

        @block.sync
        def _(sp):
            def load_attn_w(half):
                cols = slice(half * 2 * KT * D, (half + 1) * 2 * KT * D)
                sp.dma_start(region_w[:, cols], wattn[:, cols]).then_inc(attnw_in[half], 16)

            sp.dma_start(region_x[:, 0:TT * D].rearrange("p (j d) -> p j d", d=D),
                         x_rows[:, 0:TT, :]).then_inc(x0_in, 16)
            load_attn_w(0)
            sp.dma_start(cst[:, :], consts).then_inc(consts_in, 16)
            sp.dma_start(bc_raw[:, :], bcol).then_inc(small_in, 16)
            sp.dma_start(y_raw[0], y[0]).then_inc(y_in[0], 16)
            load_attn_w(1)
            for dst, src in ((gw_raw[:, :], wgate),
                             (bo[:, :], brow.rearrange("a d -> (a d)").partition_broadcast(P)),
                             (g_raw[:, :], g.partition_broadcast(P))):
                sp.dma_start(dst, src).then_inc(small_in, 16)
            sp.dma_start(y_raw[1], y[1]).then_inc(y_in[1], 16)
            sp.dma_start(region_x[:, TT * D:].rearrange("p (j d) -> p j d", d=D),
                         x_rows[:, TT:, :]).then_inc(x_in, 16)

            def load_chunk(c, buf):
                sp.dma_start(region_w[:, buf * WE:(buf + 1) * WE],
                             wffn[bass.ds(c, 1)].rearrange("a p n -> (a p) n")).then_inc(w_in[buf], 16)

            def stack(which, dst, b, q):
                high_done, low_done, places = ((q_hi, q_st, (0, 2, 1)), (k_hi, k_st, (0, 1, 2)))[which]
                for place, part in zip(places, (HI, HI, LO)):
                    sp.wait_ge(low_done if part == LO else high_done, b + 1)
                    sp.dma_start(dst[HD * place:HD * (place + 1), :, :].rearrange("p (a m) t -> p a (m t)", m=HG),
                                 qk_st[which][part][:, :, :].rearrange("p m t -> p (m t)"),
                                 ).then_inc(stack_in[q], 16)

            stack(0, q_stack[0], 0, 0)
            stack(1, k_stack[0], 0, 0)
            sp.wait_ge(aw_lo, 4)
            for buf in range(WC):
                load_chunk(buf, buf)

            def shift(b, g, q):
                sp.wait_ge(mrow_done, b * HG + g + 1)
                sp.dma_start(q_stack[q][3 * HD:3 * HD + 1, 4 * g:4 * g + 4, :].rearrange("p h (t c) -> p (h t) c", t=TT),
                             mrow[g][:, :]).then_inc(shift_in[g], 16)

            def results(b):
                sp.wait_ge(x1_done, b + 1)
                sp.dma_start(out_rows[:, bass.ds(b * TT, TT), :],
                             region_x[:, bass.ds(b * TT * D, TT * D)].rearrange("p (j d) -> p j d", d=D),
                             ).then_inc(base_stored, 16)

            def row_store(b):
                sp.wait_ge(x2h_done, b + 1)
                sp.dma_start(rows_v[:, bass.ds(b * TT, TT), 0:D],
                             x2h[:, :, :, :].rearrange("p j s d -> p j (s d)").bitcast(I32)).then_inc(rows_stored, 16)

            def step(b, q, r):
                if has(b):
                    shift(b, 0, q)
                if has(b - 2):
                    row_store(b - 2)
                if has(b - 1) and has(b):
                    sp.wait_ge(wlo_done, b * WC)
                    load_chunk(b * WC + 2, 2)
                if has(b + 2):
                    sp.wait_ge(yT_done, b + 1)
                    sp.dma_start(y_raw[q], y[bass.ds(b + 2, 1)].rearrange("a p n -> (a p) n"),
                                 ).then_inc(y_in[q], 16)
                if has(b):
                    shift(b, 1, q)
                if has(b + 1):
                    if begun(b * HG):
                        sp.wait_ge(t_mm, b * HG)
                    sp.sem_inc(stood_alone, 1)
                    stack(0, q_stack[1 - q], b + 1, 1 - q)
                    stack(1, k_stack[1 - q], b + 1, 1 - q)
                    sp.wait_ge(wlo_done, b * WC + 1)
                    load_chunk(b * WC + 3, 0)
                    sp.wait_ge(wlo_done, b * WC + 2)
                    load_chunk(b * WC + 4, 1)
                if has(b - 1):
                    results(b - 1)

            steps(sp, step)
            sp.wait_ge(pv_mm, B * HG)
            sp.wait_ge(exp_done, B * HG)
            sp.dma_start(region_a[:, :], bffn.rearrange("a d -> (a d)").partition_broadcast(P),
                         ).then_inc(bias_in, 16)
            sp.wait_ge(comb_done, 3)
            sp.dma_start(rows_v[:, :, D:], comb[:, :].bitcast(I32).rearrange("p (j c) -> p j c", j=NT),
                         ).then_inc(gates_stored, 16)
            sp.wait_ge(base_stored, 16 * B)
            sp.wait_ge(rows_stored, 16 * B)
            sp.wait_ge(gates_stored, 16)

        @block.scalar
        def _(act):
            act.sem_inc(yo_done, CREDIT)
            def attn_w_high(c):
                act.wait_ge(attnw_in[c // 2], 16)
                act.activation(aw[HI][:, c, :, :].rearrange("p k d -> p (k d)"),
                               region_w[:, c * KT * D:(c + 1) * KT * D], ACT.Copy, scale=WS).then_inc(aw_hi, 1)

            def split_chunk(b, buf):
                act.wait_ge(w_in[buf], (b + 1) * 16)
                raw = region_w[:, buf * WE:(buf + 1) * WE]
                act.activation(w_hl[HI][:, bass.ds((b * WC + buf) * WE, WE)], raw, ACT.Copy, scale=WS)
                act.activation(raw, raw, ACT.Copy, scale=WS).then_inc(whi_done, 1)

            def x_high(n):
                act.wait_ge(xn_done, n + 1)
                if begun(n):
                    act.wait_ge(lt_mm, n)
                act.activation(xh[:, :, HI, :], xn[:, :, :], ACT.Copy).then_inc(xhi_done, 1)

            def y_high(n, q, r):
                act.wait_ge(y_in[q], (r + 1) * 16)
                if begun(n):
                    act.wait_ge(v_mm, n)
                act.activation(yT[:, HI, :], y_raw[q], ACT.Copy).then_inc(yhi_done, 1)

            def qk_high(which, n):
                mm, done, src = ((q_mm, q_hi, pa), (k_mm, k_hi, pb))[which]
                act.wait_ge(mm, n + 1)
                if begun((n - 1) * HG + 1):
                    act.wait_ge(s_mm, (n - 1) * HG + 1)
                for m in range(KT):
                    last = act.activation(qk_st[which][HI][:, m, :], src[:, m * T:(m + 1) * T], ACT.Identity,
                                          bias=bc[:, which, m:m + 1])
                last.then_inc(done, 1)

            def v_out(n, q):
                act.wait_ge(v_mm, n + 1)
                if begun((n - 1) * HG):
                    act.wait_ge(pv_mm, (n - 1) * HG)
                act.activation(v_sb[q].rearrange("p t d -> p (t d)"), pa, ACT.Copy).then_inc(v_done, 1)

            def expo(b, g):
                act.wait_ge(t_mm, b * HG + g + 1)
                if begun(b * HG - HG + g + 1):
                    act.wait_ge(pv_mm, b * HG - HG + g + 1)
                act.activation(probs[g].rearrange("p s h t -> p (s h t)"),
                               score.rearrange("p s h t -> p (s h t)"), ACT.Exp,
                               scale=float(HD) ** -0.5 / (WS * WS)).then_inc(exp_done, 1)

            def ctx_high(b, g):
                act.wait_ge(umul_done, b * HG + g + 1)
                if begun(b):
                    act.wait_ge(o_mm, b)
                act.activation(ctx_hl[HI][:, g, :], ctx32[g][:, :], ACT.Identity,
                               bias=bc[:, 2, g:g + 1]).then_inc(ctxhi_done, 1)

            def x2_high(b):
                act.wait_ge(xn2_done, b + 1)
                if begun(b * 16):
                    act.wait_ge(rows_stored, b * 16)
                if begun(b):
                    act.wait_ge(rt_mm, b)
                act.activation(x2h[:, :, HI, :], xn2[:, :, :], ACT.Copy).then_inc(x2hi_done, 1)

            def x2_turn_out(b):
                act.wait_ge(rt_mm, b + 1)
                if begun(b):
                    act.wait_ge(r_mm, b)
                act.activation(x2T[:, :, :, :].rearrange("p s k t -> p (s k t)"), rout16,
                               ACT.Copy).then_inc(x2T_done, 1)

            def shift_out(b, g):
                act.wait_ge(mt_mm, b * HG + g + 1)
                if begun(b):
                    act.wait_ge(shift_in[g], b * 16)
                act.activation(mrow[g][:, :], shift16[g], ACT.Copy).then_inc(mrow_done, 1)

            attn_w_high(0)
            x_high(0)
            attn_w_high(1)
            y_high(0, 0, 0)
            attn_w_high(2)
            attn_w_high(3)
            act.wait_ge(small_in, 64)
            act.activation(gw[HI][:, :, :].rearrange("p k e -> p (k e)"), gw_raw[:, :], ACT.Copy,
                           scale=WS).then_inc(setup_a, 1)
            act.activation(tg[:, :], g_raw[:, :], ACT.Tanh).then_inc(setup_a, 1)
            act.wait_ge(setup_v, SETUP_BIAS)
            qk_high(0, 0)
            qk_high(1, 0)
            x_high(1)

            def step(b, q, r):
                if has(b):
                    v_out(b, q)
                if has(b + 1):
                    y_high(b + 1, 1 - q, r + q)
                if has(b):
                    shift_out(b, 0)
                    split_chunk(b, 0)
                if has(b - 1):
                    ctx_high(b - 1, 0)
                if final(b - 1):
                    x2_high(b - 2)
                    ctx_high(b - 1, 1)
                if has(b - 2):
                    x2_turn_out(b - 2)
                if has(b):
                    if not final(b):
                        split_chunk(b, 1)
                    shift_out(b, 1)
                if final(b):
                    expo(b, 0)
                if has(b + 1):
                    qk_high(0, b + 1)
                if has(b - 1) and not final(b - 1):
                    ctx_high(b - 1, 1)
                if has(b + 1):
                    qk_high(1, b + 1)
                if has(b):
                    if not final(b):
                        expo(b, 0)
                    expo(b, 1)
                    if final(b):
                        split_chunk(b, 1)
                    split_chunk(b, 2)
                if has(b + 2):
                    x_high(b + 2)
                if has(b - 1) and not final(b):
                    x2_high(b - 1)

            steps(act, step)
            for part, tiles in enumerate((slice(0, NT - TT), slice(NT - TT, NT))):
                act.wait_ge(route_v, part * R_TOP2 + R_DIFF)
                act.activation(ex[:, tiles], diff[:, tiles], ACT.Exp).then_inc(route_a, 1)

            def silu(i):
                act.wait_ge(g_done, i + 1)
                act.activation(gv[:, 0:F], gv[:, 0:F], ACT.Silu).then_inc(silu_done, 1)

            def h_high(i, q):
                act.wait_ge(hT_mm, i + 1)
                if begun(i - 1):
                    act.wait_ge(y_mm, i - 1)
                act.activation(hT[q][HI], hTp, ACT.Copy).then_inc(hT_hi, 1)

            def turn_out(i, q):
                act.wait_ge(xgT_mm, i + 1)
                if begun(i - 1):
                    act.wait_ge(gv_mm, i - 1)
                act.activation(xgT[q], xTp[:, 0:4 * P], ACT.Copy).then_inc(xgT_done, 1)

            def gate(i, q, q4):
                act.wait_ge(y_done, i + 1 + CREDIT)
                if begun((i - 1) * 16):
                    act.wait_ge(added, (i - 1) * 16)
                act.activation(yo[q][:, :], yb[q], ACT.Copy, scale=wslot[:, q4:q4 + 1]).then_inc(yo_done, 1)

            turn_out(0, 0)
            turn_out(1, 1)
            silu(0)
            h_high(0, 0)
            turn_out(2, 0)
            silu(1)

            def blk(i, q4, last):
                h_high(i - 1, 1 - q4 % 2)
                if not last:
                    turn_out(i + 1, 1 - q4 % 2)
                silu(i)
                gate(i - 2, q4 % 2, (q4 + 2) % 4)

            for i in range(2, 6):
                blk(i, i % 4, False)
            with act.Fori(0, (BLOCKS - 7) // 4) as j:
                for u in range(4):
                    blk(j * 4 + (u + 6), (u + 2) % 4, False)
            blk(BLOCKS - 1, (BLOCKS - 1) % 4, True)
            h_high(BLOCKS - 1, (BLOCKS - 1) % 2)
            gate(BLOCKS - 2, (BLOCKS - 2) % 2, (BLOCKS - 2) % 4)
            gate(BLOCKS - 1, (BLOCKS - 1) % 2, (BLOCKS - 1) % 4)

        @block.gpsimd
        def _(pool):
            pool.memset(half[:, :], -0.5).then_inc(setup_p, 1)
            pool.memset(onesf[:, :], 1.0).then_inc(setup_p, 1)
            for q in range(2):
                pool.wait_ge(setup_p, 2 + q)
                pool.memset(k_stack[q][96:97, :, :], WS * WS).then_inc(setup_p, 1)

            def rstd(n, var, ve, rs, done):
                pool.wait_ge(var, n + 1)
                pool.tensor_tensor(rs[:, :], ve[:, :], half[:, :], ALU.pow).then_inc(done, 1)

            def y_low(n, q):
                pool.wait_ge(yhi_done, n + 1)
                pool.tensor_tensor(yT[:, LO, :], y_raw[q], yT[:, HI, :], ALU.subtract).then_inc(yT_done, 1)

            def w_low(b, buf):
                pool.wait_ge(whi_done, b * WC + buf + 1)
                c = (b * WC + buf) * WE
                pool.tensor_tensor(w_hl[LO][:, bass.ds(c, WE)], region_w[:, buf * WE:(buf + 1) * WE],
                                   w_hl[HI][:, bass.ds(c, WE)], ALU.subtract).then_inc(wlo_done, 1)

            def add_bo(b):
                pool.wait_ge(xn_done, b + 1)
                v = region_x[:, bass.ds(b * TT * D, TT * D)].rearrange("p (j d) -> p j d", d=D)
                pool.tensor_tensor(v, v, bo[:, :].unsqueeze(1).to_broadcast([P, TT, D]), ALU.add).then_inc(xb_done, 1)

            def x_low(n):
                pool.wait_ge(xhi_done, n + 1)
                pool.tensor_tensor(xh[:, :, LO, :], xn[:, :, :], xh[:, :, HI, :], ALU.subtract,
                                   ).then_inc(xh_done, 1)

            def x2_low(n):
                pool.wait_ge(x2hi_done, n + 1)
                pool.tensor_tensor(x2h[:, :, LO, :], xn2[:, :, :], x2h[:, :, HI, :], ALU.subtract,
                                   ).then_inc(x2h_done, 1)

            pool.wait_ge(setup_p, 4)
            rstd(0, var1, ve1, rs1, rstd1)
            x_low(0)
            y_low(0, 0)
            rstd(1, var1, ve1, rs1, rstd1)
            x_low(1)
            pool.wait_ge(setup_v, SETUP_BO)

            def step(b, q, r):
                if final(b - 1):
                    x2_low(b - 2)
                    w_low(b - 1, 2)
                if has(b + 1):
                    y_low(b + 1, 1 - q)
                if has(b):
                    w_low(b, 0)
                    if not final(b):
                        w_low(b, 1)
                    add_bo(b)
                if has(b + 2):
                    rstd(b + 2, var1, ve1, rs1, rstd1)
                if has(b - 1):
                    rstd(b - 1, var2, ve2, rs2, rstd2)
                if final(b):
                    w_low(b, 1)
                if has(b + 2):
                    x_low(b + 2)
                if has(b - 1) and not final(b):
                    x2_low(b - 1)
                if has(b) and not final(b):
                    w_low(b, 2)

            steps(pool, step)

            def view(t):
                return t[:, :].rearrange("p (j e) -> p j e", e=E)

            pool.wait_ge(route_v, R_GATE)
            pool.tensor_tensor(view(tmp), view(oh1), pr1[:, :].unsqueeze(2).to_broadcast([P, NT, E]), ALU.mult,
                               ).then_inc(comb_done, 1)
            pool.tensor_tensor(view(comb), view(oh2), pr2[:, :].unsqueeze(2).to_broadcast([P, NT, E]), ALU.mult,
                               ).then_inc(comb_done, 1)
            pool.wait_ge(comb_done, 2)
            pool.tensor_tensor(comb[:, :], comb[:, :], tmp[:, :], ALU.add).then_inc(comb_done, 1)
            pool.wait_ge(route_v, R_EQ)
            for k in range(TOPK):
                half_k = hot_blk[:, k * NT:(k + 1) * NT, :]
                pool.tensor_tensor(half_k, half_k, cst[:, C_TOK:C_TOK + NT].unsqueeze(2).to_broadcast([P, NT, BLOCKS]),
                                   ALU.mult).then_inc(hot_done, 1)

            def gather(i, q):
                if begun(i - 3):
                    pool.wait_ge(v_half, i - 3)
                pool.tensor_copy(row_in[q][:, :], idx_g[:, bass.ds(i, 1)]).then_inc(row_in_done, 1)
                pool.wait_ge(row_in_done, i + 1)
                pool.sem_inc(stood_alone, 1)
                pool.indirect_dma_start(xg[q], None, rows,
                                        bass.IndirectOffsetOnAxis(ap=row_in[q][:, :], axis=0),
                                        ).then_inc(xg_in[q], 16)

            def add_rows(i, q):
                pool.tensor_copy(row_out[q][:, :], idx_s[:, bass.ds(i, 1)]).then_inc(row_out_done, 1)
                pool.wait_ge(row_out_done, i + 1)
                pool.wait_ge(yo_done, i + 1 + CREDIT)
                if not isinstance(i, int) or i > 0:
                    pool.wait_ge(added, i * 16)
                    pool.sem_inc(stood_alone, 1)
                pool.indirect_dma_start(out_flat, bass.IndirectOffsetOnAxis(ap=row_out[q][:, :], axis=0),
                                        yo[q][:, :], None, bounds_check=N - 1, oob_is_err=False,
                                        compute_op=ALU.add).then_inc(added, 16)

            pool.wait_ge(rows_stored, 16 * B)
            pool.wait_ge(gates_stored, 16)
            pool.wait_ge(base_stored, 16 * B)
            pool.wait_ge(idx_done, 4)
            for i in range(4):
                gather(i, i)

            def blk(i, q4):
                gather(i + 4, q4)
                add_rows(i, q4 % 2)

            for i in range(4):
                blk(i, i)
            with pool.Fori(0, (BLOCKS - 8) // 4) as j:
                for u in range(4):
                    blk(j * 4 + (u + 4), u)
            done = (BLOCKS - 4) // 4 * 4
            for i in range(done, BLOCKS):
                if i + 4 < BLOCKS:
                    gather(i + 4, i % 4)
                add_rows(i, i % 2)
            pool.wait_ge(added, 16 * BLOCKS)

        @block.tensor
        def _(pe):
            def split_mm(dst, left, right, kts=KT):
                n = 0
                for k in range(kts):
                    for a, c in PAIRS:
                        mm = pe.matmul(dst, left(a, k), right(c, k), start=(n == 0), stop=(n == 3 * kts - 1))
                        n += 1
                return mm

            def turns(src, dst16):
                for t in range(TT):
                    for h in (HI, LO):
                        for k in range(KT):
                            o = (h * KT + k) * T + t * P
                            mm = pe.transpose(dst16[:, o:o + P], src[:, t, h, k * P:(k + 1) * P], ident[:, :])
                return mm

            def x_turn(n):
                pe.wait_ge(xh_done, n + 1)
                if begun((n - 1) * HG):
                    pe.wait_ge(mrow_done, (n - 1) * HG)
                turns(xh, turn16).then_inc(lt_mm, 1)

            def q_mul(n):
                pe.wait_ge(xT_done, n + 1)
                if begun(n):
                    pe.wait_ge(v_done, n)
                for m in range(KT):
                    mm = split_mm(pa[:, m * T:(m + 1) * T], lambda a, k: aw[a][:, 0, k, m * P:(m + 1) * P],
                                  lambda c, k: xT[:, c, k, :])
                mm.then_inc(q_mm, 1)

            def k_mul(n):
                pe.wait_ge(yT_done, n + 1)
                if begun((n - 1) * HG + 1):
                    pe.wait_ge(mrow_done, (n - 1) * HG + 1)
                for m in range(KT):
                    mm = split_mm(pb[:, m * T:(m + 1) * T], lambda a, k: aw[a][:, 1, k, m * P:(m + 1) * P],
                                  lambda c, k: yT[:, c, k * T:(k + 1) * T])
                mm.then_inc(k_mm, 1)

            def v_mul(n):
                pe.wait_ge(q_st, n + 1)
                for t in range(TT):
                    mm = split_mm(pa[:, t * D:(t + 1) * D],
                                  lambda a, k: yT[:, a, k * T + t * P:k * T + (t + 1) * P],
                                  lambda c, k: aw[c][:, 2, k, :])
                mm.then_inc(v_mm, 1)

            def scores(b, g, q):
                for bank, (tq, tk) in enumerate(((0, 0), (1, 0), (1, 1))):
                    if tq == tk:
                        pe.matmul(score[:, bank, :, :], identb[:, :], mask_s[:, :, :], start=True, stop=True)
                    for h in range(4):
                        mm = pe.matmul(score[:, bank, h, :], q_stack[q][0:96, 4 * g + h, tq * P:(tq + 1) * P],
                                       k_stack[q][0:96, 4 * g + h, tk * P:(tk + 1) * P],
                                       start=(tq != tk and h == 0), stop=True, skip_group_check=True)
                mm.then_inc(s_mm, 1)

            def scores_t(b, g, q):
                for bank, (tk, tq) in enumerate(((0, 0), (0, 1), (1, 1))):
                    if tq == tk:
                        pe.matmul(score[:, bank, :, :], identb[:, :], mask_t[:, :, :], start=True, stop=True)
                    for h in range(4):
                        mm = pe.matmul(score[:, bank, h, :], k_stack[q][0:97, 4 * g + h, tk * P:(tk + 1) * P],
                                       q_stack[q][0:97, 4 * g + h, tq * P:(tq + 1) * P],
                                       start=(tq != tk and h == 0), stop=True, skip_group_check=True)
                mm.then_inc(t_mm, 1)

            def mix(b, g, q):
                pe.wait_ge(exp_done, b * HG + g + 1)
                if final(b) and g == 1:
                    pe.wait_ge(v_done, B)
                elif begun(b * HG + g):
                    pe.wait_ge(umul_done, b * HG + g)
                for tk, w, col in ((0, T, 0), (1, P, P)):
                    for part in range(2):
                        for h in range(4):
                            left = onesf[:, :] if part else v_sb[q][:, tk, (4 * g + h) * HD:(4 * g + h + 1) * HD]
                            p = probs[g][:, 0:2, h, :] if tk == 0 else probs[g][:, 2:3, h, :]
                            o = uden(b, g)[32 * h:32 * h + 32, part * T + col:part * T + col + w]
                            mm = pe.matmul(o.rearrange("p (s t) -> p s t", t=P), left, p,
                                           start=(tk == 0 and part == 0), stop=True,
                                           skip_group_check=True)
                mm.then_inc(pv_mm, 1)

            def o_mul(b):
                pe.wait_ge(ctx_done, (b + 1) * HG)
                if begun(b) and not final(b):
                    pe.wait_ge(logit_done, b)
                for t in range(TT):
                    mm = split_mm(attn_out(b)[:, t * D:(t + 1) * D], lambda a, k: ctx_hl[a][:, k, t * P:(t + 1) * P],
                                  lambda c, k: aw[c][:, 3, k, :])
                mm.then_inc(o_mm, 1)

            def r_turn(b):
                pe.wait_ge(x2h_done, b + 1)
                if begun(b):
                    pe.wait_ge(logit_done, b)
                turns(x2h, rout16).then_inc(rt_mm, 1)

            def r_mul(b):
                pe.wait_ge(x2T_done, b + 1)
                for t in range(TT):
                    mm = split_mm(rout[:, t * E:(t + 1) * E], lambda a, k: x2T[:, a, k, t * P:(t + 1) * P],
                                  lambda c, k: gw[c][:, k, :])
                mm.then_inc(r_mm, 1)

            pe.wait_ge(setup_v, SETUP_PE)
            pe.wait_ge(setup_p, 4)
            x_turn(0)
            pe.wait_ge(aw_lo, 1)
            q_mul(0)
            pe.wait_ge(aw_lo, 2)
            k_mul(0)
            pe.wait_ge(aw_lo, 3)
            v_mul(0)
            pe.wait_ge(aw_lo, 4)

            def shift_turn(b, g):
                pe.wait_ge(mneg_done, b * HG + g + 1)
                if g == 0:
                    pe.wait_ge(k_st, b + 1)
                elif has(b + 1):
                    pe.wait_ge(xT_done, b + 2)
                else:
                    pe.wait_ge(xT_done, B)
                pe.transpose(shift16[g], mneg[g][:, :], ident[:, :]).then_inc(mt_mm, 1)

            pe.wait_ge(setup_v, SETUP_MASKS)

            def step(b, q, r):
                if has(b):
                    pe.wait_ge(stack_in[q], (r + 1) * STACK)
                    if begun(b * HG):
                        pe.wait_ge(exp_done, b * HG)
                    scores(b, 0, q)
                if has(b - 1):
                    mix(b - 1, 0, 1 - q)
                if has(b + 1):
                    x_turn(b + 1)
                if has(b):
                    shift_turn(b, 0)
                    pe.wait_ge(max_done, b * HG + 1)
                    scores(b, 1, q)
                if has(b - 2) and has(b):
                    r_turn(b - 2)
                if has(b - 1):
                    mix(b - 1, 1, 1 - q)
                if has(b - 2) and not has(b):
                    r_turn(b - 2)
                if has(b + 1):
                    q_mul(b + 1)
                if has(b - 2) and not final(b - 1):
                    r_mul(b - 2)
                if has(b):
                    shift_turn(b, 1)
                if has(b + 1):
                    k_mul(b + 1)
                if has(b):
                    pe.wait_ge(max_done, b * HG + 2)
                    pe.wait_ge(shift_in[0], (b + 1) * 16)
                    scores_t(b, 0, q)
                if has(b - 1) and not final(b):
                    o_mul(b - 1)
                if has(b):
                    pe.wait_ge(shift_in[1], (b + 1) * 16)
                    pe.wait_ge(exp_done, b * HG + 1)
                    scores_t(b, 1, q)
                if final(b):
                    o_mul(b - 1)
                if final(b - 1):
                    r_mul(b - 2)
                if has(b + 1):
                    v_mul(b + 1)

            steps(pe, step)

            pe.wait_ge(route_v, 2 * R_TOP2)
            both_v = both[:, :].rearrange("p (j e) -> p e j", e=E)
            pe.matmul(ps[:, 1, 0:P], tri16[:, :], both_v, start=True, stop=True)
            pe.matmul(ps[:, 2, 0:P], one16[:, :], both_v, start=True, stop=True).then_inc(route_mm, 1)
            pe.wait_ge(route_v, R_HOT)
            pe.wait_ge(hot_done, 2)
            for c in range(TOPK * NT):
                mm = pe.matmul(ps[:, 3, 0:BLOCKS], hot_lo[:, c, :], hot_blk[:, c, :], start=(c == 0),
                               stop=(c == TOPK * NT - 1))
            mm.then_inc(table_mm, 1)

            def turn_in(i, q4, n4):
                pe.wait_ge(xg_in[q4], n4 * 16)
                if begun(i):
                    pe.wait_ge(xgT_done, i)
                for c in range(4):
                    mm = pe.transpose(xTp[:, c * P:(c + 1) * P], xg[q4].bitcast(F16)[:, c * P:(c + 1) * P], ident[:, :])
                mm.then_inc(xgT_mm, 1)

            def gv_mul(i, q, at):
                pe.wait_ge(xgT_done, i + 1)
                if begun(i - 1):
                    pe.wait_ge(v_half, i - 1)
                for m in range(2):
                    mm = split_mm(gvp[q][:, m, :], lambda a, k: xgT[q][:, (a * KT + k) * P:(a * KT + k + 1) * P],
                                  lambda c, k: w_hl[c][:, bass.ds(at + (m * WE + k * F), F)])
                mm.then_inc(gv_mm, 1)

            def turn_h(i):
                pe.wait_ge(h_done, i + 1)
                if begun(i):
                    pe.wait_ge(hT_done, i)
                for k in range(FT):
                    mm = pe.transpose(hTp[:, k * P:(k + 1) * P], hh[:, k * P:(k + 1) * P], cst[:, C_ID:C_ID + P])
                mm.then_inc(hT_mm, 1)

            def y_mul(i, q, at):
                pe.wait_ge(hT_done, i + 1)
                pe.wait_ge(y_done, i - 1 + CREDIT)
                split_mm(yp[q][:, 0:D], lambda a, k: hT[q][a][:, k * P:(k + 1) * P],
                         lambda c, k: w_hl[c][:, bass.ds(at + (2 * WE + k * D), D)],
                         FT).then_inc(y_mm, 1)

            pe.wait_ge(wlo_done, WC * B)
            pe.wait_ge(idx_done, 4)
            at = expert_values(mybir.EngineType.PE, wat, 0, 2, EW)
            turn_in(0, 0, 1)
            turn_in(1, 1, 1)
            gv_mul(0, 0, at[0])
            gv_mul(1, 1, at[1])
            turn_h(0)
            turn_in(2, 2, 1)

            def blk(i, q, u4, n4, last, here, before):
                gv_mul(i, q, here)
                turn_h(i - 1)
                if not last:
                    turn_in(i + 1, u4, n4)
                y_mul(i - 2, q, before)

            with pe.Fori(0, (BLOCKS - 3) // 4) as j:
                at = expert_values(mybir.EngineType.PE, wat, j * 4, 6, EW)
                for u in range(4):
                    blk(j * 4 + (u + 2), u % 2, (u + 3) % 4, j + (u + 3) // 4 + 1, False, at[u + 2], at[u])
            at = expert_values(mybir.EngineType.PE, wat, BLOCKS - 3, 3, EW)
            blk(BLOCKS - 1, (BLOCKS - 1) % 2, 0, 0, True, at[2], at[0])
            turn_h(BLOCKS - 1)
            y_mul(BLOCKS - 2, (BLOCKS - 2) % 2, at[1])
            y_mul(BLOCKS - 1, (BLOCKS - 1) % 2, at[2])

        @block.vector
        def _(dve):
            def row_stats(n, st, stats_done):
                for t in range(TT):
                    last = dve.bn_stats(st[:, t, :], region_x[:, bass.ds((n * TT + t) * D, D)])
                last.then_inc(stats_done, 1)

            def mean_var(n, st, mv, stats_done, mv_done):
                dve.wait_ge(stats_done, n + 1)
                dve.sem_inc(stood_alone, 1)
                for t in range(TT):
                    last = dve.bn_aggr(mv[:, t, :], st[:, t, :])
                last.then_inc(mv_done, 1)

            def var_eps(n, mv, ve, mv_done, var):
                dve.wait_ge(mv_done, n + 1)
                dve.tensor_scalar(ve[:, :], mv[:, :, 1], EPS, None, ALU.add).then_inc(var, 1)

            def norm(n, dst, mv, rs, rstd, done, low_done):
                dve.wait_ge(rstd, n + 1)
                if begun(n):
                    dve.wait_ge(low_done, n)
                for t in range(TT):
                    last = dve.tensor_scalar(dst[:, t, :], region_x[:, bass.ds((n * TT + t) * D, D)],
                                             mv[:, t, 0:1], rs[:, t:t + 1], ALU.subtract, ALU.mult)
                last.then_inc(done, 1)

            def x_turn_out(n):
                dve.wait_ge(lt_mm, n + 1)
                if begun(n):
                    dve.wait_ge(q_mm, n)
                dve.tensor_copy(xT[:, :, :, :].rearrange("p s k t -> p (s k t)"), turn16).then_inc(xT_done, 1)

            def qk_low(which, n):
                hi_done, done, src = ((q_hi, q_st, pa), (k_hi, k_st, pb))[which]
                dve.wait_ge(hi_done, n + 1)
                for m in range(KT):
                    last = dve.scalar_tensor_tensor(
                        out=qk_st[which][LO][:, m, :], in0=src[:, m * T:(m + 1) * T], scalar=bc[:, which, m:m + 1],
                        in1=qk_st[which][HI][:, m, :], op0=ALU.add, op1=ALU.subtract)
                last.then_inc(done, 1)

            def maxima(b, g):
                dve.wait_ge(s_mm, b * HG + g + 1)
                hs = slice(4 * g, 4 * g + 4)
                dve.tensor_reduce(mx[:, hs, 0], score[:, 0, :, :], AX.X, ALU.max)
                dve.tensor_reduce(mx[:, hs, 1], score[:, 1:3, :, :].rearrange("p s h t -> p h s t"), AX.XY,
                                  ALU.max).then_inc(max_done, 1)
                dve.wait_ge(max_done, b * HG + g + 1)
                dve.tensor_scalar(mneg[g][:, :], mx[:, hs, :].rearrange("p h t -> p (h t)"), -1.0 / (WS * WS), None,
                                  ALU.mult).then_inc(mneg_done, 1)

            def denominators(b, g):
                dve.wait_ge(pv_mm, b * HG + g + 1)
                if begun(b * HG + g):
                    dve.wait_ge(umul_done, b * HG + g)
                dve.reciprocal(rden[:, :], uden(b, g)[:, T:2 * T]).then_inc(rden_done, 1)

            def context(b, g):
                dve.wait_ge(rden_done, b * HG + g + 1)
                if begun(b * HG + g - 1):
                    dve.wait_ge(ctxhi_done, b * HG + g - 1)
                dve.tensor_tensor(ctx32[g][:, :], uden(b, g)[:, 0:T], rden[:, :], ALU.mult).then_inc(umul_done, 1)

            def context_low(b, g):
                dve.wait_ge(ctxhi_done, b * HG + g + 1)
                dve.wait_ge(umul_done, b * HG + g + 1)
                dve.scalar_tensor_tensor(out=ctx_hl[LO][:, g, :], in0=ctx32[g][:, :], scalar=bc[:, 2, g:g + 1],
                                         in1=ctx_hl[HI][:, g, :], op0=ALU.add,
                                         op1=ALU.subtract).then_inc(ctx_done, 1)

            def residual(b):
                dve.wait_ge(o_mm, b + 1)
                dve.wait_ge(xb_done, b + 1)
                v = region_x[:, bass.ds(b * TT * D, TT * D)]
                dve.scalar_tensor_tensor(out=v, in0=attn_out(b), scalar=gsc[:, 0:1], in1=v, op0=ALU.mult,
                                         op1=ALU.add).then_inc(x1_done, 1)

            def logit_out(b):
                dve.wait_ge(r_mm, b + 1)
                dve.tensor_scalar(logits[:, bass.ds(b * TT * E, TT * E)], rout[:, 0:TT * E], 1.0 / WS, None,
                                  ALU.mult).then_inc(logit_done, 1)

            dve.sem_inc(y_done, CREDIT)
            dve.wait_ge(x0_in, 16)
            row_stats(0, st1, ln1_a)
            mean_var(0, st1, mv1, ln1_a, ln1_b)
            var_eps(0, mv1, ve1, ln1_b, var1)
            norm(0, xn, mv1, rs1, rstd1, xn_done, xh_done)
            dve.wait_ge(consts_in, 16)
            dve.tensor_copy(ident[:, :], cst[:, C_ID:C_ID + P]).then_inc(setup_v, 1)
            dve.wait_ge(setup_v, 1)

            def attn_w_low(c):
                dve.wait_ge(aw_hi, c + 1)
                dve.scalar_tensor_tensor(
                    out=aw[LO][:, c, :, :].rearrange("p k d -> p (k d)"), in0=region_w[:, c * KT * D:(c + 1) * KT * D],
                    scalar=WS, in1=aw[HI][:, c, :, :].rearrange("p k d -> p (k d)"), op0=ALU.mult,
                    op1=ALU.subtract).then_inc(aw_lo, 1)

            attn_w_low(0)
            x_turn_out(0)
            attn_w_low(1)
            dve.wait_ge(small_in, 64)
            dve.tensor_scalar(bc[:, :, :].rearrange("p c k -> p (c k)"), bc_raw[:, :], WS, None, ALU.mult,
                              ).then_inc(setup_v, 1)
            dve.wait_ge(setup_v, 2)
            attn_w_low(2)
            qk_low(0, 0)
            qk_low(1, 0)
            dve.wait_ge(x_in, 16)
            row_stats(1, st1, ln1_a)
            attn_w_low(3)
            mean_var(1, st1, mv1, ln1_a, ln1_b)
            dve.tensor_copy(identb[:, :], cst[:, C_ID:C_ID + P])
            var_eps(1, mv1, ve1, ln1_b, var1)
            dve.tensor_copy(mask_s[:, :, :], cst[:, C_MS:C_MS + P].unsqueeze(1).to_broadcast([P, 4, P]))
            dve.tensor_copy(mask_t[:, :, :], cst[:, C_MT:C_MT + P].unsqueeze(1).to_broadcast([P, 4, P]),
                            ).then_inc(setup_v, 1)
            norm(1, xn, mv1, rs1, rstd1, xn_done, xh_done)
            dve.wait_ge(setup_a, 2)
            dve.scalar_tensor_tensor(out=gw[LO][:, :, :].rearrange("p k e -> p (k e)"), in0=gw_raw[:, :],
                                     scalar=WS, in1=gw[HI][:, :, :].rearrange("p k e -> p (k e)"),
                                     op0=ALU.mult, op1=ALU.subtract)
            dve.tensor_scalar(gsc[:, :], tg[:, 0:1], 1.0 / (WS * WS), None, ALU.mult)
            dve.tensor_copy(tri16[:, :], cst[:, C_TRI:C_TRI + P])
            dve.tensor_copy(one16[:, :], cst[:, C_ONE:C_ONE + P])
            dve.tensor_copy(io16[:, :], cst[:, C_IO:C_IO + P])
            dve.tensor_scalar(bo[:, :], bo[:, :], tg[:, 0:1], None, ALU.mult).then_inc(setup_v, 1)
            dve.wait_ge(setup_v, 4)

            def je(t):
                return t[:, :].rearrange("p (j e) -> p j e", e=E)

            def ej(t):
                return t[:, :].rearrange("p (e j) -> p e j", e=E)

            def top_two(part):
                tiles = (slice(0, NT - TT), slice(NT - TT, NT))[part]
                n, k = tiles.stop - tiles.start, part * R_TOP2
                cut = slice(tiles.start * E, tiles.stop * E)

                def view(t):
                    return t[:, cut].rearrange("p (j e) -> p j e", e=E)

                def each(t):
                    return t[:, tiles].unsqueeze(2).to_broadcast([P, n, E])

                e8 = view(cst[:, C_E8:C_E8 + NT * E])
                dve.wait_ge(logit_done, B - 1 + part)
                dve.wait_ge(wlo_done, WC * B)
                dve.tensor_reduce(m1[:, tiles], view(logits), AX.X, ALU.max).then_inc(route_v, 1)
                dve.wait_ge(route_v, k + 1)
                dve.tensor_tensor(view(eq), view(logits), each(m1), ALU.is_equal).then_inc(route_v, 1)
                dve.wait_ge(route_v, k + 2)
                dve.tensor_tensor(view(eq), view(eq), e8, ALU.mult).then_inc(route_v, 1)
                dve.wait_ge(route_v, k + 3)
                dve.tensor_reduce(e1[:, tiles], view(eq), AX.X, ALU.min).then_inc(route_v, 1)
                dve.wait_ge(route_v, k + 4)
                dve.tensor_tensor(view(oh1), e8, each(e1), ALU.is_equal).then_inc(route_v, 1)
                dve.wait_ge(route_v, k + 5)
                dve.scalar_tensor_tensor(out=lmask[:, cut], in0=oh1[:, cut], scalar=NEVER, in1=logits[:, cut],
                                         op0=ALU.mult, op1=ALU.add).then_inc(route_v, 1)
                dve.wait_ge(route_v, k + 6)
                dve.tensor_reduce(m2[:, tiles], view(lmask), AX.X, ALU.max).then_inc(route_v, 1)
                dve.wait_ge(route_v, k + 7)
                dve.tensor_tensor(diff[:, tiles], m2[:, tiles], m1[:, tiles], ALU.subtract).then_inc(route_v, 1)
                dve.tensor_tensor(view(eq), view(lmask), each(m2), ALU.is_equal).then_inc(route_v, 1)
                dve.wait_ge(route_v, k + 9)
                dve.tensor_tensor(view(eq), view(eq), e8, ALU.mult).then_inc(route_v, 1)
                dve.wait_ge(route_v, k + 10)
                dve.tensor_reduce(e2[:, tiles], view(eq), AX.X, ALU.min).then_inc(route_v, 1)
                dve.wait_ge(route_v, k + 11)
                dve.tensor_tensor(view(oh2), e8, each(e2), ALU.is_equal).then_inc(route_v, 1)
                dve.wait_ge(route_v, k + 12)
                dve.tensor_tensor(both[:, cut], oh1[:, cut], oh2[:, cut], ALU.add).then_inc(route_v, 1)

            def step(b, q, r):
                if has(b - 2) and not has(b - 1):
                    top_two(0)
                if has(b):
                    maxima(b, 0)
                if has(b - 1):
                    denominators(b - 1, 0)
                    context(b - 1, 0)
                if final(b - 1):
                    norm(b - 2, xn2, mv2, rs2, rstd2, xn2_done, x2h_done)
                if has(b + 1):
                    x_turn_out(b + 1)
                if has(b):
                    maxima(b, 1)
                if has(b - 1):
                    denominators(b - 1, 1)
                    context_low(b - 1, 0)
                    context(b - 1, 1)
                if has(b + 1):
                    qk_low(0, b + 1)
                if has(b - 1):
                    context_low(b - 1, 1)
                if has(b - 2) and not final(b - 1):
                    logit_out(b - 2)
                if has(b + 1):
                    qk_low(1, b + 1)
                if has(b + 2):
                    row_stats(b + 2, st1, ln1_a)
                if has(b - 1):
                    residual(b - 1)
                if has(b + 2):
                    mean_var(b + 2, st1, mv1, ln1_a, ln1_b)
                if has(b - 1):
                    dve.wait_ge(x1_done, b)
                    dve.sem_inc(stood_alone, 1)
                    row_stats(b - 1, st2, ln2_a)
                if has(b + 2):
                    var_eps(b + 2, mv1, ve1, ln1_b, var1)
                if has(b - 1):
                    if final(b - 1):
                        logit_out(b - 2)
                    mean_var(b - 1, st2, mv2, ln2_a, ln2_b)
                    var_eps(b - 1, mv2, ve2, ln2_b, var2)
                if has(b + 2):
                    norm(b + 2, xn, mv1, rs1, rstd1, xn_done, xh_done)
                if has(b - 1) and not final(b):
                    norm(b - 1, xn2, mv2, rs2, rstd2, xn2_done, x2h_done)

            steps(dve, step)

            top_two(1)
            dve.wait_ge(route_a, 2)
            dve.tensor_scalar(den[:, :], ex[:, :], 1.0, None, ALU.add).then_inc(route_v, 1)
            dve.wait_ge(route_v, 27)
            dve.reciprocal(pr1[:, :], den[:, :]).then_inc(route_v, 1)
            dve.wait_ge(route_v, 28)
            dve.tensor_scalar(pr1[:, :], pr1[:, :], tg[:, 1:2], None, ALU.mult).then_inc(route_v, 1)
            dve.wait_ge(route_v, 29)
            dve.tensor_tensor(pr2[:, :], ex[:, :], pr1[:, :], ALU.mult).then_inc(route_v, 1)
            dve.wait_ge(route_mm, 1)
            dve.tensor_copy(tot[:, :], ps[:, 2, 0:P]).then_inc(route_v, 1)
            dve.wait_ge(route_v, 31)
            dve.tensor_tensor_scan(out=scan[:, :], data0=cst[:, C_SC:C_SC + NT * E], data1=tot[:, :], initial=0.0,
                                   op0=ALU.mult, op1=ALU.add).then_inc(route_v, 1)
            dve.wait_ge(route_v, 32)
            dve.tensor_tensor(tot[:, :], scan[:, :], tot[:, :], ALU.subtract).then_inc(route_v, 1)
            dve.wait_ge(route_v, 33)
            dve.tensor_tensor(tot[:, :], ps[:, 1, 0:P], tot[:, :], ALU.add).then_inc(route_v, 1)
            dve.wait_ge(route_v, 34)
            dve.tensor_scalar(nblk[:, :], ej(scan)[:, :, NT - 1], float(P - 1), None, ALU.add).then_inc(route_v, 1)
            dve.wait_ge(route_v, 35)
            dve.tensor_scalar(nblk[:, :], nblk[:, :], 7, None, ALU.logical_shift_right).then_inc(route_v, 1)
            dve.wait_ge(route_v, 36)
            dve.tensor_copy(nblk_f[:, :], nblk[:, :]).then_inc(route_v, 1)
            dve.wait_ge(route_v, 37)
            dve.tensor_tensor_scan(out=start[:, :], data0=cst[:, C_ONE:C_ONE + E], data1=nblk_f[:, :],
                                   initial=0.0, op0=ALU.mult, op1=ALU.add).then_inc(route_v, 1)
            dve.wait_ge(route_v, 38)
            dve.tensor_tensor(start_s[:, :], start[:, :], nblk_f[:, :], ALU.subtract).then_inc(route_v, 1)
            dve.wait_ge(route_v, 39)
            dve.tensor_scalar(start_s[:, :], start_s[:, :], float(P), None, ALU.mult).then_inc(route_v, 1)
            dve.wait_ge(route_v, 40)
            dve.tensor_tensor(ej(base), ej(tot), start_s[:, :].unsqueeze(2).to_broadcast([P, E, NT]), ALU.add,
                              ).then_inc(route_v, 1)
            dve.wait_ge(route_v, 41)
            for k, oh in enumerate((oh1, oh2)):
                dve.tensor_tensor(je(eq), je(oh), base[:, :].rearrange("p (e j) -> p j e", e=E), ALU.mult,
                                  ).then_inc(route_v, 1)
                dve.wait_ge(route_v, 42 + 2 * k)
                dve.tensor_reduce(pos[:, k * NT:(k + 1) * NT], je(eq), AX.X, ALU.add).then_inc(route_v, 1)
                dve.wait_ge(route_v, 43 + 2 * k)
            dve.tensor_copy(pos_i[:, :], pos[:, :]).then_inc(route_v, 1)
            dve.wait_ge(route_v, 46)
            dve.tensor_scalar(hi_i[:, :], pos_i[:, :], 7, None, ALU.logical_shift_right).then_inc(route_v, 1)
            dve.wait_ge(route_v, 47)
            dve.tensor_scalar(lo_i[:, :], pos_i[:, :], P - 1, None, ALU.bitwise_and).then_inc(route_v, 1)
            dve.wait_ge(route_v, 48)
            dve.tensor_copy(hi_f[:, :], hi_i[:, :]).then_inc(route_v, 1)
            dve.wait_ge(route_v, 49)
            dve.tensor_copy(lo_f[:, :], lo_i[:, :]).then_inc(route_v, 1)
            dve.wait_ge(route_v, 50)
            dve.wait_ge(base_stored, 16 * B)
            dve.tensor_tensor(hot_blk, cst[:, C_BLK:C_BLK + BLOCKS].unsqueeze(1).to_broadcast([P, TOPK * NT, BLOCKS]),
                              hi_f[:, :].unsqueeze(2).to_broadcast([P, TOPK * NT, BLOCKS]), ALU.is_equal,
                              ).then_inc(route_v, 1)
            dve.tensor_tensor(hot_lo, io16[:, :].unsqueeze(1).to_broadcast([P, TOPK * NT, P]),
                              lo_f[:, :].unsqueeze(2).to_broadcast([P, TOPK * NT, P]), ALU.is_equal,
                              ).then_inc(route_v, 1)
            dve.tensor_tensor(cmp[:, :].rearrange("p (c e) -> p c e", e=E - 1),
                              cst[0:1, C_BLK:C_BLK + BLOCKS].unsqueeze(2).to_broadcast([1, BLOCKS, E - 1]),
                              start[0:1, 0:E - 1].unsqueeze(1).to_broadcast([1, BLOCKS, E - 1]), ALU.is_ge,
                              ).then_inc(route_v, 1)
            dve.wait_ge(route_v, 53)
            dve.tensor_reduce(eidf[:, :], cmp[:, :].rearrange("p (c e) -> p c e", e=E - 1), AX.X, ALU.add,
                              ).then_inc(route_v, 1)
            dve.wait_ge(route_v, 54)
            dve.tensor_copy(eid[:, :], eidf[:, :]).then_inc(idx_done, 1)
            dve.tensor_scalar(wat[:, :], eidf[:, :], float(EW), None, ALU.mult).then_inc(idx_done, 1)
            dve.wait_ge(table_mm, 1)
            dve.tensor_scalar(idx_f[:, :], ps[:, 3, 0:BLOCKS], float(N), None, ALU.add).then_inc(route_v, 1)
            dve.wait_ge(route_v, 55)
            dve.tensor_copy(idx_s[:, :], idx_f[:, :]).then_inc(idx_done, 1)
            dve.tensor_scalar(idx_g[:, :], idx_f[:, :], float(N - 1), None, ALU.min).then_inc(idx_done, 1)
            dve.wait_ge(idx_done, 4)

            def first_out(i, q, q4, e):
                dve.wait_ge(gv_mm, i + 1)
                if not isinstance(i, int) or i > 3:
                    dve.wait_ge(yo_done, i - 3 + CREDIT)
                dve.tensor_copy(wslot[:, q4:q4 + 1], xg[q4].bitcast(F32)[:, bass.ds(e + D, 1)])
                if begun(i):
                    dve.wait_ge(h_done, i)
                for m, done in enumerate((g_done, v_half)):
                    dve.scalar_tensor_tensor(out=gv[:, m * F:(m + 1) * F], in0=gvp[q][:, m, :], scalar=1.0 / WS,
                                             in1=region_a[:, bass.ds(e * EB + m * F, F)], op0=ALU.mult,
                                             op1=ALU.add).then_inc(done, 1)

            def h_out(i):
                dve.wait_ge(silu_done, i + 1)
                dve.wait_ge(v_half, i + 1)
                if begun(i):
                    dve.wait_ge(hT_mm, i)
                dve.tensor_tensor(hh, gv[:, 0:F], gv[:, F:2 * F], ALU.mult).then_inc(h_done, 1)

            def h_low(i, q):
                dve.wait_ge(hT_hi, i + 1)
                dve.tensor_tensor(hT[q][LO], hTp, hT[q][HI], ALU.subtract).then_inc(hT_done, 1)

            def y_out(i, q, e):
                dve.wait_ge(y_mm, i + 1)
                dve.wait_ge(yo_done, i - 1 + CREDIT)
                dve.scalar_tensor_tensor(out=yb[q], in0=yp[q][:, 0:D], scalar=1.0 / WS,
                                         in1=region_a[:, bass.ds(e * EB + 2 * F, D)], op0=ALU.mult,
                                         op1=ALU.add).then_inc(y_done, 1)

            dve.wait_ge(bias_in, 16)
            e = expert_values(mybir.EngineType.DVE, eid, 0, 2, 1)
            first_out(0, 0, 0, e[0])
            h_out(0)
            first_out(1, 1, 1, e[1])
            h_low(0, 0)
            h_out(1)

            def blk(i, q4, here, before):
                first_out(i, q4 % 2, q4, here)
                h_low(i - 1, 1 - q4 % 2)
                h_out(i)
                y_out(i - 2, q4 % 2, before)

            with dve.Fori(0, (BLOCKS - 3) // 4) as j:
                e = expert_values(mybir.EngineType.DVE, eid, j * 4, 6, 1)
                for u in range(4):
                    blk(j * 4 + (u + 2), (u + 2) % 4, e[u + 2], e[u])
            e = expert_values(mybir.EngineType.DVE, eid, BLOCKS - 3, 3, 1)
            blk(BLOCKS - 1, (BLOCKS - 1) % 4, e[2], e[0])
            h_low(BLOCKS - 1, (BLOCKS - 1) % 2)
            y_out(BLOCKS - 2, (BLOCKS - 2) % 2, e[1])
            y_out(BLOCKS - 1, (BLOCKS - 1) % 2, e[2])


SETUP_PE, SETUP_BIAS, SETUP_MASKS, SETUP_BO = 1, 2, 3, 4
R_DIFF, R_TOP2, R_GATE, R_EQ, R_HOT = 8, 13, 30, 51, 52


def kernel(**inputs):
    import concourse.bacc as _bacc
    from concourse.bass_utils import run_bass_kernel_spmd as _run

    a = {k: np.asarray(v) for k, v in inputs.items()}

    def tiles(w):
        o, i = w.shape[-2:]
        return np.moveaxis(np.swapaxes(w, -1, -2).reshape(*w.shape[:-2], i // P, P, o), -3, -2)

    def cols(v):
        return v.reshape(KT, P).T

    order = np.arange(D).reshape(H // HG, HG, HD).transpose(1, 2, 0).reshape(-1)

    x = a["x"]
    y = np.swapaxes(a["ctx_1024"], 1, 2).reshape(B, KT, P, T).transpose(0, 2, 1, 3).reshape(B, P, KT * T)
    g = np.concatenate([a["g_xattn"], a["g_ffn"]])
    wattn = np.stack([tiles(a["L0_xattn_W" + n][order] if n in "qk" else a["L0_xattn_W" + n]) for n in "qkvo"], 1).reshape(P, 4 * KT * D)
    bcol = np.stack([cols(a["L0_xattn_b" + n][order] if n in "qk" else a["L0_xattn_b" + n]) for n in "qkv"], 1).reshape(P, 3 * KT)
    brow = a["L0_xattn_bo"][None, :]
    wgate = tiles(a["L0_ffn_Wg"]).reshape(P, KT * E)
    wffn = np.stack([tiles(a["L0_ffn_W" + n]).reshape(E, P, WE) for n in "123"], 1).reshape(E * WC, P, WE)
    bffn = np.concatenate([a["L0_ffn_b1"], a["L0_ffn_b2"], a["L0_ffn_b3"]], 1).reshape(1, E * EB)
    arrays = {"in_" + k: np.ascontiguousarray(v) for k, v in dict(
        x=x, y=y, g=g, wattn=wattn, bcol=bcol, brow=brow, wgate=wgate, wffn=wffn, bffn=bffn,
        consts=constants()).items()}

    nc = _bacc.Bacc("TRN2", target_bir_lowering=False, num_devices=1)
    args = [nc.dram_tensor(k, v.shape, mybir.dt.from_np(v.dtype), kind="ExternalInput").ap()
            for k, v in arrays.items()]
    args.append(nc.dram_tensor("out", (B, T, D), F32, kind="ExternalOutput").ap())
    flamingo_kernel(nc, *args)
    r = _run(nc, [arrays], core_ids=[0])
    return r.results[0]["out"]
```
